# Optimizing a Trainium2 kernel written in Bass

```python
import numpy as np
import jax
import jax.numpy as jnp

def _softmax(x, axis=-1):
    return jax.nn.softmax(x, axis=axis)

def _gelu(x):
    return jax.nn.gelu(x, approximate=True)

def _silu(x):
    return jax.nn.silu(x)

def _sigmoid(x):
    return jax.nn.sigmoid(x)

def _layernorm(x, axis=-1, eps=1e-05):
    m = jnp.mean(x, axis=axis, keepdims=True)
    v = jnp.var(x, axis=axis, keepdims=True)
    return (x - m) / jnp.sqrt(v + eps)

def _scatter_add(tgt, idx, src, axis=0):
    return tgt.at[idx].add(src)

def _segment_sum(src, seg, n):
    return jax.ops.segment_sum(src, seg, n)
kernel_name = 'mk_gps_d2_gnn_r32_91c959'

def setup_inputs(seed: int=0):
    np.random.seed(seed)
    _w = jnp.asarray

    def _rec_inputs():
        import jax
        import jax.numpy as jnp
        _gk = jax.random.key(seed)
        x = -8.776e-05 + 1 * jax.random.normal(jax.random.fold_in(_gk, 1), (625, 256), jnp.float32)
        _s = jax.random.randint(jax.random.fold_in(_gk, 2), (10000,), 0, 625, jnp.int32)
        _d = jax.random.randint(jax.random.fold_in(_gk, 3), (10000,), 0, 625, jnp.int32)
        _loop = jnp.arange(625, dtype=jnp.int32)
        src = jnp.concatenate([_s, _d, _loop])
        dst = jnp.concatenate([_d, _s, _loop])
        _o = jnp.argsort(dst, stable=True)
        src = src[_o]
        dst = dst[_o]
        edge_type_8 = jax.random.randint(jax.random.fold_in(_gk, 14), (20625,), 0, 8, jnp.int32)
        edge_weight1 = 0.000937891 + 0.999965 * jax.random.normal(jax.random.fold_in(_gk, 15), (20625, 1), jnp.float32)
        return (x, src, dst, edge_type_8, edge_weight1)
    x, src, dst, edge_type_8, edge_weight1 = _rec_inputs()

    def _L0_gnn_setup():
        import jax, jax.numpy as jnp
        import numpy as np
        N_NODES = 625
        N_EDGES = 9375
        D = 256
        NUM_RELS = 8
        NUM_BASES = 4
        key = jax.random.key(seed)
        ks = jax.random.split(key, 8)
        x = jax.random.normal(ks[0], (N_NODES, D), dtype=jnp.float32)
        src = jax.random.randint(ks[1], (N_EDGES,), 0, N_NODES, dtype=jnp.int32)
        dst = jax.random.randint(ks[2], (N_EDGES,), 0, N_NODES, dtype=jnp.int32)
        etypes = jax.random.randint(ks[3], (N_EDGES,), 0, NUM_RELS, dtype=jnp.int32)
        scale = 1.0 / np.sqrt(D)
        basis = jax.random.normal(ks[4], (NUM_BASES, D, D), dtype=jnp.float32) * scale
        comp = jax.random.normal(ks[5], (NUM_RELS, NUM_BASES), dtype=jnp.float32)
        loop_weight = jax.random.normal(ks[6], (D, D), dtype=jnp.float32) * scale
        bias_param = jnp.zeros((D,), dtype=jnp.float32)
        return {'x': x, 'src': src, 'dst': dst, 'etypes': etypes, 'basis': basis, 'comp': comp, 'loop_weight': loop_weight, 'bias_param': bias_param}
    _L0_gnn_all = _L0_gnn_setup()
    _L0_gnn_in = {k: v for k, v in _L0_gnn_all.items() if k in ('basis', 'comp', 'loop_weight', 'bias_param')}
    del _L0_gnn_all

    def _L0_mix_setup():
        import jax, jax.numpy as jnp
        import numpy as np
        D_MODEL = 256
        NHEAD = 8
        D_HEAD = D_MODEL // NHEAD
        DIM_FF = 1024
        B, L = (4, 512)
        LN_EPS = 1e-05

        def _layernorm(x, g, b):
            mu = jnp.mean(x, axis=-1, keepdims=True)
            var = jnp.mean((x - mu) ** 2, axis=-1, keepdims=True)
            return (x - mu) * jax.lax.rsqrt(var + LN_EPS) * g + b

        def _phi(x):
            return jnp.where(x > 0, x + 1.0, jnp.exp(x))
        key = jax.random.key(seed)
        ks = jax.random.split(key, 16)
        s_in = 1.0 / np.sqrt(D_MODEL)
        s_ff = 1.0 / np.sqrt(DIM_FF)
        inp = {'x': jax.random.normal(ks[0], (B, L, D_MODEL), dtype=jnp.float32), 'Wq': jax.random.normal(ks[1], (D_MODEL, D_MODEL), dtype=jnp.float32) * s_in, 'bq': jnp.zeros((D_MODEL,), jnp.float32), 'Wk': jax.random.normal(ks[2], (D_MODEL, D_MODEL), dtype=jnp.float32) * s_in, 'bk': jnp.zeros((D_MODEL,), jnp.float32), 'Wv': jax.random.normal(ks[3], (D_MODEL, D_MODEL), dtype=jnp.float32) * s_in, 'bv': jnp.zeros((D_MODEL,), jnp.float32), 'Wo': jax.random.normal(ks[4], (D_MODEL, D_MODEL), dtype=jnp.float32) * s_in, 'bo': jnp.zeros((D_MODEL,), jnp.float32), 'W1': jax.random.normal(ks[5], (D_MODEL, DIM_FF), dtype=jnp.float32) * s_in, 'b1': jnp.zeros((DIM_FF,), jnp.float32), 'W2': jax.random.normal(ks[6], (DIM_FF, D_MODEL), dtype=jnp.float32) * s_ff, 'b2': jnp.zeros((D_MODEL,), jnp.float32), 'ln1_g': jnp.ones((D_MODEL,), jnp.float32), 'ln1_b': jnp.zeros((D_MODEL,), jnp.float32), 'ln2_g': jnp.ones((D_MODEL,), jnp.float32), 'ln2_b': jnp.zeros((D_MODEL,), jnp.float32)}
        return inp
    _L0_mix_all = _L0_mix_setup()
    _L0_mix_in = {k: v for k, v in _L0_mix_all.items() if k in ('Wq', 'bq', 'Wk', 'bk', 'Wv', 'bv', 'Wo', 'bo', 'W1', 'b1', 'W2', 'b2', 'ln1_g', 'ln1_b', 'ln2_g', 'ln2_b')}
    del _L0_mix_all

    def _L0_ffn_setup():
        import jax, jax.numpy as jnp
        import numpy as np
        TOP_K = 2
        LN_EPS = 1e-05
        key = jax.random.key(seed)
        ks = jax.random.split(key, 8)
        B, S, D, E, H = (16, 1024, 256, 8, 1024)
        x = jax.random.normal(ks[0], (B, S, D), dtype=jnp.float32)
        Wr = jax.random.normal(ks[1], (D, E), dtype=jnp.float32) * 0.1
        br = jnp.zeros((E,), dtype=jnp.float32)
        ln_g = jnp.ones((E, D), dtype=jnp.float32)
        ln_b = jnp.zeros((E, D), dtype=jnp.float32)
        W1 = jax.random.normal(ks[2], (E, D, H), dtype=jnp.float32) * (1.0 / np.sqrt(D))
        b1 = jnp.zeros((E, H), dtype=jnp.float32)
        W2 = jax.random.normal(ks[3], (E, H, D), dtype=jnp.float32) * (1.0 / np.sqrt(H))
        b2 = jnp.zeros((E, D), dtype=jnp.float32)
        return {'x': x, 'Wr': Wr, 'br': br, 'ln_g': ln_g, 'ln_b': ln_b, 'W1': W1, 'b1': b1, 'W2': W2, 'b2': b2}
    _L0_ffn_all = _L0_ffn_setup()
    _L0_ffn_in = {k: v for k, v in _L0_ffn_all.items() if k in ('Wr', 'br', 'ln_g', 'ln_b', 'W1', 'b1', 'W2', 'b2')}
    del _L0_ffn_all

    def _L1_gnn_setup():
        import jax, jax.numpy as jnp
        import numpy as np
        N, E, D = (50000, 25000, 256)
        H, B, A = (8, 4, 3)
        F = D // H
        G = 64
        EPS = 1e-05

        def _forward(node, W_bases, W_comb, b_comb, conv_bias, gn_weight, gn_bias, gn_mean_scale, edge_index, batch):
            n = node.shape[0]
            loops = jnp.arange(n, dtype=edge_index.dtype)
            src = jnp.concatenate([edge_index[0], loops])
            dst = jnp.concatenate([edge_index[1], loops])
            deg = jax.ops.segment_sum(jnp.ones_like(src, dtype=node.dtype), dst, num_segments=n)
            dinv = jnp.where(deg > 0, jax.lax.rsqrt(deg), 0.0)
            sym_w = dinv[src] * dinv[dst]
            bases = node @ W_bases
            comb = node @ W_comb + b_comb
            msg = bases[src]
            agg_sym = jax.ops.segment_sum(msg * sym_w[:, None], dst, num_segments=n)
            agg_sum = jax.ops.segment_sum(msg, dst, num_segments=n)
            agg_max = jax.ops.segment_max(msg, dst, num_segments=n)
            aggregated = jnp.stack([agg_sym, agg_sum, agg_max], axis=1)
            aggregated = aggregated.reshape(n, A * B, F)
            weightings = comb.reshape(n, H, B * A)
            h = jnp.einsum('nhk,nkf->nhf', weightings, aggregated).reshape(n, D) + conv_bias
            counts = jnp.maximum(jax.ops.segment_sum(jnp.ones((n,), node.dtype), batch, num_segments=G), 1.0)
            mean = jax.ops.segment_sum(h, batch, num_segments=G) / counts[:, None]
            hc = h - gn_mean_scale * mean[batch]
            var = jax.ops.segment_sum(hc * hc, batch, num_segments=G) / counts[:, None]
            out = gn_weight * hc * jax.lax.rsqrt(var[batch] + EPS) + gn_bias
            return jax.nn.relu(out)
        key = jax.random.key(seed)
        ks = jax.random.split(key, 8)
        glorot = lambda k, shape: jax.random.normal(k, shape, jnp.float32) * np.sqrt(2.0 / (shape[0] + shape[1])).astype(np.float32)
        return {'node': jax.random.normal(ks[0], (N, D), jnp.float32), 'edge_attr': jax.random.normal(ks[1], (E, 1), jnp.float32), 'W_bases': glorot(ks[2], (D, B * F)), 'W_comb': glorot(ks[3], (D, H * B * A)), 'b_comb': jnp.zeros((H * B * A,), jnp.float32), 'conv_bias': jnp.zeros((D,), jnp.float32), 'gn_weight': jnp.ones((D,), jnp.float32), 'gn_bias': jnp.zeros((D,), jnp.float32), 'gn_mean_scale': jnp.ones((D,), jnp.float32), 'edge_index': jax.random.randint(ks[4], (2, E), 0, N, dtype=jnp.int32), 'batch': jnp.sort(jax.random.randint(ks[5], (N,), 0, G, dtype=jnp.int32))}
    _L1_gnn_all = _L1_gnn_setup()
    _L1_gnn_in = {k: v for k, v in _L1_gnn_all.items() if k in ('W_bases', 'W_comb', 'b_comb', 'conv_bias', 'gn_weight', 'gn_bias', 'gn_mean_scale')}
    del _L1_gnn_all

    def _L1_mix_setup():
        import jax, jax.numpy as jnp
        import numpy as np
        BN_EPS = 1e-05
        key = jax.random.key(seed)
        ks = jax.random.split(key, 4)
        B, N, D = (8, 256, 256)
        outD = 256
        s = 1.0 / np.sqrt(D)
        return {'feature': jax.random.normal(ks[0], (B, N, D), dtype=jnp.float32), 'W_qk': jax.random.normal(ks[1], (2, D, D), dtype=jnp.float32) * s, 'b_qk': jnp.zeros((2, D), dtype=jnp.float32), 'W_v': jax.random.normal(ks[2], (D, outD), dtype=jnp.float32) * s, 'b_v': jnp.zeros((outD,), dtype=jnp.float32), 'gamma': jnp.ones((D,), dtype=jnp.float32), 'beta': jnp.zeros((D,), dtype=jnp.float32)}
    _L1_mix_all = _L1_mix_setup()
    _L1_mix_in = {k: v for k, v in _L1_mix_all.items() if k in ('W_qk', 'b_qk', 'W_v', 'b_v', 'gamma', 'beta')}
    del _L1_mix_all

    def _L1_ffn_setup():
        import jax, jax.numpy as jnp
        import numpy as np
        D_IN, D_HID, D_OUT = (256, 512, 256)
        N_EXPERTS, TOP_K = (64, 2)
        B, S = (8, 128)
        key = jax.random.key(seed)
        ks = jax.random.split(key, 8)
        scale_in = 1.0 / np.sqrt(D_IN)
        scale_hid = 1.0 / np.sqrt(D_HID)
        return {'x': jax.random.normal(ks[0], (B, S, D_IN), dtype=jnp.float32), 'Wr': jax.random.uniform(ks[1], (D_IN, N_EXPERTS), jnp.float32, -scale_in, scale_in), 'br': jax.random.uniform(ks[2], (N_EXPERTS,), jnp.float32, -scale_in, scale_in), 'W1': jax.random.uniform(ks[3], (N_EXPERTS, D_IN, D_HID), jnp.float32, -scale_in, scale_in), 'b1': jax.random.uniform(ks[4], (N_EXPERTS, D_HID), jnp.float32, -scale_in, scale_in), 'W2': jax.random.uniform(ks[5], (N_EXPERTS, D_HID, D_OUT), jnp.float32, -scale_hid, scale_hid), 'b2': jax.random.uniform(ks[6], (N_EXPERTS, D_OUT), jnp.float32, -scale_hid, scale_hid)}
    _L1_ffn_all = _L1_ffn_setup()
    _L1_ffn_in = {k: v for k, v in _L1_ffn_all.items() if k in ('Wr', 'br', 'W1', 'b1', 'W2', 'b2')}
    del _L1_ffn_all
    return {'x': x, 'src': src, 'dst': dst, 'edge_type_8': edge_type_8, 'edge_weight1': edge_weight1, 'L0_gnn_basis': _L0_gnn_in['basis'], 'L0_gnn_comp': _L0_gnn_in['comp'], 'L0_gnn_loop_weight': _L0_gnn_in['loop_weight'], 'L0_gnn_bias_param': _L0_gnn_in['bias_param'], 'L0_mix_Wq': _L0_mix_in['Wq'], 'L0_mix_bq': _L0_mix_in['bq'], 'L0_mix_Wk': _L0_mix_in['Wk'], 'L0_mix_bk': _L0_mix_in['bk'], 'L0_mix_Wv': _L0_mix_in['Wv'], 'L0_mix_bv': _L0_mix_in['bv'], 'L0_mix_Wo': _L0_mix_in['Wo'], 'L0_mix_bo': _L0_mix_in['bo'], 'L0_mix_W1': _L0_mix_in['W1'], 'L0_mix_b1': _L0_mix_in['b1'], 'L0_mix_W2': _L0_mix_in['W2'], 'L0_mix_b2': _L0_mix_in['b2'], 'L0_mix_ln1_g': _L0_mix_in['ln1_g'], 'L0_mix_ln1_b': _L0_mix_in['ln1_b'], 'L0_mix_ln2_g': _L0_mix_in['ln2_g'], 'L0_mix_ln2_b': _L0_mix_in['ln2_b'], 'L0_ffn_Wr': _L0_ffn_in['Wr'], 'L0_ffn_br': _L0_ffn_in['br'], 'L0_ffn_ln_g': _L0_ffn_in['ln_g'], 'L0_ffn_ln_b': _L0_ffn_in['ln_b'], 'L0_ffn_W1': _L0_ffn_in['W1'], 'L0_ffn_b1': _L0_ffn_in['b1'], 'L0_ffn_W2': _L0_ffn_in['W2'], 'L0_ffn_b2': _L0_ffn_in['b2'], 'L1_gnn_W_bases': _L1_gnn_in['W_bases'], 'L1_gnn_W_comb': _L1_gnn_in['W_comb'], 'L1_gnn_b_comb': _L1_gnn_in['b_comb'], 'L1_gnn_conv_bias': _L1_gnn_in['conv_bias'], 'L1_gnn_gn_weight': _L1_gnn_in['gn_weight'], 'L1_gnn_gn_bias': _L1_gnn_in['gn_bias'], 'L1_gnn_gn_mean_scale': _L1_gnn_in['gn_mean_scale'], 'L1_mix_W_qk': _L1_mix_in['W_qk'], 'L1_mix_b_qk': _L1_mix_in['b_qk'], 'L1_mix_W_v': _L1_mix_in['W_v'], 'L1_mix_b_v': _L1_mix_in['b_v'], 'L1_mix_gamma': _L1_mix_in['gamma'], 'L1_mix_beta': _L1_mix_in['beta'], 'L1_ffn_Wr': _L1_ffn_in['Wr'], 'L1_ffn_br': _L1_ffn_in['br'], 'L1_ffn_W1': _L1_ffn_in['W1'], 'L1_ffn_b1': _L1_ffn_in['b1'], 'L1_ffn_W2': _L1_ffn_in['W2'], 'L1_ffn_b2': _L1_ffn_in['b2']}

def reference(x, src, dst, edge_type_8, edge_weight1, L0_gnn_basis, L0_gnn_comp, L0_gnn_loop_weight, L0_gnn_bias_param, L0_mix_Wq, L0_mix_bq, L0_mix_Wk, L0_mix_bk, L0_mix_Wv, L0_mix_bv, L0_mix_Wo, L0_mix_bo, L0_mix_W1, L0_mix_b1, L0_mix_W2, L0_mix_b2, L0_mix_ln1_g, L0_mix_ln1_b, L0_mix_ln2_g, L0_mix_ln2_b, L0_ffn_Wr, L0_ffn_br, L0_ffn_ln_g, L0_ffn_ln_b, L0_ffn_W1, L0_ffn_b1, L0_ffn_W2, L0_ffn_b2, L1_gnn_W_bases, L1_gnn_W_comb, L1_gnn_b_comb, L1_gnn_conv_bias, L1_gnn_gn_weight, L1_gnn_gn_bias, L1_gnn_gn_mean_scale, L1_mix_W_qk, L1_mix_b_qk, L1_mix_W_v, L1_mix_b_v, L1_mix_gamma, L1_mix_beta, L1_ffn_Wr, L1_ffn_br, L1_ffn_W1, L1_ffn_b1, L1_ffn_W2, L1_ffn_b2):
    import jax
    import jax.numpy as jnp

    def _L0_gnn_ref(x, src, dst, etypes, basis, comp, loop_weight, bias_param):
        import jax, jax.numpy as jnp
        import numpy as np
        N_NODES = 625
        N_EDGES = 9375
        D = 256
        NUM_RELS = 8
        NUM_BASES = 4
        W = jnp.einsum('rb,bio->rio', comp, basis)
        H = jnp.einsum('ni,rio->nro', x, W)
        msg = H[src, etypes]
        agg = jax.ops.segment_sum(msg, dst, num_segments=N_NODES)
        out = agg + x @ loop_weight + bias_param
        return out

    def _L0_mix_ref(x, Wq, bq, Wk, bk, Wv, bv, Wo, bo, W1, b1, W2, b2, ln1_g, ln1_b, ln2_g, ln2_b):
        import jax, jax.numpy as jnp
        import numpy as np
        D_MODEL = 256
        NHEAD = 8
        D_HEAD = D_MODEL // NHEAD
        DIM_FF = 1024
        B, L = (4, 512)
        LN_EPS = 1e-05

        def _layernorm(x, g, b):
            mu = jnp.mean(x, axis=-1, keepdims=True)
            var = jnp.mean((x - mu) ** 2, axis=-1, keepdims=True)
            return (x - mu) * jax.lax.rsqrt(var + LN_EPS) * g + b

        def _phi(x):
            return jnp.where(x > 0, x + 1.0, jnp.exp(x))
        Bq, Lq, _ = x.shape
        q = (x @ Wq + bq).reshape(Bq, Lq, NHEAD, D_HEAD)
        k = (x @ Wk + bk).reshape(Bq, Lq, NHEAD, D_HEAD)
        v = (x @ Wv + bv).reshape(Bq, Lq, NHEAD, D_HEAD)
        q_phi = _phi(q)
        k_phi = _phi(k)
        kv = jnp.einsum('blhd,blhe->bhde', k_phi, v)
        k_sum = k_phi.sum(axis=1)
        z = 1.0 / (jnp.einsum('blhd,bhd->blh', q_phi, k_sum) + 1e-06)
        out = jnp.einsum('blhd,bhde,blh->blhe', q_phi, kv, z)
        out = out.reshape(Bq, Lq, D_MODEL) @ Wo + bo
        x = _layernorm(x + out, ln1_g, ln1_b)
        ff = jax.nn.relu(x @ W1 + b1) @ W2 + b2
        x = _layernorm(x + ff, ln2_g, ln2_b)
        return x

    def _L0_ffn_ref(x, Wr, br, ln_g, ln_b, W1, b1, W2, b2):
        import jax, jax.numpy as jnp
        import numpy as np
        TOP_K = 2
        LN_EPS = 1e-05
        B, S, D = x.shape
        N = B * S
        xt = x.reshape(N, D)
        logits = xt @ Wr + br
        probs = jax.nn.softmax(logits, axis=-1)
        top_p, top_idx = jax.lax.top_k(probs, TOP_K)
        weights = top_p / top_p.sum(axis=-1, keepdims=True)
        mu = xt.mean(axis=-1, keepdims=True)
        var = ((xt - mu) ** 2).mean(axis=-1, keepdims=True)
        xn = (xt - mu) * jax.lax.rsqrt(var + LN_EPS)
        xe = xn[None, :, :] * ln_g[:, None, :] + ln_b[:, None, :]
        h = jax.nn.gelu(jnp.einsum('end,edh->enh', xe, W1) + b1[:, None, :], approximate=False)
        y = jnp.einsum('enh,ehd->end', h, W2) + b2[:, None, :]
        y_tok = jnp.transpose(y, (1, 0, 2))
        sel = jnp.take_along_axis(y_tok, top_idx[:, :, None], axis=1)
        out = (weights[:, :, None] * sel).sum(axis=1)
        return out.reshape(B, S, D)

    def _L1_gnn_ref(node, edge_attr, W_bases, W_comb, b_comb, conv_bias, gn_weight, gn_bias, gn_mean_scale, edge_index, batch):
        import jax, jax.numpy as jnp
        import numpy as np
        N, E, D = (50000, 25000, 256)
        H, B, A = (8, 4, 3)
        F = D // H
        G = 64
        EPS = 1e-05

        def _forward(node, W_bases, W_comb, b_comb, conv_bias, gn_weight, gn_bias, gn_mean_scale, edge_index, batch):
            n = node.shape[0]
            loops = jnp.arange(n, dtype=edge_index.dtype)
            src = jnp.concatenate([edge_index[0], loops])
            dst = jnp.concatenate([edge_index[1], loops])
            deg = jax.ops.segment_sum(jnp.ones_like(src, dtype=node.dtype), dst, num_segments=n)
            dinv = jnp.where(deg > 0, jax.lax.rsqrt(deg), 0.0)
            sym_w = dinv[src] * dinv[dst]
            bases = node @ W_bases
            comb = node @ W_comb + b_comb
            msg = bases[src]
            agg_sym = jax.ops.segment_sum(msg * sym_w[:, None], dst, num_segments=n)
            agg_sum = jax.ops.segment_sum(msg, dst, num_segments=n)
            agg_max = jax.ops.segment_max(msg, dst, num_segments=n)
            aggregated = jnp.stack([agg_sym, agg_sum, agg_max], axis=1)
            aggregated = aggregated.reshape(n, A * B, F)
            weightings = comb.reshape(n, H, B * A)
            h = jnp.einsum('nhk,nkf->nhf', weightings, aggregated).reshape(n, D) + conv_bias
            counts = jnp.maximum(jax.ops.segment_sum(jnp.ones((n,), node.dtype), batch, num_segments=G), 1.0)
            mean = jax.ops.segment_sum(h, batch, num_segments=G) / counts[:, None]
            hc = h - gn_mean_scale * mean[batch]
            var = jax.ops.segment_sum(hc * hc, batch, num_segments=G) / counts[:, None]
            out = gn_weight * hc * jax.lax.rsqrt(var[batch] + EPS) + gn_bias
            return jax.nn.relu(out)
        del edge_attr
        return _forward(node, W_bases, W_comb, b_comb, conv_bias, gn_weight, gn_bias, gn_mean_scale, edge_index, batch)

    def _L1_mix_ref(feature, W_qk, b_qk, W_v, b_v, gamma, beta):
        import jax, jax.numpy as jnp
        import numpy as np
        BN_EPS = 1e-05
        QK = jnp.einsum('bnd,kde->bkne', feature, W_qk) + b_qk[None, :, None, :]
        value = jnp.einsum('bnd,de->bne', feature, W_v) + b_v
        query = QK[:, 0]
        key = QK[:, 1]
        sm = jax.nn.softmax(key, axis=1)
        lam = jnp.einsum('bnd,bne->bde', sm, value)
        mean = jnp.mean(lam, axis=(0, 2), keepdims=True)
        var = jnp.var(lam, axis=(0, 2), keepdims=True)
        bn = (lam - mean) * jax.lax.rsqrt(var + BN_EPS)
        bn = bn * gamma[None, :, None] + beta[None, :, None]
        return jnp.einsum('bnd,bde->bne', query, bn)

    def _L1_ffn_ref(x, Wr, br, W1, b1, W2, b2):
        import jax, jax.numpy as jnp
        import numpy as np
        D_IN, D_HID, D_OUT = (256, 512, 256)
        N_EXPERTS, TOP_K = (64, 2)
        B, S = (8, 128)
        Bx, Sx, D = x.shape
        xf = x.reshape(-1, D)
        T = xf.shape[0]
        E = Wr.shape[1]
        logits = xf @ Wr + br
        topk_logits, topk_idx = jax.lax.top_k(logits, TOP_K)
        gates = jax.nn.softmax(topk_logits, axis=1)
        combine = jnp.zeros((T, E), xf.dtype).at[jnp.arange(T)[:, None], topk_idx].add(gates)
        out = jnp.zeros((T, W2.shape[-1]), xf.dtype)
        for e in range(E):
            h = jax.nn.relu(xf @ W1[e] + b1[e])
            y = h @ W2[e] + b2[e]
            out = out + combine[:, e:e + 1] * y
        return out.reshape(Bx, Sx, -1)
    edge_index = jnp.stack([src, dst])
    batch0 = jnp.zeros((625,), jnp.int32)
    xn = _layernorm(x, axis=-1)
    x = x + _L0_gnn_ref(xn, src, dst, edge_type_8, L0_gnn_basis, L0_gnn_comp, L0_gnn_loop_weight, L0_gnn_bias_param) + _L0_mix_ref(xn[None], L0_mix_Wq, L0_mix_bq, L0_mix_Wk, L0_mix_bk, L0_mix_Wv, L0_mix_bv, L0_mix_Wo, L0_mix_bo, L0_mix_W1, L0_mix_b1, L0_mix_W2, L0_mix_b2, L0_mix_ln1_g, L0_mix_ln1_b, L0_mix_ln2_g, L0_mix_ln2_b)[0]
    x = x + _L0_ffn_ref(_layernorm(x, axis=-1)[None], L0_ffn_Wr, L0_ffn_br, L0_ffn_ln_g, L0_ffn_ln_b, L0_ffn_W1, L0_ffn_b1, L0_ffn_W2, L0_ffn_b2)[0]
    xn = _layernorm(x, axis=-1)
    x = x + _L1_gnn_ref(xn, edge_weight1, L1_gnn_W_bases, L1_gnn_W_comb, L1_gnn_b_comb, L1_gnn_conv_bias, L1_gnn_gn_weight, L1_gnn_gn_bias, L1_gnn_gn_mean_scale, edge_index, batch0) + _L1_mix_ref(xn[None], L1_mix_W_qk, L1_mix_b_qk, L1_mix_W_v, L1_mix_b_v, L1_mix_gamma, L1_mix_beta)[0]
    x = x + _L1_ffn_ref(_layernorm(x, axis=-1)[None], L1_ffn_Wr, L1_ffn_br, L1_ffn_W1, L1_ffn_b1, L1_ffn_W2, L1_ffn_b2)[0]
    return x

_drawn_inputs = setup_inputs


def setup_inputs(seed=0):
    import zlib

    import numpy as np

    out = dict(_drawn_inputs(seed))
    spreads = {'L0_gnn_bias_param': (0.0, 0.1),
     'L0_mix_bq': (0.0, 2.0),
     'L0_mix_bk': (0.0, 2.0),
     'L0_mix_bv': (0.0, 0.1),
     'L0_mix_bo': (0.0, 0.1),
     'L0_mix_b1': (0.0, 0.392),
     'L0_mix_b2': (0.0, 0.1),
     'L0_mix_ln1_g': (1.0, 0.6),
     'L0_mix_ln1_b': (0.0, 0.1),
     'L0_mix_ln2_g': (1.0, 0.2),
     'L0_mix_ln2_b': (0.0, 0.1),
     'L0_ffn_br': (0.0, 0.535),
     'L0_ffn_ln_g': (1.0, 0.6),
     'L0_ffn_ln_b': (0.0, 0.77),
     'L0_ffn_b1': (0.0, 0.8),
     'L0_ffn_b2': (0.0, 0.489),
     'L1_gnn_b_comb': (0.0, 0.8),
     'L1_gnn_conv_bias': (0.0, 2.0),
     'L1_gnn_gn_weight': (1.0, 0.6),
     'L1_gnn_gn_bias': (0.0, 0.8),
     'L1_gnn_gn_mean_scale': (1.0, 0.6),
     'L1_mix_b_qk': (0.0, 0.1),
     'L1_mix_b_v': (0.0, 0.1),
     'L1_mix_gamma': (1.0, 0.2),
     'L1_mix_beta': (0.0, 0.1)}
    factors = {'L0_mix_Wq': 8.0,
     'L0_mix_Wk': 8.0,
     'L0_mix_Wv': 3.308,
     'L1_ffn_Wr': 7.01,
     'L1_ffn_br': 8.0,
     'L1_ffn_W1': 8.0,
     'L1_ffn_b1': 8.0,
     'L1_ffn_W2': 6.994,
     'L1_ffn_b2': 63.508}
    for name, (base, spread) in spreads.items():
        noise = np.random.default_rng([zlib.crc32(name.encode()), seed]).standard_normal(out[name].shape)
        drawn = base * np.exp(spread * noise) if base else spread * noise
        out[name] = jnp.asarray(drawn.astype(out[name].dtype))
    for name, factor in factors.items():
        out[name] = (out[name] * factor).astype(out[name].dtype)
    return out
```

```python
from contextlib import ExitStack

import concourse.bass as bass
from concourse import mybir

F32 = mybir.dt.float32
BF16 = mybir.dt.bfloat16
I32 = mybir.dt.int32
U32 = mybir.dt.uint32
ALU = mybir.AluOpType
ACT = mybir.ActivationFunctionType
AX = mybir.AxisListType

N = 625
TP = 125
NT = N // TP
D = 256
KD = D // 128
NP = N + 1
HN = NP // 2
E = 20625
EP = 125
EC = E // EP
R0 = 8
NB0 = 4
DFF = 1024
E0, H0 = 8, 1024
E1, H1 = 64, 512
DB = 128
NH, NK, FH = 8, 12, 32
GRING = 15
BIG = 2.0 ** 120
EPS = 1e-5

VECS = [("bq", 2), ("b1", 8), ("bqk", 4), ("gamma", 2), ("beta", 2), ("eg", 16), ("eb", 16), ("eb1", 64)]
VCOL, _n = {}, 0
for _name, _k in VECS:
    VCOL[_name] = _n
    _n += _k
NVEC = _n
ROWS = ["bk", "bv", "bo", "b2", "ln1_g", "ln1_b", "ln2_g", "ln2_b", "gbias", "cbias", "gnw", "gnb", "gnms", "lbv"]


class Chain:

    def __init__(self, eng, sem):
        self.eng, self.sem, self.n, self.off = eng, sem, 0, None

    def mark(self, ins):
        self.n += 1
        ins.then_inc(self.sem, 1)

    def wait(self):
        self.eng.wait_ge(self.sem, self.n if self.off is None else self.off + self.n)

    def done(self, ins):
        self.mark(ins)
        self.wait()

    def enter(self, i, k):
        self.off, self.k, self.n0 = i * k, k, self.n

    def leave(self, count):
        assert self.n - self.n0 == self.k, (self.n - self.n0, self.k)
        self.n, self.off = self.n0 + self.k * count, None


def gps_kernel(nc, a):
    with ExitStack() as ctx:
        def sb(name, shape, dt=F32):
            return ctx.enter_context(nc.sbuf_tensor(name, shape, dt))

        def sem(name):
            return ctx.enter_context(nc.semaphore(name))

        ps = ctx.enter_context(nc.psum_tensor("ps", [128, 8, 512], F32))
        iota_f = sb("iota_f", [128, N])
        ident = sb("ident", [128, 128])
        identb = sb("identb", [128, 128], BF16)
        headmask = sb("headmask", [128, 128])
        ones = sb("ones", [128, 128])
        zerob = sb("zerob", [128, 512], BF16)
        srcs = sb("srcs", [EP, EC], I32)
        dsts = sb("dsts", [EP, EC], I32)
        types = sb("types", [EP, EC], I32)
        srcf = sb("srcf", [EP, EC])
        dstf = sb("dstf", [EP, EC])
        rowid = sb("rowid", [EP, EC], I32)
        vecrows = sb("vecrows", [128, 128])
        vecs = sb("vecs", [128, NVEC])
        rows = sb("rows", [128, len(ROWS), D])
        comp = sb("comp", [128, R0 * NB0])
        rb0 = sb("rb0", [128, E0])
        rb1 = sb("rb1", [128, E1])
        bcomb = sb("bcomb", [128, NH * NK])
        b1rows = sb("b1rows", [128, 2, 128])
        b1cols = sb("b1cols", [128, E1 * 4])
        b2e0 = sb("b2e0", [E0, D])
        b2e1 = sb("b2e1", [E1, D])
        shared = sb("shared", [128, 8192])
        basis = shared[:, 0:NB0 * KD * D].rearrange("p (b c d) -> p b c d", b=NB0, c=KD)
        wrel = shared[:, NB0 * KD * D:(NB0 + R0) * KD * D].rearrange("p (c r d) -> p c r d", c=KD, r=R0)
        wa = shared[:, 0:4096].rearrange("p (s n) -> p s n", s=2)
        wb = shared[:, 4096:8192].rearrange("p (s n) -> p s n", s=2)
        loopw = sb("loopw", [128, KD, D])
        wq = sb("wq", [128, KD, D])
        wkv = sb("wkv", [128, KD, 2 * D])
        wo = sb("wo", [128, KD, D])
        w1 = sb("w1", [128, KD, DFF])
        w2 = sb("w2", [128, DFF // 128, D])
        wr0 = sb("wr0", [128, KD, E0])
        wr1 = sb("wr1", [128, KD, E1])
        wbc = sb("wbc", [128, KD, DB + NH * NK])
        lwq, lwk, lwv = wq, wkv[:, :, 0:D], wkv[:, :, D:2 * D]
        x = sb("x", [TP, NT, D])
        xn = sb("xn", [TP, NT, D])
        xnT = sb("xnT", [128, KD, NP])
        xT2 = sb("xT2", [128, KD, NP])
        ya = sb("ya", [TP, NT, D])
        yb = sb("yb", [TP, NT, D])
        stats = sb("stats", [TP, NT, 6])
        mv = sb("mv", [TP, NT, 2])
        rstd = sb("rstd", [TP, NT])
        adjT = sb("adjT", [TP, NT, N])
        maskb = sb("maskb", [TP, NT, N], BF16)
        onehot = sb("onehot", [EP, 3, N])
        ohf = onehot
        ohb = onehot[:, :, :].rearrange("p s n -> p (s n)").bitcast(BF16).rearrange("p (s w n) -> p s w n",
                                                                                    s=3, w=2)
        ohs, ohd = ohb[:, :, 0, :], ohb[:, :, 1, :]
        stage = sb("stage", [TP, 2 * R0 * D])
        hrow = stage[:, :].rearrange("p (s n) -> p s n", s=2)
        gath = stage[:, 0:GRING * D].rearrange("p (s d) -> p s d", s=GRING)
        big = sb("big", [128, 8, NP])
        qphi = sb("qphi", [128, KD, NP])
        kphi = sb("kphi", [TP, NT, D])
        vext = big[0:TP, :, :].rearrange("p a b -> p (a b)")[:, 0:NT * KD * 129].rearrange(
            "p (t c n) -> p t c n", t=NT, c=KD)
        kvbd = sb("kvbd", [128, KD, 128])
        ksbd = sb("ksbd", [128, KD, 128])
        tmpf = sb("tmpf", [128, NP])
        scr = sb("scr", [128, NP])
        tmpg = scr
        tmpr = scr[0:TP, 0:2 * D]
        lg = sb("lg", [TP, NT, E1])
        lg2 = sb("lg2", [TP, NT, E1])
        m8 = sb("m8", [TP, NT, 8])
        i8 = sb("i8", [TP, NT, 8], U32)
        i8f = sb("i8f", [TP, NT, 8])
        gate = sb("gate", [TP, NT, 4])
        comb = sb("comb", [TP, NT, E1])
        combT = sb("combT", [128, N])
        bas = yb
        basT = combT
        wgt = sb("wgt", [TP, NT, NH * NK])
        agg = big[0:TP, :, :].rearrange("p a b -> p (a b)")[:, 0:NT * 3 * DB].rearrange("p (t n) -> p t n", t=NT)
        aggmT = xT2[:, 0, 0:N]
        deg = sb("deg", [TP, NT])
        dinv = sb("dinv", [TP, NT])
        prod = scr[0:TP, 0:D]
        max5 = sb("max5", [128, 5])
        held = sb("held", [128, 1])
        gmean = sb("gmean", [128, D])
        kmax = sb("kmax", [128, KD])
        ksum = sb("ksum", [128, KD])
        lam = tmpf[:, 0:KD * D].rearrange("p (c d) -> p c d", c=KD)
        lst = sb("lst", [128, KD, 6])
        lmv = sb("lmv", [128, KD, 2])
        lrs = sb("lrs", [128, KD])
        smx = bas

        msgs = nc.dram_tensor("msgs", [N * R0, D], F32, kind="Internal")

        ld_edges = sem("ld_edges")
        ld_x = sem("ld_x")
        ld_vec = sem("ld_vec")
        ld_w, ld_lw = sem("ld_w"), sem("ld_lw")
        consts_ready = sem("consts_ready")
        dchain, achain, pchain = sem("dve_step"), sem("act_step"), sem("pool_step")
        edges_ready = sem("edges_ready")
        oh_ready, oh_used = sem("oh_ready"), sem("oh_used")
        adj_mm, adj_ready = sem("adj_mm"), sem("adj_ready")
        var_ready, rstd_ready = sem("var_ready"), sem("rstd_ready")
        norm_ready = sem("norm_ready")
        tr_mm, tr_copied = sem("tr_mm"), sem("tr_copied")
        wrel_ready = sem("wrel_ready")
        h_mm, h_copied, h_stored = sem("h_mm"), sem("h_copied"), sem("h_stored")
        gathered = [sem(f"gathered{i}") for i in range(GRING)]
        g_oh, g_used, g_done = sem("g_oh"), sem("g_used"), sem("g_done")
        m_mm, m_out, m_pre, m_exp = sem("m_mm"), sem("m_out"), sem("m_pre"), sem("m_exp")
        m_relu = sem("m_relu")
        moe_w = [sem("moe_w0"), sem("moe_w1")]
        moe_used = sem("moe_used")
        moe_x, moe_h, moe_act, moe_y, moe_acc = (sem("moe_x"), sem("moe_h"), sem("moe_act"), sem("moe_y"),
                                                 sem("moe_acc"))
        r_mm, r_out, r_pre, r_exp = sem("r_mm"), sem("r_out"), sem("r_pre"), sem("r_exp")
        c_mm, c_out = sem("c_mm"), sem("c_out")
        mx_mm, mx_out, mx_kept = sem("mx_mm"), sem("mx_out"), sem("mx_kept")
        l_mm, l_out, l_pre, l_exp = sem("l_mm"), sem("l_out"), sem("l_pre"), sem("l_exp")
        o_ready, o_stored = sem("o_ready"), sem("o_stored")

        def node_major(ap):
            return ap.rearrange("(t p) d -> p t d", p=TP)

        def chunked(ap):
            return ap.rearrange("(c p) d -> p c d", p=128)

        def row(name, parts=TP):
            return rows[0:parts, ROWS.index(name), :]

        def row_ap(ap, parts=128):
            return ap.partition_broadcast(parts)

        n_vec = len(VECS) + 1 + len(ROWS) + 5
        n_w = 13

        block = ctx.enter_context(nc.Block())

        @block.sync
        def _(sp):
            for dst, src in ((srcs, a["src"]), (dsts, a["dst"]), (types, a["edge_type_8"])):
                sp.dma_start(dst[:, :], src.rearrange("(p c) -> p c", p=EP)).then_inc(ld_edges, 16)
            sp.dma_start(x[:, :, :], node_major(a["x"])).then_inc(ld_x, 16)
            for name, src in (("bq", a["L0_mix_bq"]), ("b1", a["L0_mix_b1"]),
                              ("bqk", a["L1_mix_b_qk"].rearrange("k d -> (k d)")),
                              ("gamma", a["L1_mix_gamma"]), ("beta", a["L1_mix_beta"]),
                              ("eg", a["L0_ffn_ln_g"].rearrange("e d -> (e d)")),
                              ("eb", a["L0_ffn_ln_b"].rearrange("e d -> (e d)")),
                              ("eb1", a["L0_ffn_b1"].rearrange("e d -> (e d)"))):
                v = src.rearrange("(r c) -> r c", c=128)
                sp.dma_start(vecrows[VCOL[name]:VCOL[name] + v.shape[0], :], v).then_inc(ld_vec, 16)
            sp.dma_start(b1rows[:, :, :], a["L1_ffn_b1"].rearrange("e (j c) -> (e j) c", c=128)
                         .rearrange("(h r) c -> r h c", r=128)).then_inc(ld_vec, 16)
            for name, src in zip(ROWS, (a["L0_mix_bk"], a["L0_mix_bv"], a["L0_mix_bo"], a["L0_mix_b2"],
                                        a["L0_mix_ln1_g"], a["L0_mix_ln1_b"], a["L0_mix_ln2_g"],
                                        a["L0_mix_ln2_b"], a["L0_gnn_bias_param"], a["L1_gnn_conv_bias"],
                                        a["L1_gnn_gn_weight"], a["L1_gnn_gn_bias"],
                                        a["L1_gnn_gn_mean_scale"], a["L1_mix_b_v"])):
                sp.dma_start(rows[:, ROWS.index(name), :], row_ap(src)).then_inc(ld_vec, 16)
            sp.dma_start(comp[:, :], row_ap(a["L0_gnn_comp"].rearrange("r b -> (r b)"))).then_inc(ld_vec, 16)
            sp.dma_start(rb0[:, :], row_ap(a["L0_ffn_br"])).then_inc(ld_vec, 16)
            sp.dma_start(rb1[:, :], row_ap(a["L1_ffn_br"])).then_inc(ld_vec, 16)
            sp.dma_start(bcomb[:, :], row_ap(a["L1_gnn_b_comb"])).then_inc(ld_vec, 16)
            sp.dma_start(b2e0[:, :], a["L0_ffn_b2"]).then_inc(ld_vec, 16)
            n = 0
            for dst, src in ((basis[:, :, :, :], a["L0_gnn_basis"].rearrange("b (c p) d -> p b c d", p=128)),
                             (loopw[:, :, :], chunked(a["L0_gnn_loop_weight"])),
                             (wq[:, :, :], chunked(a["L0_mix_Wq"])),
                             (wkv[:, :, 0:D], chunked(a["L0_mix_Wk"])),
                             (wkv[:, :, D:2 * D], chunked(a["L0_mix_Wv"])),
                             (wo[:, :, :], chunked(a["L0_mix_Wo"])),
                             (w1[:, :, :], chunked(a["L0_mix_W1"])),
                             (w2[:, :, :], chunked(a["L0_mix_W2"])),
                             (wr0[:, :, :], chunked(a["L0_ffn_Wr"])),
                             (wr1[:, :, :], chunked(a["L1_ffn_Wr"])),
                             (wbc[:, :, 0:DB], chunked(a["L1_gnn_W_bases"])),
                             (wbc[:, :, DB:], chunked(a["L1_gnn_W_comb"])),
                             (b2e1[:, :], a["L1_ffn_b2"])):
                sp.dma_start(dst, src).then_inc(ld_w, 16)
                n += 1
            hd = msgs.ap().rearrange("(t p r) d -> t p (r d)", p=TP, r=R0)
            for t in range(NT):
                sp.wait_ge(h_copied, 4 * (t + 1))
                sp.dma_start(hd[t], hrow[:, t % 2, :]).then_inc(h_stored, 16)
                sp.wait_ge(h_stored, 16 * (t + 1))
            sp.wait_ge(m_mm, 7)
            for dst, src in ((lwq, a["L1_mix_W_qk"][0]), (lwk, a["L1_mix_W_qk"][1]), (lwv, a["L1_mix_W_v"])):
                sp.dma_start(dst[:, :, :], chunked(src)).then_inc(ld_lw, 16)
            for (first, w1d, w2d, ne, c1, c2) in ((0, a["L0_ffn_W1"], a["L0_ffn_W2"], E0, KD, H0 // 128),
                                                  (E0, a["L1_ffn_W1"], a["L1_ffn_W2"], E1, KD, H1 // 128)):
                w1v = w1d.rearrange("e (c p) h -> e p c h", p=128)
                w2v = w2d.rearrange("e (c p) d -> e p c d", p=128)
                f = w1d.shape[2]
                with sp.Fori(0, ne // 2) as i:
                    for u in range(2):
                        if first:
                            sp.wait_ge(moe_used, i * 2 + (first + u - 1))
                        elif True:
                            sp.wait_ge(moe_used, i * 2 + max(u - 1, 0))
                        sp.dma_start(wa[:, u, 0:c1 * f].rearrange("p (c h) -> p c h", c=c1),
                                     w1v[bass.ds(i * 2 + u, 1)].rearrange("o p c h -> p (o c) h")
                                     ).then_inc(moe_w[u], 16)
                        sp.dma_start(wb[:, u, 0:c2 * D].rearrange("p (c h) -> p c h", c=c2),
                                     w2v[bass.ds(i * 2 + u, 1)].rearrange("o p c h -> p (o c) h")
                                     ).then_inc(moe_w[u], 16)
            sp.wait_ge(o_ready, NT)
            sp.dma_start(node_major(a["out"]), x[:, :, :]).then_inc(o_stored, 16)
            sp.wait_ge(o_stored, 16)

        @block.gpsimd
        def _(pool):
            step = Chain(pool, pchain)
            pool.iota(iota_f[:, :], pattern=[[1, N]], base=0, channel_multiplier=0,
                      allow_small_or_imprecise_dtypes=True).then_inc(consts_ready, 1)
            step.done(pool.memset(ident[:, :], 0.0))
            step.done(pool.affine_select(out=ident[:, :], in_=ident[:, :], compare_op=ALU.not_equal, fill=1.0,
                                         base=0, pattern=[[-1, 128]], channel_multiplier=1))
            pool.tensor_copy(identb[:, :], ident[:, :]).then_inc(consts_ready, 1)
            step.done(pool.memset(headmask[:, :], 0.0))
            for h in range(4):
                step.done(pool.memset(headmask[32 * h:32 * h + 32, 32 * h:32 * h + 32], 1.0))
            pool.memset(ones[:, :], 1.0).then_inc(consts_ready, 1)
            pool.wait_ge(edges_ready, 3)
            pool.wait_ge(h_stored, 16 * NT)
            for c in range(EC):
                if c >= GRING:
                    pool.wait_ge(g_used, c - GRING + 1)
                pool.indirect_dma_start(gath[:, c % GRING, :], None, msgs.ap(),
                                        bass.IndirectOffsetOnAxis(ap=rowid[:, c:c + 1].bitcast(U32), axis=0)
                                        ).then_inc(gathered[c % GRING], 16)

        @block.tensor
        def _(pe):
            pe.wait_ge(consts_ready, 4)

            npass = 0
            for tiles in ((0, 1, 2), (3, 4)):
                if npass:
                    pe.wait_ge(adj_ready, 3)
                for k in range(2 * len(tiles)):
                    pe.matmul(ps[0:TP, k, :], zerob[:, 0:TP], zerob[:, :], start=True, stop=True)
                base = npass * EC
                with pe.Fori(0, EC // 3) as i:
                    for u in range(3):
                        pe.wait_ge(oh_ready, i * 3 + (base + u + 1))
                        sl = (u + base) % 3
                        for k, s in enumerate(tiles):
                            for b, (lo, hi) in enumerate(((0, 512), (512, N))):
                                m = pe.matmul(ps[0:TP, 2 * k + b, 0:hi - lo], ohs[:, sl, s * TP:(s + 1) * TP],
                                              ohd[:, sl, lo:hi], start=False, stop=False, skip_group_check=True)
                        m.then_inc(oh_used, 1)
                for k in range(2 * len(tiles)):
                    m = pe.matmul(ps[0:TP, k, :], zerob[:, 0:TP], zerob[:, :], start=False, stop=True,
                                  skip_group_check=True)
                m.then_inc(adj_mm, 1)
                npass += 1
            for d in range(NT):
                pe.wait_ge(adj_ready, 5 if d == 0 else 5 + d)
                for s in range(NT):
                    bk, off = (0, s * TP) if s < 4 else (1, 0)
                    m = pe.transpose(ps[0:TP, bk, off:off + TP], adjT[:, s, d * TP:(d + 1) * TP],
                                     ident[0:TP, 0:TP])
                m.then_inc(adj_mm, 1)

            ntr = [0]

            def turn(src, ready, count, b0=0):
                pe.wait_ge(ready, count)
                for j in range(KD):
                    for t in range(NT):
                        bk, off = (b0 + j, t * TP) if t < 4 else (b0 + 2, j * TP)
                        m = pe.transpose(ps[:, bk, off:off + TP], src[:, t, j * 128:(j + 1) * 128],
                                         ident[0:TP, 0:TP])
                m.then_inc(tr_mm, 1)
                ntr[0] += 1

            def turned():
                pe.wait_ge(tr_copied, ntr[0])

            pe.wait_ge(adj_ready, 10)
            pe.wait_ge(ld_vec, 16 * n_vec)
            pe.transpose(ps[:, 0, 0:NVEC], vecrows[0:NVEC, :], ident[0:NVEC, 0:NVEC])
            pe.transpose(ps[:, 1, 0:128], b1rows[:, 0, :], ident[:, :])
            pe.transpose(ps[:, 1, 128:256], b1rows[:, 1, :], ident[:, :]).then_inc(tr_mm, 1)
            ntr[0] += 1
            turned()

            turn(xn, norm_ready, 1)
            turned()
            pe.wait_ge(ld_w, 16 * n_w)
            pe.wait_ge(wrel_ready, 1)
            for t in range(NT):
                for g in range(4):
                    n = 4 * t + g
                    if n >= 4:
                        pe.wait_ge(h_copied, n - 3)
                    for k in range(KD):
                        m = pe.matmul(ps[0:TP, g, :], xnT[:, k, t * TP:(t + 1) * TP],
                                      wrel[:, k, 2 * g:2 * g + 2, :].rearrange("p r d -> p (r d)"),
                                      start=(k == 0), stop=(k == KD - 1))
                    m.then_inc(h_mm, 1)

            nm = [0]

            def product(m):
                nm[0] += 1
                m.then_inc(m_mm, 1)

            def feature_major(w, src, j, b0, w_off=0):
                for hf in range(2):
                    for k in range(KD):
                        m = pe.matmul(ps[:, b0 + hf, 0:HN], w[:, k, w_off + j * 128:w_off + (j + 1) * 128],
                                      src[:, k, hf * HN:(hf + 1) * HN], start=(k == 0), stop=(k == KD - 1))
                return m

            pe.wait_ge(h_copied, 4 * NT)
            for j in range(KD):
                product(feature_major(wq, xnT, j, 2 * j))
            for t in range(NT):
                if t == 1:
                    pe.wait_ge(m_out, 1)
                if t >= 2:
                    pe.wait_ge(m_out, t + 1)
                for k in range(KD):
                    m = pe.matmul(ps[0:TP, 4 * (1 - t % 2), :], xnT[:, k, t * TP:(t + 1) * TP], wkv[:, k, :],
                                  start=(k == 0), stop=(k == KD - 1))
                product(m)
            pe.wait_ge(m_out, 7)
            for j in range(KD):
                for t in range(NT):
                    m = pe.matmul(ps[:, j, 0:129], kphi[:, t, j * 128:(j + 1) * 128], vext[:, t, j, :],
                                  start=(t == 0), stop=(t == NT - 1))
            product(m)
            pe.wait_ge(m_out, 8)
            for j in range(KD):
                if j:
                    pe.wait_ge(m_out, 9)
                for hf in range(2):
                    pe.matmul(ps[:, 2 + hf, 0:HN], ksbd[:, j, :], qphi[:, j, hf * HN:(hf + 1) * HN],
                              start=True, stop=True)
                    m = pe.matmul(ps[:, hf, 0:HN], kvbd[:, j, :], qphi[:, j, hf * HN:(hf + 1) * HN],
                                  start=True, stop=True)
                product(m)
            pe.wait_ge(m_out, 10)
            for t in range(NT):
                if t >= 2:
                    pe.wait_ge(m_out, 10 + t - 1)
                for k in range(KD):
                    m = pe.matmul(ps[0:TP, t % 2, 0:D], xT2[:, k, t * TP:(t + 1) * TP], wo[:, k, :],
                                  start=(k == 0), stop=(k == KD - 1))
                product(m)
            pe.wait_ge(m_out, 15)
            turn(ya, norm_ready, 2)
            turned()
            for m8_ in range(8):
                if m8_ >= 2:
                    pe.wait_ge(m_relu, m8_ - 1)
                product(feature_major(w1, xT2, m8_, 2 * (m8_ % 2)))
            pe.wait_ge(m_relu, 8)
            for t in range(NT):
                if t >= 2:
                    pe.wait_ge(m_out, 15 + t - 1)
                for k in range(8):
                    m = pe.matmul(ps[0:TP, t % 2, 0:D], big[:, k, t * TP:(t + 1) * TP], w2[:, k, :],
                                  start=(k == 0), stop=(k == 7))
                product(m)

            def acc(t):
                return ps[0:TP, 5 + t // 2, (t % 2) * D:(t % 2 + 1) * D]

            for b in range(3):
                pe.matmul(ps[0:TP, 5 + b, :], zerob[:, 0:TP], zerob[:, :], start=True, stop=True)
            for t in range(NT):
                for k in range(KD):
                    pe.matmul(acc(t), xnT[:, k, t * TP:(t + 1) * TP], loopw[:, k, :], start=False, stop=False,
                              skip_group_check=True)
            with pe.Fori(0, EC // GRING) as i:
                for u in range(GRING):
                    pe.wait_ge(g_oh, i * GRING + (u + 1))
                    pe.wait_ge(gathered[u], i * 16 + 16)
                    for t in range(NT):
                        m = pe.matmul(acc(t), ohf[:, u % 3, t * TP:(t + 1) * TP], gath[:, u, :], start=False,
                                      stop=False, skip_group_check=True)
                    m.then_inc(g_used, 1)
            for b in range(3):
                m = pe.matmul(ps[0:TP, 5 + b, :], zerob[:, 0:TP], zerob[:, :], start=False, stop=True,
                              skip_group_check=True)
            m.then_inc(g_done, 1)

            moe = dict(h=0, y=0, r=0, x=0, e=0)

            def experts(ne, nh, w_r, b2, ready, logits_src, exp_src, per_expert_x):
                for t in range(NT):
                    for k in range(KD):
                        m = pe.matmul(ps[0:TP, 6, t * ne:(t + 1) * ne], logits_src[:, k, t * TP:(t + 1) * TP],
                                      w_r[:, k, :], start=(k == 0), stop=(k == KD - 1))
                m.then_inc(r_mm, 1)
                moe["r"] += 1
                pe.wait_ge(r_out, moe["r"])
                for t in range(NT):
                    bk, off = (6, t * TP) if t < 4 else (7, 0)
                    m = pe.transpose(ps[0:ne, bk, off:off + TP], comb[:, t, 0:ne], ident[0:TP, 0:TP])
                m.then_inc(r_mm, 1)
                moe["r"] += 1
                pe.wait_ge(r_out, moe["r"])
                y0 = moe["y"]
                for t in range(NT):
                    if t >= 2:
                        pe.wait_ge(moe_acc, y0 + t - 1)
                    pe.matmul(ps[0:TP, 4 + t % 2, 0:D], combT[0:ne, t * TP:(t + 1) * TP], b2[:, :], start=True,
                              stop=True).then_inc(moe_y, 1)
                moe["y"] = y0 + NT
                pe.wait_ge(moe_acc, moe["y"])
                h0, y0, x0, e0 = moe["h"], moe["y"], moe["x"], moe["e"]
                with pe.Fori(0, ne // 2) as i:
                    for u in range(2):
                        pe.wait_ge(moe_w[u], i * 32 + (e0 // 2 * 32 + 32))
                        if per_expert_x:
                            pe.wait_ge(moe_x, i * 2 + (x0 + u + 1))
                        wav = wa[:, u, 0:KD * nh * 128].rearrange("p (c h) -> p c h", c=KD)
                        wbv = wb[:, u, 0:nh * D].rearrange("p (c h) -> p c h", c=nh)
                        for m_ in range(nh):
                            q = u * nh + m_
                            if h0 + q >= 2:
                                pe.wait_ge(moe_act, i * (2 * nh) + (h0 + q - 1))
                            elif q == 1:
                                pe.wait_ge(moe_act, i * (2 * nh))
                            else:
                                pe.wait_ge(moe_act, i * (2 * nh))
                            feature_major(wav, exp_src, m_, 2 * (m_ % 2)).then_inc(moe_h, 1)
                        pe.wait_ge(moe_act, i * (2 * nh) + (h0 + (u + 1) * nh))
                        for t in range(NT):
                            pe.wait_ge(moe_acc, i * (2 * NT) + (y0 + u * NT + t - 1))
                            for k in range(nh):
                                m = pe.matmul(ps[0:TP, 4 + (u * NT + t) % 2, 0:D], big[:, k, t * TP:(t + 1) * TP],
                                              wbv[:, k, :], start=(k == 0), stop=(k == nh - 1))
                            m.then_inc(moe_y, 1)
                        m = pe.matmul(ps[0:1, 7, 0:1], zerob[:, 0:1], zerob[:, 0:1], start=True, stop=True)
                        m.then_inc(moe_used, 1)
                moe["h"], moe["y"], moe["e"] = h0 + ne * nh, y0 + ne * NT, e0 + ne
                moe["x"] = x0 + (ne if per_expert_x else 0)

            turn(ya, norm_ready, 3)
            turned()
            turn(xn, norm_ready, 4)
            turned()
            experts(E0, H0 // 128, wr0, b2e0, None, xT2, qphi, True)

            turn(xn, norm_ready, 5)
            turned()
            nc_ = [0]

            def cproduct(m):
                nc_[0] += 1
                m.then_inc(c_mm, 1)

            for t in range(NT):
                if t >= 2:
                    pe.wait_ge(c_out, t - 1)
                for k in range(KD):
                    m = pe.matmul(ps[0:TP, t % 2, 0:DB + NH * NK], xnT[:, k, t * TP:(t + 1) * TP], wbc[:, k, :],
                                  start=(k == 0), stop=(k == KD - 1))
                cproduct(m)
            for hf in range(2):
                for k in range(KD):
                    m = pe.matmul(ps[:, 2 + hf, 0:HN], wbc[:, k, 0:DB], xnT[:, k, hf * HN:(hf + 1) * HN],
                                  start=(k == 0), stop=(k == KD - 1))
            cproduct(m)
            pe.wait_ge(c_out, 5)
            for t in range(NT):
                for s in range(NT):
                    m = pe.matmul(ps[0:TP, 4, t:t + 1], adjT[:, s, t * TP:(t + 1) * TP], ones[0:TP, 0:1],
                                  start=(s == 0), stop=(s == NT - 1))
            cproduct(m)
            pe.wait_ge(c_out, 7)
            for t in range(NT):
                if t >= 2:
                    pe.wait_ge(c_out, 7 + t - 1)
                for s in range(NT):
                    m = pe.matmul(ps[0:TP, t % 2, 0:2 * DB], adjT[:, s, t * TP:(t + 1) * TP], bas[:, s, :],
                                  start=(s == 0), stop=(s == NT - 1))
                cproduct(m)
            pe.wait_ge(c_out, 12)
            for t in range(NT):
                with pe.Fori(0, TP // 5) as i:
                    for u in range(5):
                        pe.wait_ge(mx_out, i * 5 + max(t * TP + u - 1, 0))
                        sel = identb[0:TP, bass.ds(i * 5 + u, 1)].to_broadcast([TP, 128])
                        b0 = 0 if u in (0, 2) else 2 if u in (1, 3) else 4
                        pe.matmul(ps[:, b0, 0:512], sel, maskb[:, t, 0:512], start=True, stop=True)
                        pe.matmul(ps[:, b0 + 1, 0:N - 512], sel, maskb[:, t, 512:N], start=True,
                                  stop=True).then_inc(mx_mm, 1)
            pe.wait_ge(mx_kept, N // 5)
            for t in range(NT):
                bk, off = (0, t * 128) if t < 4 else (1, 0)
                m = pe.transpose(ps[0:TP, bk, off:off + 128], aggmT[:, t * TP:(t + 1) * TP], ident[:, :])
            cproduct(m)
            pe.wait_ge(c_out, 14)
            for t in range(NT):
                m = pe.matmul(ps[:, 2, 0:D], ones[0:TP, :], ya[:, t, :], start=(t == 0), stop=(t == NT - 1))
            cproduct(m)
            pe.wait_ge(c_out, 16)
            for t in range(NT):
                m = pe.matmul(ps[:, 3, 0:D], ones[0:TP, :], yb[:, t, :], start=(t == 0), stop=(t == NT - 1))
            cproduct(m)
            pe.wait_ge(c_out, 17)

            def lproduct(m):
                m.then_inc(l_mm, 1)

            pe.wait_ge(ld_lw, 48)
            for j in range(KD):
                lproduct(feature_major(lwq, xnT, j, 2 * j))
            for j in range(KD):
                pe.wait_ge(l_out, j + 1)
                lproduct(feature_major(lwk, xnT, j, 2 * j))
            for t in range(NT):
                if t >= 2:
                    pe.wait_ge(l_out, 4 + t - 1)
                for k in range(KD):
                    m = pe.matmul(ps[0:TP, 4 + t % 2, 0:D], xnT[:, k, t * TP:(t + 1) * TP], lwv[:, k, :],
                                  start=(k == 0), stop=(k == KD - 1))
                lproduct(m)
            pe.wait_ge(l_out, 9)
            for t in range(NT):
                for j in range(KD):
                    q = 2 * t + j
                    m = pe.transpose(ps[0:TP, q // 4, (q % 4) * 128:(q % 4 + 1) * 128],
                                     big[:, j, t * TP:(t + 1) * TP], ident[:, :])
            lproduct(m)
            pe.wait_ge(l_out, 10)
            for j in range(KD):
                for t in range(NT):
                    m = pe.matmul(ps[:, j, 0:D], smx[:, t, j * 128:(j + 1) * 128], kphi[:, t, :],
                                  start=(t == 0), stop=(t == NT - 1))
            lproduct(m)
            pe.wait_ge(l_out, 11)
            for t in range(NT):
                if t >= 2:
                    pe.wait_ge(l_out, 11 + t - 1)
                for k in range(KD):
                    m = pe.matmul(ps[0:TP, 4 + t % 2, 0:D], qphi[:, k, t * TP:(t + 1) * TP], lam[:, k, :],
                                  start=(k == 0), stop=(k == KD - 1))
                lproduct(m)
            pe.wait_ge(l_out, 16)
            turn(xn, norm_ready, 6)
            turned()
            experts(E1, H1 // 128, wr1, b2e1, None, xnT, xnT, False)

        @block.scalar
        def _(act):
            def sqrt_of(dst, src, count):
                act.wait_ge(var_ready, count)
                nc.scalar.activation(dst, src, ACT.Sqrt).then_inc(rstd_ready, 1)

            sqrt_of(rstd[:, :], rstd[:, :], 1)
            for t in range(NT):
                for g in range(4):
                    act.wait_ge(h_mm, 4 * t + g + 1)
                    if g == 0 and t >= 2:
                        act.wait_ge(h_stored, 16 * (t - 1))
                    nc.scalar.activation(hrow[:, t % 2, g * 512:(g + 1) * 512], ps[0:TP, g, :],
                                         ACT.Copy).then_inc(h_copied, 1)
            for j in range(KD):
                act.wait_ge(m_pre, j + 1)
                nc.scalar.activation((tmpf, tmpg)[j][:, :], (tmpf, tmpg)[j][:, :], ACT.Exp).then_inc(m_exp, 1)
            for t in range(NT):
                act.wait_ge(m_pre, 3 + t)
                nc.scalar.activation(tmpr[:, (t % 2) * D:(t % 2 + 1) * D], tmpr[:, (t % 2) * D:(t % 2 + 1) * D],
                                     ACT.Exp).then_inc(m_exp, 1)
            sqrt_of(rstd[:, :], rstd[:, :], 2)
            for m_ in range(8):
                act.wait_ge(m_mm, 16 + m_)
                c = VCOL["b1"] + m_
                nc.scalar.activation(big[:, m_, :].rearrange("p (b n) -> p b n", b=2),
                                     ps[:, 2 * (m_ % 2):2 * (m_ % 2) + 2, 0:HN], ACT.Relu,
                                     bias=vecs[:, c:c + 1]).then_inc(m_relu, 1)
            for n in (3, 4, 5):
                sqrt_of(rstd[:, :], rstd[:, :], n)
            moe = dict(h=0, y=0, r=0)

            def experts(ne, nh, func, bias_of):
                moe["r"] += 1
                act.wait_ge(r_pre, moe["r"])
                nc.scalar.activation(gate[:, :, 1:2], gate[:, :, 0:1], ACT.Exp).then_inc(r_exp, 1)
                h0, y0 = moe["h"], moe["y"] + NT
                with act.Fori(0, ne // 2) as i:
                    for u in range(2):
                        for m_ in range(nh):
                            act.wait_ge(moe_h, i * (2 * nh) + (h0 + u * nh + m_ + 1))
                            if m_ == 0:
                                act.wait_ge(moe_acc, i * (2 * NT) + (y0 + u * NT))
                            nc.scalar.activation(big[:, m_, :].rearrange("p (b n) -> p b n", b=2),
                                                 ps[:, 2 * (m_ % 2):2 * (m_ % 2) + 2, 0:HN], func,
                                                 bias=bias_of(i, u, m_)).then_inc(moe_act, 1)
                moe["h"], moe["y"] = h0 + ne * nh, y0 + ne * NT

            experts(E0, 8, ACT.Gelu, lambda i, u, m_: vecs[:, bass.ds(i * 16 + (VCOL["eb1"] + u * 8 + m_), 1)])
            sqrt_of(rstd[:, :], rstd[:, :], 6)
            act.wait_ge(var_ready, 7)
            nc.scalar.activation(dinv[:, :], dinv[:, :], ACT.Sqrt).then_inc(rstd_ready, 1)
            act.wait_ge(var_ready, 8)
            nc.scalar.activation(gmean[:, :], gmean[:, :], ACT.Sqrt).then_inc(rstd_ready, 1)
            for j in range(KD):
                act.wait_ge(l_pre, j + 1)
                nc.scalar.activation(big[:, j, 0:N], big[:, j, 0:N], ACT.Exp, bias=kmax[:, j:j + 1],
                                     accum_out=ksum[:, j:j + 1]).then_inc(l_exp, 1)
            act.wait_ge(var_ready, 9)
            nc.scalar.activation(lrs[:, :], lrs[:, :], ACT.Sqrt).then_inc(rstd_ready, 1)
            sqrt_of(rstd[:, :], rstd[:, :], 10)
            experts(E1, 4, ACT.Relu, lambda i, u, m_: b1cols[:, bass.ds(i * 8 + (u * 4 + m_), 1)])

        @block.vector
        def _(dve):
            v = nc.vector
            step = Chain(dve, dchain)
            done, mark = step.done, step.mark

            def tt(out, p, q, op):
                return v.tensor_tensor(out, p, q, op)

            v.memset(zerob[:, :], 0.0).then_inc(consts_ready, 1)
            for dst in (xnT, xT2, qphi):
                mark(v.memset(dst[:, :, N:NP], 0.0))
            step.wait()
            mark(v.memset(vext[:, :, :, 128:129], 1.0))
            dve.wait_ge(ld_edges, 48)
            dve.wait_ge(consts_ready, 4)
            v.tensor_copy(srcf[:, :], srcs[:, :]).then_inc(edges_ready, 1)
            v.tensor_copy(dstf[:, :], dsts[:, :]).then_inc(edges_ready, 1)
            v.scalar_tensor_tensor(out=rowid[:, :], in0=srcs[:, :], scalar=float(R0), in1=types[:, :],
                                   op0=ALU.mult, op1=ALU.add).then_inc(edges_ready, 1)
            dve.wait_ge(edges_ready, 3)

            for p_, tiles in enumerate(((0, 1, 2), (3, 4))):
                base = p_ * EC
                with dve.Fori(0, EC // 3) as i:
                    for u in range(3):
                        sl = (u + base) % 3
                        if p_ or True:
                            dve.wait_ge(oh_used, i * 3 + max(base + u - 2, 0))
                        v.tensor_scalar(ohs[:, sl, :], iota_f[0:EP, :], srcf[:, bass.ds(i * 3 + u, 1)], None,
                                        ALU.is_equal)
                        v.tensor_scalar(ohd[:, sl, :], iota_f[0:EP, :], dstf[:, bass.ds(i * 3 + u, 1)], None,
                                        ALU.is_equal).then_inc(oh_ready, 1)
                dve.wait_ge(adj_mm, p_ + 1)
                for k, s in enumerate(tiles):
                    mark(v.tensor_copy(adjT[:, s, 0:512], ps[0:TP, 2 * k, 0:512]))
                    done(v.tensor_copy(adjT[:, s, 512:N], ps[0:TP, 2 * k + 1, 0:N - 512]))
                    tt(adjT[:, s, s * TP:(s + 1) * TP], adjT[:, s, s * TP:(s + 1) * TP], ident[0:TP, 0:TP],
                       ALU.add).then_inc(adj_ready, 1)
            for d in range(NT):
                dve.wait_ge(adj_mm, 3 + d)
                mark(v.tensor_scalar(maskb[:, d, 0:4 * TP], ps[0:TP, 0, 0:4 * TP], 0.0, -BIG, ALU.is_equal,
                                     ALU.mult))
                v.tensor_scalar(maskb[:, d, 4 * TP:N], ps[0:TP, 1, 0:TP], 0.0, -BIG, ALU.is_equal,
                                ALU.mult).then_inc(adj_ready, 1)

            ntr = [0]
            ntr[0] += 1
            dve.wait_ge(tr_mm, 1)
            mark(v.tensor_copy(vecs[:, :], ps[:, 0, 0:NVEC]))
            v.tensor_copy(b1cols[:, :], ps[:, 1, 0:256]).then_inc(tr_copied, 1)

            def turn(dst, b0=0):
                ntr[0] += 1
                dve.wait_ge(tr_mm, ntr[0])
                for j in range(KD):
                    mark(v.tensor_copy(dst[:, j, 0:4 * TP], ps[:, b0 + j, 0:4 * TP]))
                v.tensor_copy(dst[:, :, 4 * TP:N], ps[:, b0 + 2, 0:KD * TP].rearrange("p (c n) -> p c n", c=KD)
                              ).then_inc(tr_copied, 1)

            nsq = [0]

            def root(out, var, eps):
                done(v.tensor_scalar(out, var, eps, None, ALU.add))
                v.reciprocal(out, out).then_inc(var_ready, 1)
                nsq[0] += 1
                dve.wait_ge(rstd_ready, nsq[0])

            nnorm = [0]

            def layernorm(dst, src, last=True):
                for t in range(NT):
                    mark(v.bn_stats(stats[:, t, :], src[:, t, :]))
                step.wait()
                for t in range(NT):
                    mark(v.bn_aggr(mv[:, t, :], stats[:, t, :]))
                step.wait()
                root(rstd[:, :], mv[:, :, 1:2].rearrange("p t o -> p (t o)"), EPS)
                for t in range(NT):
                    m = v.tensor_scalar(dst[:, t, :], src[:, t, :], mv[:, t, 0:1], rstd[:, t:t + 1],
                                        ALU.subtract, ALU.mult)
                    if t < NT - 1 or not last:
                        mark(m)
                if last:
                    m.then_inc(norm_ready, 1)
                    nnorm[0] += 1
                    dve.wait_ge(norm_ready, nnorm[0])
                else:
                    step.wait()

            def affine(dst, g, b, t):
                done(tt(dst[:, t, :], dst[:, t, :], row(g), ALU.mult))
                return tt(dst[:, t, :], dst[:, t, :], row(b), ALU.add)

            dve.wait_ge(ld_x, 16)
            layernorm(xn, x)
            dve.wait_ge(ld_w, 16 * n_w)
            for r in range(R0):
                for b in range(NB0):
                    c = comp[:, r * NB0 + b:r * NB0 + b + 1]
                    if b == 0:
                        m = v.tensor_scalar(wrel[:, :, r, :], basis[:, b, :, :], c, None, ALU.mult)
                    else:
                        m = v.scalar_tensor_tensor(out=wrel[:, :, r, :], in0=basis[:, b, :, :], scalar=c,
                                                   in1=wrel[:, :, r, :], op0=ALU.mult, op1=ALU.add)
                    if r == R0 - 1 and b == NB0 - 1:
                        m.then_inc(wrel_ready, 1)
                    else:
                        done(m)
            turn(xnT)

            dve.wait_ge(h_copied, 4 * NT)
            for j in range(KD):
                dve.wait_ge(m_mm, j + 1)
                src = ps[:, 2 * j:2 * j + 2, 0:HN]
                bq = vecs[:, VCOL["bq"] + j:VCOL["bq"] + j + 1]
                tf = (tmpf, tmpg)[j][:, :].rearrange("p (b n) -> p b n", b=2)
                v.tensor_scalar(tf, src, bq, 0.0, ALU.add, ALU.min).then_inc(m_pre, 1)
                mark(v.tensor_scalar(qphi[:, j, :].rearrange("p (b n) -> p b n", b=2), src, bq, 0.0, ALU.add,
                                     ALU.max))
                step.wait()
                dve.wait_ge(m_exp, j + 1)
                tt(qphi[:, j, :], qphi[:, j, :], (tmpf, tmpg)[j][:, :], ALU.add).then_inc(m_out, 1)
            for t in range(NT):
                dve.wait_ge(m_mm, 3 + t)
                bank = 4 * (1 - t % 2)
                done(tt(kphi[:, t, :], ps[0:TP, bank, 0:D], row("bk"), ALU.add))
                e_ = tmpr[:, (t % 2) * D:(t % 2 + 1) * D]
                v.tensor_scalar(e_, kphi[:, t, :], 0.0, None, ALU.min).then_inc(m_pre, 1)
                mark(tt(vext[:, t, :, 0:128], ps[0:TP, bank, D:2 * D].rearrange("p (c n) -> p c n", c=KD),
                        row("bv").rearrange("p (c n) -> p c n", c=KD), ALU.add))
                dve.wait_ge(m_exp, 3 + t)
                v.scalar_tensor_tensor(out=kphi[:, t, :], in0=kphi[:, t, :], scalar=0.0, in1=e_, op0=ALU.max,
                                       op1=ALU.add).then_inc(m_out, 1)
            dve.wait_ge(m_mm, 8)
            for j in range(KD):
                mark(tt(kvbd[:, j, :], ps[:, j, 0:128], headmask[:, :], ALU.mult))
                mark(v.tensor_copy(scr[:, j:j + 1], ps[:, j, 128:129]))
                step.wait()
                m = v.tensor_scalar(ksbd[:, j, :], headmask[:, :], scr[:, j:j + 1], None, ALU.mult)
                if j == KD - 1:
                    m.then_inc(m_out, 1)
                else:
                    mark(m)
            for j in range(KD):
                dve.wait_ge(m_mm, 9 + j)
                t3 = tmpf[:, :].rearrange("p (b n) -> p b n", b=2)
                done(v.tensor_scalar(t3, ps[:, 2:4, 0:HN], 1e-6, None, ALU.add))
                done(v.reciprocal(tmpf[:, :], tmpf[:, :]))
                tt(xT2[:, j, :].rearrange("p (b n) -> p b n", b=2), ps[:, 0:2, 0:HN], t3,
                   ALU.mult).then_inc(m_out, 1)
                dve.wait_ge(m_out, 9 + j)
            for t in range(NT):
                dve.wait_ge(m_mm, 11 + t)
                done(tt(ya[:, t, :], ps[0:TP, t % 2, 0:D], row("bo"), ALU.add))
                tt(ya[:, t, :], ya[:, t, :], xn[:, t, :], ALU.add).then_inc(m_out, 1)
            dve.wait_ge(m_out, 15)
            layernorm(ya, ya, last=False)
            for t in range(NT):
                m = affine(ya, "ln1_g", "ln1_b", t)
                if t < NT - 1:
                    mark(m)
                else:
                    m.then_inc(norm_ready, 1)
            nnorm[0] += 1
            dve.wait_ge(norm_ready, nnorm[0])
            turn(xT2)
            for t in range(NT):
                dve.wait_ge(m_mm, 24 + t)
                done(tt(yb[:, t, :], ps[0:TP, t % 2, 0:D], row("b2"), ALU.add))
                tt(yb[:, t, :], yb[:, t, :], ya[:, t, :], ALU.add).then_inc(m_out, 1)
            dve.wait_ge(m_out, 20)
            layernorm(yb, yb, last=False)
            for t in range(NT):
                done(affine(yb, "ln2_g", "ln2_b", t))

            with dve.Fori(0, EC // GRING) as i:
                for u in range(GRING):
                    if u >= 3:
                        dve.wait_ge(g_used, i * GRING + (u - 2))
                    elif u == 0:
                        dve.wait_ge(g_used, i * GRING)
                    v.tensor_scalar(ohf[:, u % 3, :], iota_f[0:EP, :], dstf[:, bass.ds(i * GRING + u, 1)], None,
                                    ALU.is_equal).then_inc(g_oh, 1)
            dve.wait_ge(g_done, 1)
            for t in range(NT):
                acc = ps[0:TP, 5 + t // 2, (t % 2) * D:(t % 2 + 1) * D]
                done(tt(ya[:, t, :], acc, row("gbias"), ALU.add))
                done(tt(ya[:, t, :], ya[:, t, :], yb[:, t, :], ALU.add))
                done(tt(x[:, t, :], x[:, t, :], ya[:, t, :], ALU.add))

            moe = dict(y=0, r=0, x=0, g=0)

            def experts(ne, rb, per_expert_x):
                r0 = moe["r"]
                dve.wait_ge(r_mm, r0 + 1)
                step.done(tt(lg[:, :, 0:ne], ps[0:TP, 6, 0:NT * ne].rearrange("p (t e) -> p t e", t=NT),
                             rb[0:TP, :].unsqueeze(1).to_broadcast([TP, NT, ne]), ALU.add))
                for k in range(2):
                    cur = (lg, lg2)[k]
                    for t in range(NT):
                        mark(v.max(m8[:, t, :], cur[:, t, 0:ne]))
                    step.wait()
                    for t in range(NT):
                        mark(v.max_index(i8[:, t, :], m8[:, t, :], cur[:, t, 0:ne]))
                    step.wait()
                    done(v.tensor_copy(i8f[:, :, k:k + 1], i8[:, :, 0:1]))
                    mark(v.tensor_copy(gate[:, :, 2 * k:2 * k + 1], m8[:, :, 0:1]))
                    for t in range(NT):
                        mark(v.tensor_scalar((comb, lg2)[k][:, t, 0:ne], iota_f[0:TP, 0:ne],
                                             i8f[:, t, k:k + 1], None, ALU.is_equal))
                    step.wait()
                    if k == 0:
                        done(v.scalar_tensor_tensor(out=lg2[:, :, 0:ne], in0=comb[:, :, 0:ne], scalar=-3e38,
                                                    in1=lg[:, :, 0:ne], op0=ALU.mult, op1=ALU.add))
                tt(gate[:, :, 0:1], gate[:, :, 2:3], gate[:, :, 0:1], ALU.subtract).then_inc(r_pre, 1)
                moe["g"] += 1
                dve.wait_ge(r_exp, moe["g"])
                done(v.tensor_scalar(gate[:, :, 2:3], gate[:, :, 1:2], 1.0, None, ALU.add))
                done(v.reciprocal(gate[:, :, 2:3], gate[:, :, 2:3]))
                done(tt(gate[:, :, 3:4], gate[:, :, 1:2], gate[:, :, 2:3], ALU.mult))
                done(tt(comb[:, :, 0:ne], comb[:, :, 0:ne], gate[:, :, 2:3].to_broadcast([TP, NT, ne]), ALU.mult))
                done(tt(lg2[:, :, 0:ne], lg2[:, :, 0:ne], gate[:, :, 3:4].to_broadcast([TP, NT, ne]), ALU.mult))
                tt(comb[:, :, 0:ne], comb[:, :, 0:ne], lg2[:, :, 0:ne], ALU.add).then_inc(r_out, 1)
                dve.wait_ge(r_out, r0 + 1)
                dve.wait_ge(r_mm, r0 + 2)
                mark(v.tensor_copy(combT[0:ne, 0:4 * TP], ps[0:ne, 6, 0:4 * TP]))
                v.tensor_copy(combT[0:ne, 4 * TP:N], ps[0:ne, 7, 0:TP]).then_inc(r_out, 1)
                moe["r"] = r0 + 2
                y0 = moe["y"]
                for t in range(NT):
                    dve.wait_ge(moe_y, y0 + t + 1)
                    tt(x[:, t, :], x[:, t, :], ps[0:TP, 4 + t % 2, 0:D], ALU.add).then_inc(moe_acc, 1)
                y0 += NT
                dve.wait_ge(moe_acc, y0)

                def scaled(i, u):
                    for j in range(KD):
                        c = i * 4 + (VCOL["eg"] + 2 * u + j), i * 4 + (VCOL["eb"] + 2 * u + j)
                        m = v.tensor_scalar(qphi[:, j, :], xnT[:, j, :], vecs[:, bass.ds(c[0], 1)],
                                            vecs[:, bass.ds(c[1], 1)], ALU.mult, ALU.add)
                    m.then_inc(moe_x, 1)

                with dve.Fori(0, ne // 2) as i:
                    step.enter(i, 0)
                    for u in range(2):
                        if per_expert_x:
                            dve.wait_ge(moe_acc, i * (2 * NT) + (y0 + u * NT))
                            scaled(i, u)
                        for t in range(NT):
                            dve.wait_ge(moe_y, i * (2 * NT) + (y0 + u * NT + t + 1))
                            dve.wait_ge(moe_acc, i * (2 * NT) + (y0 + u * NT + t - (NT - 1)))
                            v.scalar_tensor_tensor(out=x[:, t, :], in0=ps[0:TP, 4 + (u * NT + t) % 2, 0:D],
                                                   scalar=comb[:, t, bass.ds(i * 2 + u, 1)], in1=x[:, t, :],
                                                   op0=ALU.mult, op1=ALU.add).then_inc(moe_acc, 1)
                    step.leave(ne // 2)
                moe["y"] = y0 + ne * NT
                dve.wait_ge(moe_acc, moe["y"])

            layernorm(ya, x)
            turn(xT2)
            layernorm(xn, ya)
            turn(xnT)
            experts(E0, rb0, True)

            layernorm(xn, x)
            turn(xnT)
            for t in range(NT):
                dve.wait_ge(c_mm, t + 1)
                mark(v.tensor_copy(bas[:, t, 0:DB], ps[0:TP, t % 2, 0:DB]))
                tt(wgt[:, t, :], ps[0:TP, t % 2, DB:DB + NH * NK], bcomb[0:TP, :], ALU.add).then_inc(c_out, 1)
            dve.wait_ge(c_mm, 6)
            mark(v.tensor_copy(basT[:, 0:HN], ps[:, 2, 0:HN]))
            v.tensor_copy(basT[:, HN:N], ps[:, 3, 0:N - HN]).then_inc(c_out, 1)
            dve.wait_ge(c_mm, 7)
            done(v.tensor_copy(deg[:, :], ps[0:TP, 4, 0:NT]))
            v.reciprocal(dinv[:, :], deg[:, :]).then_inc(var_ready, 1)
            nsq[0] += 1
            dve.wait_ge(rstd_ready, nsq[0])
            for t in range(NT):
                m = v.tensor_scalar(bas[:, t, DB:2 * DB], bas[:, t, 0:DB], dinv[:, t:t + 1], None, ALU.mult)
                if t < NT - 1:
                    mark(m)
            m.then_inc(c_out, 1)
            for t in range(NT):
                dve.wait_ge(c_mm, 8 + t)
                mark(v.tensor_scalar(agg[:, t, 0:DB], ps[0:TP, t % 2, DB:2 * DB], dinv[:, t:t + 1], None,
                                     ALU.mult))
                v.tensor_copy(agg[:, t, DB:2 * DB], ps[0:TP, t % 2, 0:DB]).then_inc(c_out, 1)
            dve.wait_ge(c_out, 12)
            for t in range(NT):
                with dve.Fori(0, TP // 5) as i:
                    for u in range(5):
                        n = t * TP + u
                        dve.wait_ge(mx_mm, i * 5 + (n + 1))
                        dve.wait_ge(mx_out, i * 5 + n)
                        v.memset(held[:, :], 0.0)
                        b0 = 0 if u in (0, 2) else 2 if u in (1, 3) else 4
                        src = ps[:, b0:b0 + 2, :].rearrange("p b n -> p (b n)")[:, 0:N]
                        v.tensor_tensor_reduce(out=scr[:, 0:N], in0=src, in1=basT[:, :], scale=1.0,
                                               scalar=-3e38, op0=ALU.add, op1=ALU.max,
                                               accum_out=max5[:, u:u + 1]).then_inc(mx_out, 1)
                    dve.wait_ge(mx_out, i * 5 + (t * TP + 5))
                    v.tensor_copy(aggmT[:, bass.ds(i * 5 + t * TP, 5)], max5[:, :]).then_inc(mx_kept, 1)
                    dve.wait_ge(mx_kept, i + (t * TP // 5 + 1))
            dve.wait_ge(c_mm, 13)
            mark(v.tensor_copy(agg[:, 0:4, 2 * DB:3 * DB], ps[0:TP, 0, :].rearrange("p (t d) -> p t d", t=4)))
            done(v.tensor_copy(agg[:, 4, 2 * DB:3 * DB], ps[0:TP, 1, 0:DB]))
            v.nop()
            mark(v.memset(scr[:, 0:1], 0.0))
            ya4 = ya[:, :, :].rearrange("p t (h f) -> p t h f", h=NH)
            pr = prod[:, :].rearrange("p (h f) -> p h f", h=NH)
            for t in range(NT):
                for k in range(NK):
                    w = wgt[:, t, :].rearrange("p (h k) -> p h k", h=NH)[:, :, k:k + 1].to_broadcast(
                        [TP, NH, FH])
                    g = agg[:, t, k * FH:(k + 1) * FH].unsqueeze(1).to_broadcast([TP, NH, FH])
                    if k == 0:
                        done(tt(ya4[:, t], w, g, ALU.mult))
                        done(tt(ya[:, t, :], ya[:, t, :], row("cbias"), ALU.add))
                    else:
                        done(tt(pr, w, g, ALU.mult))
                        m = tt(ya[:, t, :], ya[:, t, :], prod[:, :], ALU.add)
                        if t == NT - 1 and k == NK - 1:
                            m.then_inc(c_out, 2)
                            dve.wait_ge(c_out, 14)
                        else:
                            done(m)
            dve.wait_ge(c_mm, 14)
            done(v.scalar_tensor_tensor(out=gmean[:, :], in0=ps[:, 2, 0:D], scalar=1.0 / N,
                                        in1=row("gnms", 128), op0=ALU.mult, op1=ALU.mult))
            for t in range(NT):
                mark(tt(ya[:, t, :], ya[:, t, :], gmean[0:TP, :], ALU.subtract))
            step.wait()
            for t in range(NT):
                m = tt(yb[:, t, :], ya[:, t, :], ya[:, t, :], ALU.mult)
                if t < NT - 1:
                    mark(m)
            m.then_inc(c_out, 2)
            dve.wait_ge(c_mm, 15)
            done(v.tensor_scalar(gmean[:, :], ps[:, 3, 0:D], 1.0 / N, EPS, ALU.mult, ALU.add))
            v.reciprocal(gmean[:, :], gmean[:, :]).then_inc(var_ready, 1)
            nsq[0] += 1
            dve.wait_ge(rstd_ready, nsq[0])
            done(tt(gmean[:, :], gmean[:, :], row("gnw", 128), ALU.mult))
            for t in range(NT):
                done(tt(ya[:, t, :], ya[:, t, :], gmean[0:TP, :], ALU.mult))
                done(tt(ya[:, t, :], ya[:, t, :], row("gnb"), ALU.add))
                m = v.scalar_tensor_tensor(out=x[:, t, :], in0=ya[:, t, :], scalar=0.0, in1=x[:, t, :],
                                           op0=ALU.max, op1=ALU.add)
                if t < NT - 1:
                    done(m)
            m.then_inc(c_out, 1)
            dve.wait_ge(c_out, 17)

            for j in range(KD):
                dve.wait_ge(l_mm, j + 1)
                c = VCOL["bqk"] + j
                v.tensor_scalar(qphi[:, j, :].rearrange("p (b n) -> p b n", b=2), ps[:, 2 * j:2 * j + 2, 0:HN],
                                vecs[:, c:c + 1], None, ALU.add).then_inc(l_out, 1)
            for j in range(KD):
                dve.wait_ge(l_mm, 3 + j)
                c = VCOL["bqk"] + 2 + j
                done(v.tensor_scalar(big[:, j, :].rearrange("p (b n) -> p b n", b=2),
                                     ps[:, 2 * j:2 * j + 2, 0:HN], vecs[:, c:c + 1], None, ALU.add))
                v.tensor_reduce(kmax[:, j:j + 1], big[:, j, 0:N], AX.X, ALU.max, negate=True
                                ).then_inc(l_pre, 1)
                dve.wait_ge(l_exp, j + 1)
                v.reciprocal(ksum[:, j:j + 1], ksum[:, j:j + 1]).then_inc(l_out, 1)
            for t in range(NT):
                dve.wait_ge(l_mm, 5 + t)
                tt(kphi[:, t, :], ps[0:TP, 4 + t % 2, 0:D], row("lbv"), ALU.add).then_inc(l_out, 1)
            dve.wait_ge(l_mm, 10)
            mark(v.tensor_copy(smx[:, 0:4, :], ps[0:TP, 0:2, :].rearrange("p b (t d) -> p (b t) d", t=2)))
            v.tensor_copy(smx[:, 4, :], ps[0:TP, 2, 0:D]).then_inc(l_out, 1)
            dve.wait_ge(l_mm, 11)
            for j in range(KD):
                mark(v.tensor_scalar(lam[:, j, :], ps[:, j, 0:D], ksum[:, j:j + 1], None, ALU.mult))
            step.wait()
            for j in range(KD):
                mark(v.bn_stats(lst[:, j, :], lam[:, j, :]))
            step.wait()
            for j in range(KD):
                mark(v.bn_aggr(lmv[:, j, :], lst[:, j, :]))
            step.wait()
            root(lrs[:, :], lmv[:, :, 1:2].rearrange("p t o -> p (t o)"), EPS)
            done(tt(lrs[:, :], lrs[:, :], vecs[:, VCOL["gamma"]:VCOL["gamma"] + KD], ALU.mult))
            for j in range(KD):
                done(v.tensor_scalar(lam[:, j, :], lam[:, j, :], lmv[:, j, 0:1], lrs[:, j:j + 1], ALU.subtract,
                                     ALU.mult))
                m = v.tensor_scalar(lam[:, j, :], lam[:, j, :], vecs[:, VCOL["beta"] + j:VCOL["beta"] + j + 1],
                                    None, ALU.add)
                if j < KD - 1:
                    mark(m)
            m.then_inc(l_out, 1)
            for t in range(NT):
                dve.wait_ge(l_mm, 12 + t)
                tt(x[:, t, :], x[:, t, :], ps[0:TP, 4 + t % 2, 0:D], ALU.add).then_inc(l_out, 1)
            dve.wait_ge(l_out, 16)
            layernorm(xn, x)
            turn(xnT)
            experts(E1, rb1, False)
            v.memset(scr[:, 0:1], 0.0).then_inc(o_ready, NT)


_INS = ["x", "src", "dst", "edge_type_8", "L0_gnn_basis", "L0_gnn_comp", "L0_gnn_loop_weight",
        "L0_gnn_bias_param", "L0_mix_Wq", "L0_mix_bq", "L0_mix_Wk", "L0_mix_bk", "L0_mix_Wv", "L0_mix_bv",
        "L0_mix_Wo", "L0_mix_bo", "L0_mix_W1", "L0_mix_b1", "L0_mix_W2", "L0_mix_b2", "L0_mix_ln1_g",
        "L0_mix_ln1_b", "L0_mix_ln2_g", "L0_mix_ln2_b", "L0_ffn_Wr", "L0_ffn_br", "L0_ffn_ln_g", "L0_ffn_ln_b",
        "L0_ffn_W1", "L0_ffn_b1", "L0_ffn_W2", "L0_ffn_b2", "L1_gnn_W_bases", "L1_gnn_W_comb",
        "L1_gnn_b_comb", "L1_gnn_conv_bias", "L1_gnn_gn_weight", "L1_gnn_gn_bias", "L1_gnn_gn_mean_scale",
        "L1_mix_W_qk", "L1_mix_b_qk", "L1_mix_W_v", "L1_mix_b_v", "L1_mix_gamma", "L1_mix_beta", "L1_ffn_Wr",
        "L1_ffn_br", "L1_ffn_W1", "L1_ffn_b1", "L1_ffn_W2", "L1_ffn_b2"]


def kernel(**inputs):
    import numpy as _np
    import concourse.bacc as _bacc
    from concourse import mybir as _mybir
    from concourse.bass_utils import run_bass_kernel_spmd as _run

    nc = _bacc.Bacc("TRN2", target_bir_lowering=False, num_devices=1)
    arrays, args = {}, {}
    for name in _INS:
        v = _np.ascontiguousarray(inputs[name])
        arrays[f"in_{name}_dram"] = v
        args[name] = nc.dram_tensor(f"in_{name}_dram", v.shape, _mybir.dt.from_np(v.dtype),
                                    kind="ExternalInput").ap()
    args["out"] = nc.dram_tensor("out_0_dram", (N, D), _mybir.dt.float32, kind="ExternalOutput").ap()
    gps_kernel(nc, args)
    r = _run(nc, [arrays], core_ids=[0])
    return r.results[0]["out_0_dram"]
```

```python
from contextlib import ExitStack

import concourse.bass as bass
from concourse import mybir

F32 = mybir.dt.float32
BF16 = mybir.dt.bfloat16
I32 = mybir.dt.int32
U32 = mybir.dt.uint32
ALU = mybir.AluOpType
ACT = mybir.ActivationFunctionType
AX = mybir.AxisListType

N = 625
TP = 125
NT = N // TP
D = 256
KD = D // 128
NP = N + 1
HN = NP // 2
E = 20625
EP = 125
EC = E // EP
R0 = 8
NB0 = 4
DFF = 1024
E0, H0 = 8, 1024
E1, H1 = 64, 512
DB = 128
NH, NK, FH = 8, 12, 32
CAP = 64
SPARE = E1 * CAP
GRING = 15
WIN = 128
SEAM = 384
GAP = 512 - SEAM
ROWCH = (128, EC - 128)
BIG = 2.0 ** 120
EPS = 1e-5

VECS = [("bq", 2), ("b1", 8), ("bqk", 4), ("gamma", 2), ("beta", 2), ("eg", 16), ("eb", 16), ("eb1", 64)]
VCOL, _n = {}, 0
for _name, _k in VECS:
    VCOL[_name] = _n
    _n += _k
NVEC = _n
ROWS = ["bk", "bv", "bo", "b2", "ln1_g", "ln1_b", "ln2_g", "ln2_b", "gbias", "cbias", "gnw", "gnb", "gnms", "lbv"]


class Chain:

    def __init__(self, eng, sem):
        self.eng, self.sem, self.n, self.off = eng, sem, 0, None

    def mark(self, ins):
        self.n += 1
        ins.then_inc(self.sem, 1)

    def wait(self):
        self.eng.wait_ge(self.sem, self.n if self.off is None else self.off + self.n)

    def done(self, ins):
        self.mark(ins)
        self.wait()

    def enter(self, i, k):
        self.off, self.k, self.n0 = i * k, k, self.n

    def leave(self, count):
        assert self.n - self.n0 == self.k, (self.n - self.n0, self.k)
        self.n, self.off = self.n0 + self.k * count, None


def gps_kernel(nc, a):
    with ExitStack() as ctx:
        def sb(name, shape, dt=F32):
            return ctx.enter_context(nc.sbuf_tensor(name, shape, dt))

        def sem(name):
            return ctx.enter_context(nc.semaphore(name))

        ps = ctx.enter_context(nc.psum_tensor("ps", [128, 8, 512], F32))
        iota_f = sb("iota_f", [128, N])
        ident = sb("ident", [128, 128])
        identb = sb("identb", [128, 128], BF16)
        headmask = sb("headmask", [128, 128])
        ones = sb("ones", [128, 128])
        zerob = sb("zerob", [128, 512], BF16)
        srcf = sb("srcf", [EP, EC])
        dstf = sb("dstf", [EP, EC])
        dstw = sb("dstw", [EP, EC])
        rowid = sb("rowid", [EP, EC], I32)
        wincol = sb("wincol", [1, EC], I32)
        wide = sb("wide", [1, 1], I32)
        srcs = sb("srcs", [EP, EC], I32)
        apart = sb("apart", [EP, EC])
        unsorted = sb("unsorted", [EP, 1])
        loose = sb("loose", [1, 1], I32)
        cnt = sb("cnt", [TP, NT])
        first = sb("first", [TP, NT])
        ends = sb("ends", [TP, 2, NT], U32)
        miss = sb("miss", [TP, 2, NT])
        nt2 = sb("nt2", [TP, NT])
        vecrows = sb("vecrows", [128, 128])
        vecs = sb("vecs", [128, NVEC])
        rows = sb("rows", [128, len(ROWS), D])
        comp = sb("comp", [128, R0 * NB0])
        rb0 = sb("rb0", [128, E0])
        rb1 = sb("rb1", [128, E1])
        bcomb = sb("bcomb", [128, NH * NK])
        b1rows = sb("b1rows", [128, 2, 128])
        b1cols = sb("b1cols", [128, E1 * 4])
        b2e0 = sb("b2e0", [E0, D])
        b2e1 = sb("b2e1", [E1, D])
        shared = sb("shared", [128, 8192])
        basis = shared[:, 0:NB0 * KD * D].rearrange("p (b c d) -> p b c d", b=NB0, c=KD)
        wrel = shared[:, NB0 * KD * D:(NB0 + R0) * KD * D].rearrange("p (c r d) -> p c r d", c=KD, r=R0)
        wa = shared[:, 0:4096].rearrange("p (s n) -> p s n", s=2)
        wb = shared[:, 4096:8192].rearrange("p (s n) -> p s n", s=2)
        loopw = sb("loopw", [128, KD, D])
        wq = sb("wq", [128, KD, D])
        wkv = sb("wkv", [128, KD, 2 * D])
        wo = sb("wo", [128, KD, D])
        w1 = sb("w1", [128, KD, DFF])
        w2 = sb("w2", [128, DFF // 128, D])
        wr0 = sb("wr0", [128, KD, E0])
        wr1 = sb("wr1", [128, KD, E1])
        wbc = sb("wbc", [128, KD, DB + NH * NK])
        lwq, lwk, lwv = wq, wkv[:, :, 0:D], wkv[:, :, D:2 * D]
        x = sb("x", [TP, NT, D])
        xn = sb("xn", [TP, NT, D])
        xnT = sb("xnT", [128, KD, NP])
        xT2 = sb("xT2", [128, KD, NP])
        ya = sb("ya", [TP, NT, D])
        yb = sb("yb", [TP, NT, D])
        stats = sb("stats", [TP, NT, 6])
        mv = sb("mv", [TP, NT, 2])
        rstd = sb("rstd", [TP, NT])
        adjT = sb("adjT", [TP, NT, N])
        ohf = sb("ohf", [EP, 3, N])
        stage = sb("stage", [TP, 2 * R0 * D])
        hrow = stage[:, :].rearrange("p (s n) -> p s n", s=2)
        maskb = stage[:, :].bitcast(BF16)[:, 0:NT * N].rearrange("p (t n) -> p t n", t=NT)
        gath = stage[:, 0:GRING * D].rearrange("p (s d) -> p s d", s=GRING)
        big = sb("big", [128, 8, NP])
        qphi = sb("qphi", [128, KD, NP])
        kphi = sb("kphi", [TP, NT, D])
        vext = big[0:TP, :, :].rearrange("p a b -> p (a b)")[:, 0:NT * KD * 129].rearrange(
            "p (t c n) -> p t c n", t=NT, c=KD)
        kvbd = sb("kvbd", [128, KD, 128])
        ksbd = sb("ksbd", [128, KD, 128])
        tmpf = sb("tmpf", [128, NP])
        scr = sb("scr", [128, NP])
        tmpg = scr
        tmpr = scr[0:TP, 0:2 * D]
        lg = sb("lg", [TP, NT, E1])
        lg2 = sb("lg2", [TP, NT, E1])
        m8 = sb("m8", [TP, NT, 8])
        i8 = sb("i8", [TP, NT, 8], U32)
        i8f = sb("i8f", [TP, NT, 8])
        gate = sb("gate", [TP, NT, 4])
        comb = sb("comb", [TP, NT, E1])
        combT = sb("combT", [128, N])
        bas = yb
        basT = combT
        wgt = sb("wgt", [TP, NT, NH * NK])
        agg = big[0:TP, :, :].rearrange("p a b -> p (a b)")[:, 0:NT * 3 * DB].rearrange("p (t n) -> p t n", t=NT)
        aggmT = xT2[:, 0, 0:N]
        deg = sb("deg", [TP, NT])
        dinv = sb("dinv", [TP, NT])
        prod = scr[0:TP, 0:D]
        max5 = sb("max5", [128, 5])
        held = sb("held", [128, 1])
        gmean = tmpf[:, 0:D]
        kmax = sb("kmax", [128, KD])
        ksum = sb("ksum", [128, KD])
        lam = tmpf[:, 0:KD * D].rearrange("p (c d) -> p c d", c=KD)
        sel = adjT[:, :, :].rearrange("p t n -> p (t n)")[:, 0:2 * NT * E1].rearrange(
            "p (k t e) -> p k t e", k=2, t=NT)
        tri = sb("tri", [TP, TP])
        nodeid = sb("nodeid", [TP, NT])
        slotf = sb("slotf", [TP, NT, 2])
        fits = sb("fits", [TP, NT, 2])
        put = sb("put", [TP, 2, NT], U32)
        get = sb("get", [TP, 2, NT], U32)
        rowf = sb("rowf", [TP, NT, 2])
        over = sb("over", [TP, 1])
        overi = sb("overi", [TP, 1], I32)
        flat = big[:, :, :].rearrange("p a b -> p (a b)")
        raw = flat[:, 2048:2048 + 6 * EP].bitcast(I32).rearrange("p (w h e) -> p w h e", w=3, h=2)
        crow = flat[:, 2048 + 6 * EP:2048 + 14 * EP].rearrange("p (w h e) -> p w h e", w=4, h=2)
        dpm = flat[0:EP, 3800:3800 + EC].bitcast(I32)
        dnx = flat[0:EP, 3800 + EC:3800 + 2 * EC].bitcast(I32)
        dcmp = flat[0:EP, 3800 + 2 * EC:3800 + 3 * EC]
        span = flat[:, 4400:4408].rearrange("p (h k) -> p h k", h=2)
        bound = flat[0:TP, 0:TP]
        below = flat[0:TP, TP:TP + NT * TP].rearrange("p (t q) -> p t q", t=NT)
        ohs = kphi[:, :, :].rearrange("p t d -> p (t d)").bitcast(BF16)[:, 0:3 * N].rearrange(
            "p (s n) -> p s n", s=3)
        ohd = qphi[0:EP, :, :].rearrange("p c n -> p (c n)").bitcast(BF16)[:, 0:3 * N].rearrange(
            "p (s n) -> p s n", s=3)
        psf = ps[:, :, :].rearrange("p b n -> p (b n)")
        run = stage[:, 0:2 * GRING * DB].rearrange("p (s d) -> p s d", d=DB)
        zerof = flat[:, 0:SPARE // 512 * D]
        xe = flat[0:CAP, 0:1024].rearrange("p (s d) -> p s d", s=4)
        ye = flat[0:CAP, 1024:2048].rearrange("p (s d) -> p s d", s=4)
        hs = flat[0:CAP, 2048:3072].rearrange("p (s d) -> p s d", s=2)
        hact = flat[:, 3072:3072 + 8 * CAP].rearrange("p (s c n) -> p s c n", s=2, c=4)
        xeT = flat[:, 3584:3584 + 4 * CAP].rearrange("p (s c n) -> p s c n", s=2, c=2)
        ew1 = shared[:, 0:4096].rearrange("p (s c h) -> p s c h", s=4, c=KD)
        ew2 = shared[:, 4096:8192].rearrange("p (s c d) -> p s c d", s=4, c=4)
        lst = sb("lst", [128, KD, 6])
        lmv = sb("lmv", [128, KD, 2])
        lrs = sb("lrs", [128, KD])
        smx = bas

        rtab = nc.dram_tensor("rtab", [E, DB], F32, kind="Internal")
        btab = nc.dram_tensor("btab", [N, DB], F32, kind="Internal")
        xs = nc.dram_tensor("xs", [SPARE + 2 * N, D], F32, kind="Internal")
        ys = nc.dram_tensor("ys", [SPARE, D], F32, kind="Internal")
        msgs = nc.dram_tensor("msgs", [N * R0, D], F32, kind="Internal")

        ld_edges = sem("ld_edges")
        ld_x = sem("ld_x")
        ld_vec = sem("ld_vec")
        ld_w, ld_lw = sem("ld_w"), sem("ld_lw")
        consts_ready = sem("consts_ready")
        dchain, achain, pchain = sem("dve_step"), sem("act_step"), sem("pool_step")
        edges_ready, ed_mm, ed_out = sem("edges_ready"), sem("ed_mm"), sem("ed_out")
        e_oh, e_used, sums_out = sem("e_oh"), sem("e_used"), sem("sums_out")
        p_mm, p_out = sem("p_mm"), sem("p_out")
        run_loaded = [sem("run_loaded0"), sem("run_loaded1")]
        run_stored = [sem("run_stored0"), sem("run_stored1")]
        run_head, run_done, ends_got = sem("run_head"), sem("run_done"), sem("ends_got")
        btab_stored, mask_mm, mask_out, mx_turned = (sem("btab_stored"), sem("mask_mm"), sem("mask_out"),
                                                     sem("mx_turned"))
        adj_mm, adj_ready = sem("adj_mm"), sem("adj_ready")
        var_ready, rstd_ready = sem("var_ready"), sem("rstd_ready")
        norm_ready = sem("norm_ready")
        tr_mm, tr_copied = sem("tr_mm"), sem("tr_copied")
        wrel_ready = sem("wrel_ready")
        h_mm, h_copied, h_stored = sem("h_mm"), sem("h_copied"), sem("h_stored")
        gathered = [sem(f"gathered{i}") for i in range(GRING)]
        m_mm, m_out, m_pre, m_exp = sem("m_mm"), sem("m_out"), sem("m_pre"), sem("m_exp")
        m_relu = sem("m_relu")
        moe_w = [sem("moe_w0"), sem("moe_w1")]
        moe_used = sem("moe_used")
        moe_x, moe_h, moe_act, moe_y, moe_acc = (sem("moe_x"), sem("moe_h"), sem("moe_act"), sem("moe_y"),
                                                 sem("moe_acc"))
        run_step, mx_agg = sem("run_step"), sem("mx_agg")
        r_mm, r_out, r_pre, r_exp = sem("r_mm"), sem("r_out"), sem("r_pre"), sem("r_exp")
        c_mm, c_out = sem("c_mm"), sem("c_out")
        mx_mm, mx_out, mx_kept = sem("mx_mm"), sem("mx_out"), sem("mx_kept")
        l_mm, l_out, l_pre, l_exp = sem("l_mm"), sem("l_out"), sem("l_pre"), sem("l_exp")
        xs_zero, put_ready, xs_put = sem("xs_zero"), sem("put_ready"), sem("xs_put")
        xe_loaded = [sem(f"xe_loaded{i}") for i in range(4)]
        ew_loaded = [sem(f"ew_loaded{i}") for i in range(4)]
        y_stored = [sem(f"y_stored{i}") for i in range(4)]
        s_xT, s_xT_out, s_h, s_h_out = sem("s_xT"), sem("s_xT_out"), sem("s_h"), sem("s_h_out")
        s_hT, s_hT_out, s_y, s_y_out = sem("s_hT"), sem("s_hT_out"), sem("s_y"), sem("s_y_out")
        y_got, sparse_done = sem("y_got"), sem("sparse_done")
        o_ready, o_stored = sem("o_ready"), sem("o_stored")

        def node_major(ap):
            return ap.rearrange("(t p) d -> p t d", p=TP)

        def chunked(ap):
            return ap.rearrange("(c p) d -> p c d", p=128)

        def row(name, parts=TP):
            return rows[0:parts, ROWS.index(name), :]

        def row_ap(ap, parts=128):
            return ap.partition_broadcast(parts)

        n_vec = len(VECS) + 1 + len(ROWS) + 5
        n_w = 13

        def dense_weights(sp, first, w1d, w2d, ne):
            c1, f = KD, w1d.shape[2]
            c2 = f // 128
            w1v = w1d.rearrange("e (c p) h -> e p c h", p=128)
            w2v = w2d.rearrange("e (c p) d -> e p c d", p=128)
            for i, n in ((0, 1), (1, ne // 2 - 1)):
                if i == 0:
                    passes(sp, None, first, w1v, w2v, c1, c2, f)
                else:
                    with sp.Fori(1, ne // 2) as r:
                        passes(sp, r, first, w1v, w2v, c1, c2, f)

        def passes(sp, i, first, w1v, w2v, c1, c2, f):
            for u in range(2):
                e = u if i is None else i * 2 + u
                if i is not None or first:
                    sp.wait_ge(moe_used, first + u - 1 if i is None else i * 2 + (first + u - 1))
                sp.dma_start(wa[:, u, 0:c1 * f].rearrange("p (c h) -> p c h", c=c1),
                             w1v[bass.ds(e, 1)].rearrange("o p c h -> p (o c) h")).then_inc(moe_w[u], 16)
                sp.dma_start(wb[:, u, 0:c2 * D].rearrange("p (c h) -> p c h", c=c2),
                             w2v[bass.ds(e, 1)].rearrange("o p c h -> p (o c) h")).then_inc(moe_w[u], 16)

        def at(s, c, plus):
            return s + plus if isinstance(s, int) else s[0] * 4 + (c + plus)

        def back(s):
            return s - 1 if isinstance(s, int) else s

        def ahead(s):
            return s + 1 if isinstance(s, int) else s

        block = ctx.enter_context(nc.Block())

        @block.sync
        def _(sp):
            for w, name in enumerate(("src", "dst", "edge_type_8")):
                by_chunk = a[name].rearrange("(c e) -> c e", e=EP)
                sp.dma_start(raw[:, w, 0, :], by_chunk[0:128]).then_inc(ld_edges, 16)
                sp.dma_start(raw[0:ROWCH[1], w, 1, :], by_chunk[128:EC]).then_inc(ld_edges, 16)
            sp.dma_start(srcs[:, :], a["src"].rearrange("(p c) -> p c", p=EP)).then_inc(ld_edges, 16)
            sp.dma_start(dpm, a["dst"].rearrange("(p c) -> p c", p=EP)).then_inc(ld_edges, 16)
            sp.dma_start(dnx[0:EP - 1, :], a["dst"][1:1 + (EP - 1) * EC].rearrange("(p c) -> p c", c=EC)
                         ).then_inc(ld_edges, 16)
            sp.dma_start(dnx[EP - 1:EP, 0:EC - 1], a["dst"][E - EC + 1:E].rearrange("(p c) -> p c", p=1)
                         ).then_inc(ld_edges, 16)
            sp.dma_start(x[:, :, :], node_major(a["x"])).then_inc(ld_x, 16)
            for name, src in (("bq", a["L0_mix_bq"]), ("b1", a["L0_mix_b1"]),
                              ("bqk", a["L1_mix_b_qk"].rearrange("k d -> (k d)")),
                              ("gamma", a["L1_mix_gamma"]), ("beta", a["L1_mix_beta"]),
                              ("eg", a["L0_ffn_ln_g"].rearrange("e d -> (e d)")),
                              ("eb", a["L0_ffn_ln_b"].rearrange("e d -> (e d)")),
                              ("eb1", a["L0_ffn_b1"].rearrange("e d -> (e d)"))):
                v = src.rearrange("(r c) -> r c", c=128)
                sp.dma_start(vecrows[VCOL[name]:VCOL[name] + v.shape[0], :], v).then_inc(ld_vec, 16)
            sp.dma_start(b1rows[:, :, :], a["L1_ffn_b1"].rearrange("e (j c) -> (e j) c", c=128)
                         .rearrange("(h r) c -> r h c", r=128)).then_inc(ld_vec, 16)
            for name, src in zip(ROWS, (a["L0_mix_bk"], a["L0_mix_bv"], a["L0_mix_bo"], a["L0_mix_b2"],
                                        a["L0_mix_ln1_g"], a["L0_mix_ln1_b"], a["L0_mix_ln2_g"],
                                        a["L0_mix_ln2_b"], a["L0_gnn_bias_param"], a["L1_gnn_conv_bias"],
                                        a["L1_gnn_gn_weight"], a["L1_gnn_gn_bias"],
                                        a["L1_gnn_gn_mean_scale"], a["L1_mix_b_v"])):
                sp.dma_start(rows[:, ROWS.index(name), :], row_ap(src)).then_inc(ld_vec, 16)
            sp.dma_start(comp[:, :], row_ap(a["L0_gnn_comp"].rearrange("r b -> (r b)"))).then_inc(ld_vec, 16)
            sp.dma_start(rb0[:, :], row_ap(a["L0_ffn_br"])).then_inc(ld_vec, 16)
            sp.dma_start(rb1[:, :], row_ap(a["L1_ffn_br"])).then_inc(ld_vec, 16)
            sp.dma_start(bcomb[:, :], row_ap(a["L1_gnn_b_comb"])).then_inc(ld_vec, 16)
            sp.dma_start(b2e0[:, :], a["L0_ffn_b2"]).then_inc(ld_vec, 16)
            n = 0
            for dst, src in ((basis[:, :, :, :], a["L0_gnn_basis"].rearrange("b (c p) d -> p b c d", p=128)),
                             (loopw[:, :, :], chunked(a["L0_gnn_loop_weight"])),
                             (wq[:, :, :], chunked(a["L0_mix_Wq"])),
                             (wkv[:, :, 0:D], chunked(a["L0_mix_Wk"])),
                             (wkv[:, :, D:2 * D], chunked(a["L0_mix_Wv"])),
                             (wo[:, :, :], chunked(a["L0_mix_Wo"])),
                             (w1[:, :, :], chunked(a["L0_mix_W1"])),
                             (w2[:, :, :], chunked(a["L0_mix_W2"])),
                             (wr0[:, :, :], chunked(a["L0_ffn_Wr"])),
                             (wr1[:, :, :], chunked(a["L1_ffn_Wr"])),
                             (wbc[:, :, 0:DB], chunked(a["L1_gnn_W_bases"])),
                             (wbc[:, :, DB:], chunked(a["L1_gnn_W_comb"])),
                             (b2e1[:, :], a["L1_ffn_b2"])):
                sp.dma_start(dst, src).then_inc(ld_w, 16)
                n += 1
            hd = msgs.ap().rearrange("(t p r) d -> t p (r d)", p=TP, r=R0)
            for t in range(NT):
                sp.wait_ge(h_copied, 4 * (t + 1))
                sp.dma_start(hd[t], hrow[:, t % 2, :]).then_inc(h_stored, 16)
                sp.wait_ge(h_stored, 16 * (t + 1))
            sp.wait_ge(m_mm, 7)
            for dst, src in ((lwq, a["L1_mix_W_qk"][0]), (lwk, a["L1_mix_W_qk"][1]), (lwv, a["L1_mix_W_v"])):
                sp.dma_start(dst[:, :, :], chunked(src)).then_inc(ld_lw, 16)
            dense_weights(sp, 0, a["L0_ffn_W1"], a["L0_ffn_W2"], E0)
            w1v = a["L1_ffn_W1"].rearrange("e (c p) h -> e p c h", p=128)
            w2v = a["L1_ffn_W2"].rearrange("e (c p) d -> e p c d", p=128)

            def expert_weights(e, slot):
                sp.dma_start(ew1[:, slot], w1v[bass.ds(e, 1)].rearrange("o p c h -> p (o c) h")
                             ).then_inc(ew_loaded[slot], 16)
                sp.dma_start(ew2[:, slot], w2v[bass.ds(e, 1)].rearrange("o p c h -> p (o c) h")
                             ).then_inc(ew_loaded[slot], 16)

            for q in range(4):
                sp.wait_ge(moe_used, E0)
                expert_weights(q, q)
            with sp.Fori(1, E1 // 4) as i:
                for q in range(4):
                    sp.wait_ge(s_y, i * 4 + (q - 3))
                    expert_weights(i * 4 + q, q)
            sp.wait_ge(sparse_done, 1)
            crowded = sp.value_load(overi[0:1, 0:1], min_val=0, max_val=1)
            with sp.If(crowded > 0):
                dense_weights(sp, E0, a["L1_ffn_W1"], a["L1_ffn_W2"], E1)
            with sp.Else():
                sp.nop()
            sp.wait_ge(o_ready, NT)
            sp.dma_start(node_major(a["out"]), x[:, :, :]).then_inc(o_stored, 16)
            sp.wait_ge(o_stored, 16)

        @block.gpsimd
        def _(pool):
            step = Chain(pool, pchain)
            pool.iota(iota_f[:, :], pattern=[[1, N]], base=0, channel_multiplier=0,
                      allow_small_or_imprecise_dtypes=True).then_inc(consts_ready, 1)
            step.done(pool.memset(ident[:, :], 0.0))
            step.done(pool.affine_select(out=ident[:, :], in_=ident[:, :], compare_op=ALU.not_equal, fill=1.0,
                                         base=0, pattern=[[-1, 128]], channel_multiplier=1))
            pool.tensor_copy(identb[:, :], ident[:, :]).then_inc(consts_ready, 1)
            step.done(pool.memset(headmask[:, :], 0.0))
            for h in range(4):
                step.done(pool.memset(headmask[32 * h:32 * h + 32, 32 * h:32 * h + 32], 1.0))
            step.done(pool.memset(tri[:, :], 1.0))
            step.done(pool.affine_select(out=tri[:, :], in_=tri[:, :], compare_op=ALU.is_gt, fill=0.0, base=0,
                                         pattern=[[1, TP]], channel_multiplier=-1))
            step.done(pool.iota(nodeid[:, :], pattern=[[TP, NT]], base=0, channel_multiplier=1,
                                allow_small_or_imprecise_dtypes=True))
            pool.memset(ones[:, :], 1.0).then_inc(consts_ready, 1)
            pool.wait_ge(ed_out, 1)
            pool.wait_ge(h_stored, 16 * NT)
            for c in range(EC):
                if c >= GRING:
                    pool.wait_ge(e_used, c - GRING + 4)
                pool.indirect_dma_start(gath[:, c % GRING, :], None, msgs.ap(),
                                        bass.IndirectOffsetOnAxis(ap=rowid[:, c:c + 1].bitcast(U32), axis=0)
                                        ).then_inc(gathered[c % GRING], 16)

            pool.wait_ge(p_out, 2)
            pool.wait_ge(btab_stored, 16)
            slow = pool.value_load(loose[0:1, 0:1], min_val=0, max_val=E)
            with pool.If(slow > 0):
                pool.nop()
            with pool.Else():
                for g in range(EC // GRING):
                    if g >= 2:
                        pool.wait_ge(run_stored[g % 2], 16 * (g // 2))
                        pool.wait_ge(run_head, g - 1)
                    for u in range(GRING):
                        c = g * GRING + u
                        pool.indirect_dma_start(run[:, (g % 2) * GRING + u, :], None, btab.ap(),
                                                bass.IndirectOffsetOnAxis(ap=srcs[:, c:c + 1].bitcast(U32),
                                                                          axis=0)).then_inc(run_loaded[g % 2], 16)
                pool.wait_ge(run_stored[0], 16 * 6)
                pool.wait_ge(run_stored[1], 16 * 5)
                for k in range(2):
                    for t in range(NT):
                        pool.indirect_dma_start(kphi[:, t, k * DB:(k + 1) * DB], None, rtab.ap(),
                                                bass.IndirectOffsetOnAxis(ap=ends[:, k, t:t + 1], axis=0)
                                                ).then_inc(ends_got, 16)
                pool.nop()
            pool.wait_ge(put_ready, 1)
            pool.wait_ge(xs_zero, 16 * 4)
            for k in range(2):
                for t in range(NT):
                    pool.indirect_dma_start(xs.ap(), bass.IndirectOffsetOnAxis(ap=put[:, k, t:t + 1], axis=0),
                                            xn[:, t, :], None).then_inc(xs_put, 16)
            for q in range(4):
                pool.wait_ge(y_stored[q], 16 * (E1 // 4))
            for k in range(2):
                for t in range(NT):
                    pool.indirect_dma_start((ya, yb)[k][:, t, :], None, ys.ap(),
                                            bass.IndirectOffsetOnAxis(ap=get[:, k, t:t + 1], axis=0)
                                            ).then_inc(y_got, 16)

        @block.tensor
        def _(pe):
            pe.wait_ge(consts_ready, 4)

            pe.wait_ge(edges_ready, 1)
            for w in range(4):
                for h, n in enumerate(ROWCH):
                    pe.transpose(ps[0:EP, w // 2, (w % 2) * EC + h * 128:(w % 2) * EC + h * 128 + n],
                                 crow[0:n, w, h, :], ident[0:n, 0:n])
            for h, n in enumerate(ROWCH):
                pe.transpose(ps[0:1, 2, h * 128:h * 128 + n], span[0:n, h, 2:3], ident[0:n, 0:n])
                m = pe.matmul(ps[0:1, 3, 0:1], span[0:n, h, 3:4], ones[0:n, 0:1], start=(h == 0), stop=(h == 1))
            m.then_inc(ed_mm, 1)
            pe.wait_ge(ed_out, 1)

            ntr = [0]

            def turn(src, ready, count, b0=0):
                pe.wait_ge(ready, count)
                for j in range(KD):
                    for t in range(NT):
                        bk, off = (b0 + j, t * TP) if t < 4 else (b0 + 2, j * TP)
                        m = pe.transpose(ps[:, bk, off:off + TP], src[:, t, j * 128:(j + 1) * 128],
                                         ident[0:TP, 0:TP])
                m.then_inc(tr_mm, 1)
                ntr[0] += 1

            def turned():
                pe.wait_ge(tr_copied, ntr[0])

            turn(xn, norm_ready, 1)
            turned()
            pe.wait_ge(ld_w, 16 * n_w)
            pe.wait_ge(wrel_ready, 1)
            for t in range(NT):
                for g in range(4):
                    n = 4 * t + g
                    if n >= 4:
                        pe.wait_ge(h_copied, n - 3)
                    for k in range(KD):
                        m = pe.matmul(ps[0:TP, g, :], xnT[:, k, t * TP:(t + 1) * TP],
                                      wrel[:, k, 2 * g:2 * g + 2, :].rearrange("p r d -> p (r d)"),
                                      start=(k == 0), stop=(k == KD - 1))
                    m.then_inc(h_mm, 1)

            def spans(i, u, oh_col):
                if oh_col is None:
                    return ((0, 0, 512), (512 + GAP, 512, N))
                return ((oh_col, 0, WIN),)

            def clear(pairs, parts):
                for b in pairs:
                    pe.matmul(ps[0:parts, b, :], zerob[:, 0:parts], zerob[:, :], start=True, stop=True)

            def edge_pass(base, tiles, pair0, with_sums, windows):
                with pe.Fori(0, EC // GRING) as i:
                    for u in range(GRING):
                        col = pe.value_load(wincol[0:1, bass.ds(i * GRING + u, 1)], min_val=0,
                                            max_val=1024 - WIN) if windows else None
                        pe.wait_ge(e_oh, i * GRING + (base + u + 1))
                        if with_sums:
                            pe.wait_ge(gathered[u], i * 16 + 16)
                            for j in range(KD):
                                for at_, lo, hi in spans(i, u, col):
                                    pe.matmul(psf[:, bass.ds(at_ + j * 1024, hi - lo)],
                                              gath[:, u, j * 128:(j + 1) * 128], ohf[:, u % 3, lo:hi],
                                              start=False, stop=False, skip_group_check=True)
                        for k, s in enumerate(tiles):
                            for at_, lo, hi in spans(i, u, col):
                                m = pe.matmul(psf[0:TP, bass.ds(at_ + (pair0 + k) * 1024, hi - lo)],
                                              ohs[:, u % 3, s * TP:(s + 1) * TP], ohd[:, u % 3, lo:hi],
                                              start=False, stop=False, skip_group_check=True)
                        m.then_inc(e_used, 1)

            pe.sem_inc(e_used, 3)
            pe.wait_ge(h_copied, 4 * NT)
            clear(range(4), 128)
            clear(range(4, 8), TP)
            for j in range(KD):
                for at_, lo, hi in spans(0, 0, None):
                    for k in range(KD):
                        pe.matmul(psf[:, at_ + j * 1024:at_ + j * 1024 + hi - lo],
                                  loopw[:, k, j * 128:(j + 1) * 128], xnT[:, k, lo:hi], start=False, stop=False,
                                  skip_group_check=True)
            spread = pe.value_load(wide[0:1, 0:1], min_val=0, max_val=E)
            with pe.If(spread > 0):
                edge_pass(0, (0, 1), 2, True, False)
                pe.nop()
            with pe.Else():
                edge_pass(0, (0, 1), 2, True, True)
                pe.nop()
            pe.wait_ge(sums_out, 1)
            for t in range(NT):
                for j in range(KD):
                    m = pe.transpose(ps[0:TP, t // 2, (t % 2) * D + j * 128:(t % 2) * D + (j + 1) * 128],
                                     xT2[:, j, t * TP:(t + 1) * TP], ident[:, :])
            m.then_inc(adj_mm, 1)
            pe.wait_ge(sums_out, 2)
            clear(range(6), TP)
            with pe.If(spread > 0):
                edge_pass(EC, (2, 3, 4), 0, False, False)
                pe.nop()
            with pe.Else():
                edge_pass(EC, (2, 3, 4), 0, False, True)
                pe.nop()
            pe.wait_ge(adj_ready, 5)
            for t in range(NT):
                for s in range(NT):
                    m = pe.matmul(ps[0:TP, 6, t:t + 1], adjT[:, s, t * TP:(t + 1) * TP], ones[0:TP, 0:1],
                                  start=(s == 0), stop=(s == NT - 1))
            m.then_inc(p_mm, 1)
            pe.wait_ge(p_out, 1)
            for t in range(NT):
                for s in range(t + 1):
                    pe.matmul(ps[0:TP, 6, t:t + 1], (tri if s == t else ones)[0:TP, 0:TP], cnt[:, s:s + 1],
                              start=(s == 0), stop=(s == t))
            pe.matmul(ps[0:1, 7, 0:1], unsorted[:, :], ones[0:EP, 0:1], start=True, stop=True).then_inc(p_mm, 1)

            pe.wait_ge(ld_vec, 16 * n_vec)
            pe.transpose(ps[:, 0, 0:NVEC], vecrows[0:NVEC, :], ident[0:NVEC, 0:NVEC])
            pe.transpose(ps[:, 1, 0:128], b1rows[:, 0, :], ident[:, :])
            pe.transpose(ps[:, 1, 128:256], b1rows[:, 1, :], ident[:, :]).then_inc(tr_mm, 1)
            ntr[0] += 1
            turned()

            nm = [0]

            def product(m):
                nm[0] += 1
                m.then_inc(m_mm, 1)

            def feature_major(w, src, j, b0, w_off=0):
                for hf in range(2):
                    for k in range(KD):
                        m = pe.matmul(ps[:, b0 + hf, 0:HN], w[:, k, w_off + j * 128:w_off + (j + 1) * 128],
                                      src[:, k, hf * HN:(hf + 1) * HN], start=(k == 0), stop=(k == KD - 1))
                return m

            pe.wait_ge(h_copied, 4 * NT)
            for j in range(KD):
                product(feature_major(wq, xnT, j, 2 * j))
            for t in range(NT):
                if t == 1:
                    pe.wait_ge(m_out, 1)
                if t >= 2:
                    pe.wait_ge(m_out, t + 1)
                for k in range(KD):
                    m = pe.matmul(ps[0:TP, 4 * (1 - t % 2), :], xnT[:, k, t * TP:(t + 1) * TP], wkv[:, k, :],
                                  start=(k == 0), stop=(k == KD - 1))
                product(m)
            pe.wait_ge(m_out, 7)
            for j in range(KD):
                for t in range(NT):
                    m = pe.matmul(ps[:, j, 0:129], kphi[:, t, j * 128:(j + 1) * 128], vext[:, t, j, :],
                                  start=(t == 0), stop=(t == NT - 1))
            product(m)
            pe.wait_ge(m_out, 8)
            for j in range(KD):
                if j:
                    pe.wait_ge(m_out, 9)
                for hf in range(2):
                    pe.matmul(ps[:, 2 + hf, 0:HN], ksbd[:, j, :], qphi[:, j, hf * HN:(hf + 1) * HN],
                              start=True, stop=True)
                    m = pe.matmul(ps[:, hf, 0:HN], kvbd[:, j, :], qphi[:, j, hf * HN:(hf + 1) * HN],
                                  start=True, stop=True)
                product(m)
            pe.wait_ge(m_out, 10)
            for t in range(NT):
                if t >= 2:
                    pe.wait_ge(m_out, 10 + t - 1)
                for k in range(KD):
                    m = pe.matmul(ps[0:TP, t % 2, 0:D], xT2[:, k, t * TP:(t + 1) * TP], wo[:, k, :],
                                  start=(k == 0), stop=(k == KD - 1))
                product(m)
            pe.wait_ge(m_out, 15)
            turn(ya, norm_ready, 2)
            turned()
            for m8_ in range(8):
                if m8_ >= 2:
                    pe.wait_ge(m_relu, m8_ - 1)
                product(feature_major(w1, xT2, m8_, 2 * (m8_ % 2)))
            pe.wait_ge(m_relu, 8)
            for t in range(NT):
                if t >= 2:
                    pe.wait_ge(m_out, 15 + t - 1)
                for k in range(8):
                    m = pe.matmul(ps[0:TP, t % 2, 0:D], big[:, k, t * TP:(t + 1) * TP], w2[:, k, :],
                                  start=(k == 0), stop=(k == 7))
                product(m)

            moe = dict(h=0, y=0, r=0, x=0, e=0)

            def router(ne, w_r, b2, logits_src):
                for t in range(NT):
                    for k in range(KD):
                        m = pe.matmul(ps[0:TP, 6, t * ne:(t + 1) * ne], logits_src[:, k, t * TP:(t + 1) * TP],
                                      w_r[:, k, :], start=(k == 0), stop=(k == KD - 1))
                m.then_inc(r_mm, 1)
                moe["r"] += 1
                pe.wait_ge(r_out, moe["r"])
                for t in range(NT):
                    bk, off = (6, t * TP) if t < 4 else (7, 0)
                    m = pe.transpose(ps[0:ne, bk, off:off + TP], comb[:, t, 0:ne], ident[0:TP, 0:TP])
                m.then_inc(r_mm, 1)
                moe["r"] += 1
                pe.wait_ge(r_out, moe["r"])
                y0 = moe["y"]
                for t in range(NT):
                    if t >= 2:
                        pe.wait_ge(moe_acc, y0 + t - 1)
                    pe.matmul(ps[0:TP, 4 + t % 2, 0:D], combT[0:ne, t * TP:(t + 1) * TP], b2[:, :], start=True,
                              stop=True).then_inc(moe_y, 1)
                moe["y"] = y0 + NT
                pe.wait_ge(moe_acc, moe["y"])

            def dense(ne, nh, exp_src, per_expert_x):
                h0, y0, x0, e0 = moe["h"], moe["y"], moe["x"], moe["e"]
                with pe.Fori(0, ne // 2) as i:
                    for u in range(2):
                        pe.wait_ge(moe_w[u], i * 32 + (e0 // 2 * 32 + 32))
                        if per_expert_x:
                            pe.wait_ge(moe_x, i * 2 + (x0 + u + 1))
                        wav = wa[:, u, 0:KD * nh * 128].rearrange("p (c h) -> p c h", c=KD)
                        wbv = wb[:, u, 0:nh * D].rearrange("p (c h) -> p c h", c=nh)
                        for m_ in range(nh):
                            pe.wait_ge(moe_act, i * (2 * nh) + (h0 + u * nh + m_ + 1))
                            feature_major(wav, exp_src, m_, 2 * (m_ % 2)).then_inc(moe_h, 1)
                        pe.wait_ge(moe_act, i * (2 * nh) + (h0 + 2 + (u + 1) * nh))
                        for t in range(NT):
                            pe.wait_ge(moe_acc, i * (2 * NT) + (y0 + u * NT + t - 1))
                            for k in range(nh):
                                m = pe.matmul(ps[0:TP, 4 + (u * NT + t) % 2, 0:D], big[:, k, t * TP:(t + 1) * TP],
                                              wbv[:, k, :], start=(k == 0), stop=(k == nh - 1))
                            m.then_inc(moe_y, 1)
                        m = pe.matmul(ps[0:1, 7, 0:1], zerob[:, 0:1], zerob[:, 0:1], start=True, stop=True)
                        m.then_inc(moe_used, 1)
                moe["h"], moe["y"], moe["e"] = h0 + ne * nh, y0 + ne * NT, e0 + ne
                moe["x"] = x0 + (ne if per_expert_x else 0)

            turn(ya, norm_ready, 3)
            turned()
            turn(xn, norm_ready, 4)
            turned()
            router(E0, wr0, b2e0, xT2)
            dense(E0, H0 // 128, qphi, True)

            turn(xn, norm_ready, 5)
            turned()
            nc_ = [0]

            def cproduct(m):
                nc_[0] += 1
                m.then_inc(c_mm, 1)

            for t in range(NT):
                if t >= 2:
                    pe.wait_ge(c_out, t - 1)
                for k in range(KD):
                    m = pe.matmul(ps[0:TP, t % 2, 0:DB + NH * NK], xnT[:, k, t * TP:(t + 1) * TP], wbc[:, k, :],
                                  start=(k == 0), stop=(k == KD - 1))
                cproduct(m)
            for hf in range(2):
                for k in range(KD):
                    m = pe.matmul(ps[:, 2 + hf, 0:HN], wbc[:, k, 0:DB], xnT[:, k, hf * HN:(hf + 1) * HN],
                                  start=(k == 0), stop=(k == KD - 1))
            cproduct(m)
            pe.wait_ge(c_out, 7)
            for t in range(NT):
                if t >= 2:
                    pe.wait_ge(c_out, 7 + t - 1)
                for s in range(NT):
                    m = pe.matmul(ps[0:TP, t % 2, 0:2 * DB], adjT[:, s, t * TP:(t + 1) * TP], bas[:, s, :],
                                  start=(s == 0), stop=(s == NT - 1))
                cproduct(m)
            pe.wait_ge(c_out, 12)
            pe.wait_ge(p_out, 2)
            slow = pe.value_load(loose[0:1, 0:1], min_val=0, max_val=E)
            with pe.If(slow > 0):
                for d in range(NT):
                    if d:
                        pe.wait_ge(mask_out, 2 * d)
                    for s in range(NT):
                        bk, off = (0, s * TP) if s < 4 else (1, 0)
                        m = pe.transpose(ps[0:TP, bk, off:off + TP], adjT[:, s, d * TP:(d + 1) * TP],
                                         ident[0:TP, 0:TP])
                    m.then_inc(mask_mm, 1)
                pe.wait_ge(mask_out, 2 * NT)
                for t in range(NT):
                    with pe.Fori(0, TP // 5) as i:
                        for u in range(5):
                            pe.wait_ge(mx_out, i * 5 + max(t * TP + u, 1))
                            row_ = identb[0:TP, bass.ds(i * 5 + u, 1)].to_broadcast([TP, 128])
                            b0 = 0 if u in (0, 2) else 2 if u in (1, 3) else 4
                            pe.matmul(ps[:, b0, 0:512], row_, maskb[:, t, 0:512], start=True, stop=True)
                            pe.matmul(ps[:, b0 + 1, 0:N - 512], row_, maskb[:, t, 512:N], start=True,
                                      stop=True).then_inc(mx_mm, 1)
                pe.wait_ge(mx_kept, N // 5)
                for t in range(NT):
                    bk, off = (0, t * 128) if t < 4 else (1, 0)
                    m = pe.transpose(ps[0:TP, bk, off:off + 128], aggmT[:, t * TP:(t + 1) * TP], ident[:, :])
                m.then_inc(mx_turned, 1)
                pe.nop()
            with pe.Else():
                pe.nop()
            pe.wait_ge(c_out, 14)
            for t in range(NT):
                m = pe.matmul(ps[:, 2, 0:D], ones[0:TP, :], ya[:, t, :], start=(t == 0), stop=(t == NT - 1))
            cproduct(m)
            pe.wait_ge(c_out, 16)
            for t in range(NT):
                m = pe.matmul(ps[:, 3, 0:D], ones[0:TP, :], yb[:, t, :], start=(t == 0), stop=(t == NT - 1))
            cproduct(m)
            pe.wait_ge(c_out, 17)

            def lproduct(m):
                m.then_inc(l_mm, 1)

            pe.wait_ge(ld_lw, 48)
            for j in range(KD):
                lproduct(feature_major(lwq, xnT, j, 2 * j))
            for j in range(KD):
                pe.wait_ge(l_out, j + 1)
                lproduct(feature_major(lwk, xnT, j, 2 * j))
            for t in range(NT):
                if t >= 2:
                    pe.wait_ge(l_out, 4 + t - 1)
                for k in range(KD):
                    m = pe.matmul(ps[0:TP, 4 + t % 2, 0:D], xnT[:, k, t * TP:(t + 1) * TP], lwv[:, k, :],
                                  start=(k == 0), stop=(k == KD - 1))
                lproduct(m)
            pe.wait_ge(l_out, 9)
            for t in range(NT):
                for j in range(KD):
                    q = 2 * t + j
                    m = pe.transpose(ps[0:TP, q // 4, (q % 4) * 128:(q % 4 + 1) * 128],
                                     big[:, j, t * TP:(t + 1) * TP], ident[:, :])
            lproduct(m)
            pe.wait_ge(l_out, 10)
            for j in range(KD):
                for t in range(NT):
                    m = pe.matmul(ps[:, j, 0:D], smx[:, t, j * 128:(j + 1) * 128], kphi[:, t, :],
                                  start=(t == 0), stop=(t == NT - 1))
            lproduct(m)
            pe.wait_ge(l_out, 11)
            for t in range(NT):
                if t >= 2:
                    pe.wait_ge(l_out, 11 + t - 1)
                for k in range(KD):
                    m = pe.matmul(ps[0:TP, 4 + t % 2, 0:D], qphi[:, k, t * TP:(t + 1) * TP], lam[:, k, :],
                                  start=(k == 0), stop=(k == KD - 1))
                lproduct(m)
            pe.wait_ge(l_out, 16)
            turn(xn, norm_ready, 6)
            turned()
            router(E1, wr1, b2e1, xnT)
            pe.wait_ge(r_out, moe["r"] + 1)
            for t in range(NT):
                for s in range(t + 1):
                    pe.matmul(ps[0:TP, 6, t * E1:(t + 1) * E1], (tri if s == t else ones)[0:TP, 0:TP],
                              lg[:, s, :], start=(s == 0), stop=(s == t))
            for s in range(NT):
                m = pe.matmul(ps[0:TP, 7, 0:E1], ones[0:TP, 0:TP], lg[:, s, :], start=(s == 0),
                              stop=(s == NT - 1))
            m.then_inc(r_mm, 1)
            pe.wait_ge(put_ready, 1)

            def carry_waits(bank):
                pe.matmul(ps[:, bank, 511:512], zerob[:, 0:128], zerob[:, 0:1], start=True, stop=True)

            def turn_rows(s, c):
                pe.wait_ge(xe_loaded[c % 4], 16 * (s // 4 + 1) if isinstance(s, int) else (s[0] + (c // 4 + 1)) * 16)
                if c >= 2:
                    pe.wait_ge(s_xT_out, at(s, c, -1))
                carry_waits(c % 2)
                for j in range(KD):
                    m = pe.transpose(ps[:, c % 2, j * CAP:(j + 1) * CAP], xe[:, c % 4, j * 128:(j + 1) * 128],
                                     ident[0:CAP, 0:CAP])
                m.then_inc(s_xT, 1)

            def hidden(s, c):
                pe.wait_ge(ew_loaded[c % 4], 32 * (s // 4 + 1) if isinstance(s, int) else (s[0] + (c // 4 + 1)) * 32)
                pe.wait_ge(s_xT_out, at(s, c, 1))
                if c >= 2:
                    pe.wait_ge(s_h_out, at(s, c, -1))
                for k in range(KD):
                    m = pe.matmul(ps[0:CAP, 2 + c % 2, :], xeT[:, c % 2, k, :], ew1[:, c % 4, k, :],
                                  start=(k == 0), stop=(k == KD - 1))
                m.then_inc(s_h, 1)

            def turn_hidden(s, c):
                pe.wait_ge(s_h_out, at(s, c, 1))
                if c >= 2:
                    pe.wait_ge(s_hT_out, at(s, c, -1))
                carry_waits(4 + c % 2)
                for j in range(4):
                    m = pe.transpose(ps[:, 4 + c % 2, j * CAP:(j + 1) * CAP], hs[:, c % 2, j * 128:(j + 1) * 128],
                                     ident[0:CAP, 0:CAP])
                m.then_inc(s_hT, 1)

            def result(s, c):
                pe.wait_ge(s_hT_out, at(s, c, 1))
                if c >= 2:
                    pe.wait_ge(s_y_out, at(s, c, -1))
                for k in range(4):
                    m = pe.matmul(ps[0:CAP, 6 + c % 2, 0:D], hact[:, c % 2, k, :], ew2[:, c % 4, k, :],
                                  start=(k == 0), stop=(k == 3))
                m.then_inc(s_y, 1)

            def pe_step(s, c, first=False, last=False):
                if not first:
                    turn_hidden(back(s), c - 1)
                hidden(s, c)
                if not first:
                    result(back(s), c - 1)
                if not last:
                    turn_rows(ahead(s), c + 1)

            turn_rows(0, 0)
            for s in range(3):
                pe_step(s, s, first=(s == 0))
            with pe.Fori(0, (E1 - 4) // 4) as i:
                for c in range(3, 7):
                    pe_step((i,), c)
            pe_step(E1 - 1, E1 - 1, last=True)
            turn_hidden(E1 - 1, E1 - 1)
            result(E1 - 1, E1 - 1)
            pe.wait_ge(sparse_done, 1)
            crowded = pe.value_load(overi[0:1, 0:1], min_val=0, max_val=1)
            with pe.If(crowded > 0):
                dense(E1, H1 // 128, xnT, False)
            with pe.Else():
                pe.nop()

        @block.scalar
        def _(act):
            def sqrt_of(dst, src, count):
                act.wait_ge(var_ready, count)
                nc.scalar.activation(dst, src, ACT.Sqrt).then_inc(rstd_ready, 1)

            act.sem_inc(moe_act, 2)
            act.wait_ge(consts_ready, 4)
            for q in range(4):
                act.dma_start(xs.ap()[0:SPARE, :].rearrange("(q p r) d -> q p (r d)", q=4, p=128)[q],
                              zerof[:, :]).then_inc(xs_zero, 16)
            sqrt_of(rstd[:, :], rstd[:, :], 1)
            for t in range(NT):
                for g in range(4):
                    act.wait_ge(h_mm, 4 * t + g + 1)
                    if g == 0 and t >= 2:
                        act.wait_ge(h_stored, 16 * (t - 1))
                    nc.scalar.activation(hrow[:, t % 2, g * 512:(g + 1) * 512], ps[0:TP, g, :],
                                         ACT.Copy).then_inc(h_copied, 1)
            for j in range(KD):
                act.wait_ge(m_pre, j + 1)
                nc.scalar.activation((tmpf, tmpg)[j][:, :], (tmpf, tmpg)[j][:, :], ACT.Exp).then_inc(m_exp, 1)
            for t in range(NT):
                act.wait_ge(m_pre, 3 + t)
                nc.scalar.activation(tmpr[:, (t % 2) * D:(t % 2 + 1) * D], tmpr[:, (t % 2) * D:(t % 2 + 1) * D],
                                     ACT.Exp).then_inc(m_exp, 1)
            sqrt_of(rstd[:, :], rstd[:, :], 2)
            for m_ in range(8):
                act.wait_ge(m_mm, 16 + m_)
                c = VCOL["b1"] + m_
                nc.scalar.activation(big[:, m_, :].rearrange("p (b n) -> p b n", b=2),
                                     ps[:, 2 * (m_ % 2):2 * (m_ % 2) + 2, 0:HN], ACT.Relu,
                                     bias=vecs[:, c:c + 1]).then_inc(m_relu, 1)
            for n in (3, 4, 5):
                sqrt_of(rstd[:, :], rstd[:, :], n)
            moe = dict(h=0, y=0, r=0)

            def gates():
                moe["r"] += 1
                act.wait_ge(r_pre, moe["r"])
                nc.scalar.activation(gate[:, :, 1:2], gate[:, :, 0:1], ACT.Exp).then_inc(r_exp, 1)

            def dense(ne, nh, func, bias_of):
                h0, y0 = moe["h"], moe["y"] + NT
                with act.Fori(0, ne // 2) as i:
                    for u in range(2):
                        for m_ in range(nh):
                            act.wait_ge(moe_h, i * (2 * nh) + (h0 + u * nh + m_ + 1))
                            if m_ == 0:
                                act.wait_ge(moe_acc, i * (2 * NT) + (y0 + u * NT))
                            nc.scalar.activation(big[:, m_, :].rearrange("p (b n) -> p b n", b=2),
                                                 ps[:, 2 * (m_ % 2):2 * (m_ % 2) + 2, 0:HN], func,
                                                 bias=bias_of(i, u, m_)).then_inc(moe_act, 1)
                moe["h"], moe["y"] = h0 + ne * nh, y0 + ne * NT

            gates()
            dense(E0, 8, ACT.Gelu, lambda i, u, m_: vecs[:, bass.ds(i * 16 + (VCOL["eb1"] + u * 8 + m_), 1)])
            sqrt_of(rstd[:, :], rstd[:, :], 6)
            act.wait_ge(var_ready, 7)
            nc.scalar.activation(dinv[:, :], dinv[:, :], ACT.Sqrt).then_inc(rstd_ready, 1)
            act.wait_ge(c_out, 5)
            act.dma_start(node_major(btab.ap()), bas[:, :, 0:DB]).then_inc(btab_stored, 16)
            act.wait_ge(p_out, 2)
            slow = act.value_load(loose[0:1, 0:1], min_val=0, max_val=E)
            with act.If(slow > 0):
                act.nop()
            with act.Else():
                for g in range(EC // GRING):
                    act.wait_ge(run_done, g + 1)
                    act.dma_start(rtab.ap().rearrange("(p c) d -> p c d", c=EC)[:, g * GRING:(g + 1) * GRING, :],
                                  run[:, (g % 2) * GRING:(g % 2 + 1) * GRING, :]).then_inc(run_stored[g % 2], 16)
                act.nop()
            act.wait_ge(var_ready, 8)
            nc.scalar.activation(gmean[:, :], gmean[:, :], ACT.Sqrt).then_inc(rstd_ready, 1)
            for j in range(KD):
                act.wait_ge(l_pre, j + 1)
                nc.scalar.activation(big[:, j, 0:N], big[:, j, 0:N], ACT.Exp, bias=kmax[:, j:j + 1],
                                     accum_out=ksum[:, j:j + 1]).then_inc(l_exp, 1)
            act.wait_ge(var_ready, 9)
            nc.scalar.activation(lrs[:, :], lrs[:, :], ACT.Sqrt).then_inc(rstd_ready, 1)
            sqrt_of(rstd[:, :], rstd[:, :], 10)
            gates()
            act.wait_ge(xs_put, 160)

            def load_rows(s, c):
                e = s if isinstance(s, int) else s[0] * 4 + c
                act.dma_start(xe[:, c % 4, :], xs.ap()[bass.ds(e * CAP, CAP), :]).then_inc(xe_loaded[c % 4], 16)

            def keep_hidden(s, c):
                act.wait_ge(s_h, at(s, c, 1))
                if c >= 2:
                    act.wait_ge(s_hT, at(s, c, -1))
                nc.scalar.copy(hs[:, c % 2, :], ps[0:CAP, 2 + c % 2, :]).then_inc(s_h_out, 1)

            def keep_result(s, c):
                act.wait_ge(s_y, at(s, c, 1))
                if c >= 4:
                    act.wait_ge(y_stored[c % 4], 16 * (s // 4) if isinstance(s, int) else (s[0] + c // 4) * 16)
                nc.scalar.copy(ye[:, c % 4, :], ps[0:CAP, 6 + c % 2, 0:D]).then_inc(s_y_out, 1)
                act.wait_ge(s_y_out, at(s, c, 1))
                e = s if isinstance(s, int) else s[0] * 4 + c
                act.dma_start(ys.ap()[bass.ds(e * CAP, CAP), :], ye[:, c % 4, :]).then_inc(y_stored[c % 4], 16)

            for q in range(4):
                load_rows(q, q)

            def act_step(s, c, load=True):
                keep_hidden(s, c)
                if c >= 1:
                    keep_result(back(s), c - 1)
                if load:
                    act.wait_ge(s_xT, at(s, c, 1))
                    load_rows(s + 4 if isinstance(s, int) else s, c + 4)

            for s in range(3):
                act_step(s, s)
            with act.Fori(0, (E1 - 8) // 4) as i:
                for c in range(3, 7):
                    act_step((i,), c)
            for s in range(E1 - 5, E1):
                act_step(s, s, load=(s + 4 < E1))
            keep_result(E1 - 1, E1 - 1)
            act.wait_ge(sparse_done, 1)
            crowded = act.value_load(overi[0:1, 0:1], min_val=0, max_val=1)
            with act.If(crowded > 0):
                dense(E1, 4, ACT.Relu, lambda i, u, m_: b1cols[:, bass.ds(i * 8 + (u * 4 + m_), 1)])
            with act.Else():
                act.nop()

        @block.vector
        def _(dve):
            v = nc.vector
            step = Chain(dve, dchain)
            done, mark = step.done, step.mark

            def mark_free(ins):
                ins.then_inc(mx_agg, 1)

            def tt(out, p, q, op):
                return v.tensor_tensor(out, p, q, op)

            mark(v.memset(zerof[:, :], 0.0))
            step.wait()
            v.memset(zerob[:, :], 0.0).then_inc(consts_ready, 1)
            for dst in (xnT, xT2, qphi):
                mark(v.memset(dst[:, :, N:NP], 0.0))
            step.wait()
            dve.wait_ge(ld_edges, 160)
            dve.wait_ge(consts_ready, 4)
            for h, n in enumerate(ROWCH):
                srow, drow, wrow, rrow = (crow[0:n, w, h, :] for w in range(4))
                mark(v.tensor_copy(srow, raw[0:n, 0, h, :]))
                mark(v.tensor_copy(drow, raw[0:n, 1, h, :]))
                mark(v.scalar_tensor_tensor(out=rrow, in0=raw[0:n, 0, h, :], scalar=float(R0),
                                            in1=raw[0:n, 2, h, :], op0=ALU.mult, op1=ALU.add))
                step.wait()
                low, high, col, over_ = (span[0:n, h, k:k + 1] for k in range(4))
                mark(v.tensor_reduce(low, drow, AX.X, ALU.min))
                done(v.tensor_reduce(high, drow, AX.X, ALU.max))
                mark(v.tensor_scalar(wrow, drow, low, None, ALU.subtract))
                mark(v.tensor_scalar(over_, high, low, float(WIN), ALU.subtract, ALU.is_ge))
                done(v.tensor_scalar(col, low, float(SEAM), float(GAP), ALU.is_ge, ALU.mult))
                m = tt(col, col, low, ALU.add)
                if h:
                    m.then_inc(edges_ready, 1)
                else:
                    mark(m)
            mark(v.memset(apart[:, 0:1], 0.0))
            done(tt(apart[:, 1:EC], dpm[:, 1:EC], dpm[:, 0:EC - 1], ALU.not_equal))
            mark(v.tensor_scalar(apart[:, 1:EC], apart[:, 1:EC], -BIG, None, ALU.mult))
            done(v.memset(dcmp[:, :], 0.0))
            mark(tt(dcmp[0:EP, 0:EC - 1], dpm[:, 0:EC - 1], dnx[:, 0:EC - 1], ALU.is_gt))
            done(tt(dcmp[0:EP - 1, EC - 1:EC], dpm[0:EP - 1, EC - 1:EC], dnx[0:EP - 1, EC - 1:EC], ALU.is_gt))
            mark(v.tensor_reduce(unsorted[:, :], dcmp[:, :], AX.X, ALU.add))
            dve.wait_ge(ed_mm, 1)
            mark(v.tensor_copy(srcf[:, :], ps[0:EP, 0, 0:EC]))
            mark(v.tensor_copy(dstf[:, :], ps[0:EP, 0, EC:2 * EC]))
            mark(v.tensor_copy(dstw[:, :], ps[0:EP, 1, 0:EC]))
            mark(v.tensor_copy(rowid[:, :], ps[0:EP, 1, EC:2 * EC]))
            mark(v.tensor_copy(wincol[:, :], ps[0:1, 2, 0:EC]))
            step.wait()
            v.tensor_copy(wide[:, :], ps[0:1, 3, 0:1]).then_inc(ed_out, 1)
            dve.wait_ge(ed_out, 1)
            ntr = [0]

            def turn(dst, b0=0):
                ntr[0] += 1
                dve.wait_ge(tr_mm, ntr[0])
                for j in range(KD):
                    mark(v.tensor_copy(dst[:, j, 0:4 * TP], ps[:, b0 + j, 0:4 * TP]))
                v.tensor_copy(dst[:, :, 4 * TP:N], ps[:, b0 + 2, 0:KD * TP].rearrange("p (c n) -> p c n", c=KD)
                              ).then_inc(tr_copied, 1)

            nsq = [0]

            def root(out, var, eps):
                done(v.tensor_scalar(out, var, eps, None, ALU.add))
                v.reciprocal(out, out).then_inc(var_ready, 1)
                nsq[0] += 1
                dve.wait_ge(rstd_ready, nsq[0])

            nnorm = [0]

            def layernorm(dst, src, last=True):
                for t in range(NT):
                    mark(v.bn_stats(stats[:, t, :], src[:, t, :]))
                step.wait()
                for t in range(NT):
                    mark(v.bn_aggr(mv[:, t, :], stats[:, t, :]))
                step.wait()
                root(rstd[:, :], mv[:, :, 1:2].rearrange("p t o -> p (t o)"), EPS)
                for t in range(NT):
                    m = v.tensor_scalar(dst[:, t, :], src[:, t, :], mv[:, t, 0:1], rstd[:, t:t + 1],
                                        ALU.subtract, ALU.mult)
                    if t < NT - 1 or not last:
                        mark(m)
                if last:
                    m.then_inc(norm_ready, 1)
                    nnorm[0] += 1
                    dve.wait_ge(norm_ready, nnorm[0])
                else:
                    step.wait()

            def affine(dst, g, b, t):
                done(tt(dst[:, t, :], dst[:, t, :], row(g), ALU.mult))
                return tt(dst[:, t, :], dst[:, t, :], row(b), ALU.add)

            dve.wait_ge(ld_x, 16)
            layernorm(xn, x)
            dve.wait_ge(ld_w, 16 * n_w)
            for r in range(R0):
                for b in range(NB0):
                    c = comp[:, r * NB0 + b:r * NB0 + b + 1]
                    if b == 0:
                        m = v.tensor_scalar(wrel[:, :, r, :], basis[:, b, :, :], c, None, ALU.mult)
                    else:
                        m = v.scalar_tensor_tensor(out=wrel[:, :, r, :], in0=basis[:, b, :, :], scalar=c,
                                                   in1=wrel[:, :, r, :], op0=ALU.mult, op1=ALU.add)
                    if r == R0 - 1 and b == NB0 - 1:
                        m.then_inc(wrel_ready, 1)
                    else:
                        done(m)
            turn(xnT)

            def edge_pass(base, with_sums, windows):
                wn, dn = (WIN, dstw) if windows else (N, dstf)
                with dve.Fori(0, EC // GRING) as i:
                    for u in range(GRING):
                        dve.wait_ge(e_used, i * GRING + (base + u + 1))
                        at_ = bass.ds(i * GRING + u, 1)
                        m = v.tensor_scalar(ohs[:, u % 3, :], iota_f[0:EP, :], srcf[:, at_], None, ALU.is_equal)
                        if with_sums:
                            v.tensor_scalar(ohf[:, u % 3, 0:wn], iota_f[0:EP, 0:wn], dn[:, at_], None,
                                            ALU.is_equal)
                        v.tensor_scalar(ohd[:, u % 3, 0:wn], iota_f[0:EP, 0:wn], dn[:, at_], None,
                                        ALU.is_equal).then_inc(e_oh, 1)

            def join(dst, bank, parts):
                mark(v.tensor_copy(dst[:, 0:512], ps[0:parts, bank, 0:512]))
                mark(v.tensor_copy(dst[:, 512:N], ps[0:parts, bank + 1, GAP:GAP + N - 512]))
                step.wait()
                return tt(dst[:, SEAM:512], dst[:, SEAM:512], ps[0:parts, bank + 1, 0:GAP], ALU.add)

            def keep_adj(tiles, pair0):
                for k, s in enumerate(tiles):
                    done(join(adjT[:, s, :], 2 * (pair0 + k), TP))
                    tt(adjT[:, s, s * TP:(s + 1) * TP], adjT[:, s, s * TP:(s + 1) * TP], ident[0:TP, 0:TP],
                       ALU.add).then_inc(adj_ready, 1)

            spread = dve.value_load(wide[0:1, 0:1], min_val=0, max_val=E)
            with dve.If(spread > 0):
                edge_pass(0, True, False)
                dve.nop()
            with dve.Else():
                edge_pass(0, True, True)
                dve.nop()
            dve.wait_ge(e_used, EC + 3)
            mark(join(xT2[:, 0, 0:N], 0, 128))
            join(xT2[:, 1, 0:N], 2, 128).then_inc(sums_out, 1)
            keep_adj((0, 1), 2)
            dve.wait_ge(adj_mm, 1)
            done(tt(x[:, 0:4, :], x[:, 0:4, :], ps[0:TP, 0:2, :].rearrange("p b (t d) -> p (b t) d", t=2),
                    ALU.add))
            done(tt(x[:, 4, :], x[:, 4, :], ps[0:TP, 2, 0:D], ALU.add))
            tt(x[:, :, :], x[:, :, :], row("gbias").unsqueeze(1).to_broadcast([TP, NT, D]), ALU.add
               ).then_inc(sums_out, 1)
            with dve.If(spread > 0):
                edge_pass(EC, False, False)
                dve.nop()
            with dve.Else():
                edge_pass(EC, False, True)
                dve.nop()
            dve.wait_ge(e_used, 2 * EC + 3)
            keep_adj((2, 3, 4), 0)
            dve.wait_ge(xs_zero, 16 * 4)
            dve.wait_ge(p_mm, 1)
            done(v.tensor_copy(deg[:, :], ps[0:TP, 6, 0:NT]))
            done(v.tensor_scalar(cnt[:, :], deg[:, :], 1.0, None, ALU.subtract))
            done(v.tensor_scalar(nt2[:, :], cnt[:, :], float(EC), None, ALU.is_gt))
            done(v.tensor_reduce(over[:, :], nt2[:, :], AX.X, ALU.add))
            tt(unsorted[:, :], unsorted[:, :], over[:, :], ALU.add).then_inc(p_out, 1)
            dve.wait_ge(p_mm, 2)
            mark(v.tensor_copy(first[:, :], ps[0:TP, 6, 0:NT]))
            mark(v.tensor_copy(loose[:, :], ps[0:1, 7, 0:1]))
            mark(v.tensor_scalar(bound[:, :], iota_f[0:TP, 0:TP], float(EC), None, ALU.mult))
            mark(v.tensor_scalar(miss[:, 0, :], cnt[:, :], 0.0, -BIG, ALU.is_equal, ALU.mult))
            step.wait()
            done(tt(nt2[:, :], first[:, :], cnt[:, :], ALU.add))
            done(v.tensor_scalar(nt2[:, :], nt2[:, :], -1.0, 0.0, ALU.add, ALU.max))
            mark(v.tensor_copy(ends[:, 0, :], nt2[:, :]))
            done(tt(below[:, :, :], bound[:, :].unsqueeze(1).to_broadcast([TP, NT, TP]),
                    nt2[:, :].unsqueeze(2).to_broadcast([TP, NT, TP]), ALU.is_le))
            done(v.tensor_reduce(nt2[:, :], below[:, :, :], AX.X, ALU.add))
            done(v.tensor_scalar(nt2[:, :], nt2[:, :], float(EC), float(EC + 1), ALU.mult, ALU.subtract))
            done(tt(miss[:, 1, :], first[:, :], nt2[:, :], ALU.is_gt))
            mark(v.tensor_scalar(miss[:, 1, :], miss[:, 1, :], -BIG, None, ALU.mult))
            done(v.tensor_scalar(nt2[:, :], nt2[:, :], 0.0, None, ALU.max))
            v.tensor_copy(ends[:, 1, :], nt2[:, :]).then_inc(p_out, 1)
            dve.wait_ge(p_out, 2)

            ntr[0] += 1
            dve.wait_ge(tr_mm, ntr[0])
            mark(v.tensor_copy(vecs[:, :], ps[:, 0, 0:NVEC]))
            v.tensor_copy(b1cols[:, :], ps[:, 1, 0:256]).then_inc(tr_copied, 1)

            mark(v.memset(vext[:, :, :, 128:129], 1.0))
            dve.wait_ge(h_copied, 4 * NT)
            for j in range(KD):
                dve.wait_ge(m_mm, j + 1)
                src = ps[:, 2 * j:2 * j + 2, 0:HN]
                bq = vecs[:, VCOL["bq"] + j:VCOL["bq"] + j + 1]
                tf = (tmpf, tmpg)[j][:, :].rearrange("p (b n) -> p b n", b=2)
                v.tensor_scalar(tf, src, bq, 0.0, ALU.add, ALU.min).then_inc(m_pre, 1)
                mark(v.tensor_scalar(qphi[:, j, :].rearrange("p (b n) -> p b n", b=2), src, bq, 0.0, ALU.add,
                                     ALU.max))
                step.wait()
                dve.wait_ge(m_exp, j + 1)
                tt(qphi[:, j, :], qphi[:, j, :], (tmpf, tmpg)[j][:, :], ALU.add).then_inc(m_out, 1)
            for t in range(NT):
                dve.wait_ge(m_mm, 3 + t)
                bank = 4 * (1 - t % 2)
                done(tt(kphi[:, t, :], ps[0:TP, bank, 0:D], row("bk"), ALU.add))
                e_ = tmpr[:, (t % 2) * D:(t % 2 + 1) * D]
                v.tensor_scalar(e_, kphi[:, t, :], 0.0, None, ALU.min).then_inc(m_pre, 1)
                mark(tt(vext[:, t, :, 0:128], ps[0:TP, bank, D:2 * D].rearrange("p (c n) -> p c n", c=KD),
                        row("bv").rearrange("p (c n) -> p c n", c=KD), ALU.add))
                dve.wait_ge(m_exp, 3 + t)
                v.scalar_tensor_tensor(out=kphi[:, t, :], in0=kphi[:, t, :], scalar=0.0, in1=e_, op0=ALU.max,
                                       op1=ALU.add).then_inc(m_out, 1)
            dve.wait_ge(m_mm, 8)
            for j in range(KD):
                mark(tt(kvbd[:, j, :], ps[:, j, 0:128], headmask[:, :], ALU.mult))
                mark(v.tensor_copy(scr[:, j:j + 1], ps[:, j, 128:129]))
                step.wait()
                m = v.tensor_scalar(ksbd[:, j, :], headmask[:, :], scr[:, j:j + 1], None, ALU.mult)
                if j == KD - 1:
                    m.then_inc(m_out, 1)
                else:
                    mark(m)
            for j in range(KD):
                dve.wait_ge(m_mm, 9 + j)
                t3 = tmpf[:, :].rearrange("p (b n) -> p b n", b=2)
                done(v.tensor_scalar(t3, ps[:, 2:4, 0:HN], 1e-6, None, ALU.add))
                done(v.reciprocal(tmpf[:, :], tmpf[:, :]))
                tt(xT2[:, j, :].rearrange("p (b n) -> p b n", b=2), ps[:, 0:2, 0:HN], t3,
                   ALU.mult).then_inc(m_out, 1)
                dve.wait_ge(m_out, 9 + j)
            for t in range(NT):
                dve.wait_ge(m_mm, 11 + t)
                done(tt(ya[:, t, :], ps[0:TP, t % 2, 0:D], row("bo"), ALU.add))
                tt(ya[:, t, :], ya[:, t, :], xn[:, t, :], ALU.add).then_inc(m_out, 1)
            dve.wait_ge(m_out, 15)
            layernorm(ya, ya, last=False)
            for t in range(NT):
                m = affine(ya, "ln1_g", "ln1_b", t)
                if t < NT - 1:
                    mark(m)
                else:
                    m.then_inc(norm_ready, 1)
            nnorm[0] += 1
            dve.wait_ge(norm_ready, nnorm[0])
            turn(xT2)
            for t in range(NT):
                dve.wait_ge(m_mm, 24 + t)
                done(tt(yb[:, t, :], ps[0:TP, t % 2, 0:D], row("b2"), ALU.add))
                tt(yb[:, t, :], yb[:, t, :], ya[:, t, :], ALU.add).then_inc(m_out, 1)
            dve.wait_ge(m_out, 20)
            layernorm(yb, yb, last=False)
            for t in range(NT):
                done(affine(yb, "ln2_g", "ln2_b", t))

            for t in range(NT):
                done(tt(x[:, t, :], x[:, t, :], yb[:, t, :], ALU.add))

            moe = dict(y=0, r=0, x=0, g=0)

            def router(ne, rb, keep=False):
                r0 = moe["r"]
                dve.wait_ge(r_mm, r0 + 1)
                step.done(tt(lg[:, :, 0:ne], ps[0:TP, 6, 0:NT * ne].rearrange("p (t e) -> p t e", t=NT),
                             rb[0:TP, :].unsqueeze(1).to_broadcast([TP, NT, ne]), ALU.add))
                for k in range(2):
                    cur = (lg, lg2)[k]
                    for t in range(NT):
                        mark(v.max(m8[:, t, :], cur[:, t, 0:ne]))
                    step.wait()
                    for t in range(NT):
                        mark(v.max_index(i8[:, t, :], m8[:, t, :], cur[:, t, 0:ne]))
                    step.wait()
                    done(v.tensor_copy(i8f[:, :, k:k + 1], i8[:, :, 0:1]))
                    mark(v.tensor_copy(gate[:, :, 2 * k:2 * k + 1], m8[:, :, 0:1]))
                    for t in range(NT):
                        mark(v.tensor_scalar((comb, lg2)[k][:, t, 0:ne], iota_f[0:TP, 0:ne],
                                             i8f[:, t, k:k + 1], None, ALU.is_equal))
                    step.wait()
                    if k == 0:
                        done(v.scalar_tensor_tensor(out=lg2[:, :, 0:ne], in0=comb[:, :, 0:ne], scalar=-3e38,
                                                    in1=lg[:, :, 0:ne], op0=ALU.mult, op1=ALU.add))
                if keep:
                    mark(v.tensor_copy(sel[:, 0], comb[:, :, 0:ne]))
                    mark(v.tensor_copy(sel[:, 1], lg2[:, :, 0:ne]))
                tt(gate[:, :, 0:1], gate[:, :, 2:3], gate[:, :, 0:1], ALU.subtract).then_inc(r_pre, 1)
                moe["g"] += 1
                dve.wait_ge(r_exp, moe["g"])
                done(v.tensor_scalar(gate[:, :, 2:3], gate[:, :, 1:2], 1.0, None, ALU.add))
                done(v.reciprocal(gate[:, :, 2:3], gate[:, :, 2:3]))
                done(tt(gate[:, :, 3:4], gate[:, :, 1:2], gate[:, :, 2:3], ALU.mult))
                done(tt(comb[:, :, 0:ne], comb[:, :, 0:ne], gate[:, :, 2:3].to_broadcast([TP, NT, ne]), ALU.mult))
                done(tt(lg2[:, :, 0:ne], lg2[:, :, 0:ne], gate[:, :, 3:4].to_broadcast([TP, NT, ne]), ALU.mult))
                tt(comb[:, :, 0:ne], comb[:, :, 0:ne], lg2[:, :, 0:ne], ALU.add).then_inc(r_out, 1)
                dve.wait_ge(r_out, r0 + 1)
                dve.wait_ge(r_mm, r0 + 2)
                mark(v.tensor_copy(combT[0:ne, 0:4 * TP], ps[0:ne, 6, 0:4 * TP]))
                v.tensor_copy(combT[0:ne, 4 * TP:N], ps[0:ne, 7, 0:TP]).then_inc(r_out, 1)
                moe["r"] = r0 + 2
                y0 = moe["y"]
                for t in range(NT):
                    dve.wait_ge(moe_y, y0 + t + 1)
                    tt(x[:, t, :], x[:, t, :], ps[0:TP, 4 + t % 2, 0:D], ALU.add).then_inc(moe_acc, 1)
                moe["y"] = y0 + NT
                dve.wait_ge(moe_acc, y0 + NT)

            def dense(ne, per_expert_x):
                y0 = moe["y"]

                def scaled(i, u):
                    for j in range(KD):
                        c = i * 4 + (VCOL["eg"] + 2 * u + j), i * 4 + (VCOL["eb"] + 2 * u + j)
                        m = v.tensor_scalar(qphi[:, j, :], xnT[:, j, :], vecs[:, bass.ds(c[0], 1)],
                                            vecs[:, bass.ds(c[1], 1)], ALU.mult, ALU.add)
                    m.then_inc(moe_x, 1)

                with dve.Fori(0, ne // 2) as i:
                    step.enter(i, 0)
                    for u in range(2):
                        if per_expert_x:
                            dve.wait_ge(moe_acc, i * (2 * NT) + (y0 + u * NT))
                            scaled(i, u)
                        for t in range(NT):
                            dve.wait_ge(moe_y, i * (2 * NT) + (y0 + u * NT + t + 1))
                            dve.wait_ge(moe_acc, i * (2 * NT) + (y0 + u * NT + t - (NT - 1)))
                            v.scalar_tensor_tensor(out=x[:, t, :], in0=ps[0:TP, 4 + (u * NT + t) % 2, 0:D],
                                                   scalar=comb[:, t, bass.ds(i * 2 + u, 1)], in1=x[:, t, :],
                                                   op0=ALU.mult, op1=ALU.add).then_inc(moe_acc, 1)
                    step.leave(ne // 2)
                moe["y"] = y0 + ne * NT
                dve.wait_ge(moe_acc, moe["y"])

            layernorm(ya, x)
            turn(xT2)
            layernorm(xn, ya)
            turn(xnT)
            router(E0, rb0)
            dense(E0, True)

            layernorm(xn, x)
            turn(xnT)
            for t in range(NT):
                dve.wait_ge(c_mm, t + 1)
                mark(v.tensor_copy(bas[:, t, 0:DB], ps[0:TP, t % 2, 0:DB]))
                tt(wgt[:, t, :], ps[0:TP, t % 2, DB:DB + NH * NK], bcomb[0:TP, :], ALU.add).then_inc(c_out, 1)
            dve.wait_ge(c_mm, 6)
            mark(v.tensor_copy(basT[:, 0:HN], ps[:, 2, 0:HN]))
            v.tensor_copy(basT[:, HN:N], ps[:, 3, 0:N - HN]).then_inc(c_out, 1)
            v.reciprocal(dinv[:, :], deg[:, :]).then_inc(var_ready, 1)
            nsq[0] += 1
            dve.wait_ge(rstd_ready, nsq[0])
            for t in range(NT):
                m = v.tensor_scalar(bas[:, t, DB:2 * DB], bas[:, t, 0:DB], dinv[:, t:t + 1], None, ALU.mult)
                if t < NT - 1:
                    mark(m)
            m.then_inc(c_out, 1)
            for t in range(NT):
                dve.wait_ge(c_mm, 7 + t)
                mark(v.tensor_scalar(agg[:, t, 0:DB], ps[0:TP, t % 2, DB:2 * DB], dinv[:, t:t + 1], None,
                                     ALU.mult))
                v.tensor_copy(agg[:, t, DB:2 * DB], ps[0:TP, t % 2, 0:DB]).then_inc(c_out, 1)
            dve.wait_ge(c_out, 12)
            slow = dve.value_load(loose[0:1, 0:1], min_val=0, max_val=E)
            with dve.If(slow > 0):
                for d in range(NT):
                    dve.wait_ge(mask_mm, 1 + d)
                    v.tensor_scalar(maskb[:, d, 0:4 * TP], ps[0:TP, 0, 0:4 * TP], 0.0, -BIG, ALU.is_equal,
                                    ALU.mult).then_inc(mask_out, 1)
                    v.tensor_scalar(maskb[:, d, 4 * TP:N], ps[0:TP, 1, 0:TP], 0.0, -BIG, ALU.is_equal,
                                    ALU.mult).then_inc(mask_out, 1)
                dve.sem_inc(mx_out, 1)
                for t in range(NT):
                    with dve.Fori(0, TP // 5) as i:
                        for u in range(5):
                            n = t * TP + u
                            dve.wait_ge(mx_mm, i * 5 + (n + 1))
                            dve.wait_ge(mx_out, i * 5 + (n + 1))
                            v.memset(held[:, :], 0.0)
                            b0 = 0 if u in (0, 2) else 2 if u in (1, 3) else 4
                            src = ps[:, b0:b0 + 2, :].rearrange("p b n -> p (b n)")[:, 0:N]
                            v.tensor_tensor_reduce(out=scr[:, 0:N], in0=src, in1=basT[:, :], scale=1.0,
                                                   scalar=-3e38, op0=ALU.add, op1=ALU.max,
                                                   accum_out=max5[:, u:u + 1]).then_inc(mx_out, 1)
                        dve.wait_ge(mx_out, i * 5 + (t * TP + 6))
                        v.tensor_copy(aggmT[:, bass.ds(i * 5 + t * TP, 5)], max5[:, :]).then_inc(mx_kept, 1)
                        dve.wait_ge(mx_kept, i + (t * TP // 5 + 1))
                dve.wait_ge(mx_turned, 1)
                mark_free(v.tensor_copy(agg[:, 0:4, 2 * DB:3 * DB],
                                        ps[0:TP, 0, :].rearrange("p (t d) -> p t d", t=4)))
                mark_free(v.tensor_copy(agg[:, 4, 2 * DB:3 * DB], ps[0:TP, 1, 0:DB]))
                dve.wait_ge(mx_agg, 2)
                dve.nop()
            with dve.Else():
                def chunk_max(c, slot, before, k):
                    mk = bass.ds(k[0] * 30 + k[1], 1) if isinstance(k, tuple) else slice(k, k + 1)
                    m = v.scalar_tensor_tensor(out=run[:, slot, :], in0=run[:, before, :], scalar=apart[:, mk],
                                               in1=run[:, slot, :], op0=ALU.add, op1=ALU.max)
                    m.then_inc(run_step, 1)
                    dve.wait_ge(run_step, k[0] * 30 + k[1] if isinstance(k, tuple) else k)
                    return m

                def group(g, i=None):
                    half = g % 2
                    dve.wait_ge(run_loaded[half], 16 * GRING * (g // 2 + 1) if i is None
                                else (i + 1) * (16 * GRING))
                    for u in range(GRING):
                        slot = half * GRING + u
                        if i is None and g == 0 and u == 0:
                            continue
                        k = g * GRING + u if i is None else (i, half * GRING + u)
                        chunk_max(None, slot, (slot - 1) % (2 * GRING), k)
                        if u == 0:
                            v.memset(held[:, :], 0.0).then_inc(run_head, 1)
                    v.memset(held[:, :], 0.0).then_inc(run_done, 1)

                group(0)
                group(1)
                with dve.Fori(1, 5) as i:
                    group(0, i)
                    group(1, i)
                group(10)
                dve.wait_ge(ends_got, 160)
                got = [kphi[:, :, k * DB:(k + 1) * DB] for k in range(2)]
                for k in range(2):
                    mark_free(tt(got[k], got[k], miss[:, k, :].unsqueeze(2).to_broadcast([TP, NT, DB]), ALU.add))
                dve.wait_ge(mx_agg, 2)
                mark_free(tt(got[0], got[0], got[1], ALU.max))
                dve.wait_ge(mx_agg, 3)
                mark_free(tt(agg[:, :, 2 * DB:3 * DB], got[0], bas[:, :, 0:DB], ALU.max))
                dve.wait_ge(mx_agg, 4)
                dve.nop()
            ya4 = ya[:, :, :].rearrange("p t (h f) -> p t h f", h=NH)
            pr = prod[:, :].rearrange("p (h f) -> p h f", h=NH)
            for t in range(NT):
                for k in range(NK):
                    w = wgt[:, t, :].rearrange("p (h k) -> p h k", h=NH)[:, :, k:k + 1].to_broadcast(
                        [TP, NH, FH])
                    g = agg[:, t, k * FH:(k + 1) * FH].unsqueeze(1).to_broadcast([TP, NH, FH])
                    if k == 0:
                        done(tt(ya4[:, t], w, g, ALU.mult))
                        done(tt(ya[:, t, :], ya[:, t, :], row("cbias"), ALU.add))
                    else:
                        done(tt(pr, w, g, ALU.mult))
                        m = tt(ya[:, t, :], ya[:, t, :], prod[:, :], ALU.add)
                        if t == NT - 1 and k == NK - 1:
                            m.then_inc(c_out, 2)
                            dve.wait_ge(c_out, 14)
                        else:
                            done(m)
            dve.wait_ge(c_mm, 12)
            done(v.scalar_tensor_tensor(out=gmean[:, :], in0=ps[:, 2, 0:D], scalar=1.0 / N,
                                        in1=row("gnms", 128), op0=ALU.mult, op1=ALU.mult))
            for t in range(NT):
                mark(tt(ya[:, t, :], ya[:, t, :], gmean[0:TP, :], ALU.subtract))
            step.wait()
            dve.wait_ge(btab_stored, 16)
            for t in range(NT):
                m = tt(yb[:, t, :], ya[:, t, :], ya[:, t, :], ALU.mult)
                if t < NT - 1:
                    mark(m)
            m.then_inc(c_out, 2)
            dve.wait_ge(c_mm, 13)
            done(v.tensor_scalar(gmean[:, :], ps[:, 3, 0:D], 1.0 / N, EPS, ALU.mult, ALU.add))
            v.reciprocal(gmean[:, :], gmean[:, :]).then_inc(var_ready, 1)
            nsq[0] += 1
            dve.wait_ge(rstd_ready, nsq[0])
            done(tt(gmean[:, :], gmean[:, :], row("gnw", 128), ALU.mult))
            for t in range(NT):
                done(tt(ya[:, t, :], ya[:, t, :], gmean[0:TP, :], ALU.mult))
                done(tt(ya[:, t, :], ya[:, t, :], row("gnb"), ALU.add))
                m = v.scalar_tensor_tensor(out=x[:, t, :], in0=ya[:, t, :], scalar=0.0, in1=x[:, t, :],
                                           op0=ALU.max, op1=ALU.add)
                if t < NT - 1:
                    done(m)
            m.then_inc(c_out, 1)
            dve.wait_ge(c_out, 17)

            for j in range(KD):
                dve.wait_ge(l_mm, j + 1)
                c = VCOL["bqk"] + j
                v.tensor_scalar(qphi[:, j, :].rearrange("p (b n) -> p b n", b=2), ps[:, 2 * j:2 * j + 2, 0:HN],
                                vecs[:, c:c + 1], None, ALU.add).then_inc(l_out, 1)
            for j in range(KD):
                dve.wait_ge(l_mm, 3 + j)
                c = VCOL["bqk"] + 2 + j
                done(v.tensor_scalar(big[:, j, :].rearrange("p (b n) -> p b n", b=2),
                                     ps[:, 2 * j:2 * j + 2, 0:HN], vecs[:, c:c + 1], None, ALU.add))
                v.tensor_reduce(kmax[:, j:j + 1], big[:, j, 0:N], AX.X, ALU.max, negate=True
                                ).then_inc(l_pre, 1)
                dve.wait_ge(l_exp, j + 1)
                v.reciprocal(ksum[:, j:j + 1], ksum[:, j:j + 1]).then_inc(l_out, 1)
            for t in range(NT):
                dve.wait_ge(l_mm, 5 + t)
                tt(kphi[:, t, :], ps[0:TP, 4 + t % 2, 0:D], row("lbv"), ALU.add).then_inc(l_out, 1)
            dve.wait_ge(l_mm, 10)
            mark(v.tensor_copy(smx[:, 0:4, :], ps[0:TP, 0:2, :].rearrange("p b (t d) -> p (b t) d", t=2)))
            v.tensor_copy(smx[:, 4, :], ps[0:TP, 2, 0:D]).then_inc(l_out, 1)
            dve.wait_ge(l_mm, 11)
            for j in range(KD):
                mark(v.tensor_scalar(lam[:, j, :], ps[:, j, 0:D], ksum[:, j:j + 1], None, ALU.mult))
            step.wait()
            for j in range(KD):
                mark(v.bn_stats(lst[:, j, :], lam[:, j, :]))
            step.wait()
            for j in range(KD):
                mark(v.bn_aggr(lmv[:, j, :], lst[:, j, :]))
            step.wait()
            root(lrs[:, :], lmv[:, :, 1:2].rearrange("p t o -> p (t o)"), EPS)
            done(tt(lrs[:, :], lrs[:, :], vecs[:, VCOL["gamma"]:VCOL["gamma"] + KD], ALU.mult))
            for j in range(KD):
                done(v.tensor_scalar(lam[:, j, :], lam[:, j, :], lmv[:, j, 0:1], lrs[:, j:j + 1], ALU.subtract,
                                     ALU.mult))
                m = v.tensor_scalar(lam[:, j, :], lam[:, j, :], vecs[:, VCOL["beta"] + j:VCOL["beta"] + j + 1],
                                    None, ALU.add)
                if j < KD - 1:
                    mark(m)
            m.then_inc(l_out, 1)
            for t in range(NT):
                dve.wait_ge(l_mm, 12 + t)
                tt(x[:, t, :], x[:, t, :], ps[0:TP, 4 + t % 2, 0:D], ALU.add).then_inc(l_out, 1)
            dve.wait_ge(l_out, 16)
            layernorm(xn, x)
            turn(xnT)
            router(E1, rb1, keep=True)
            tt(lg[:, :, :], sel[:, 0], sel[:, 1], ALU.add).then_inc(r_out, 1)
            dve.wait_ge(r_out, moe["r"] + 1)
            dve.wait_ge(r_mm, moe["r"] + 1)
            pos = ps[0:TP, 6, 0:NT * E1].rearrange("p (t e) -> p t e", t=NT)
            for k in range(2):
                done(tt(lg2[:, :, :], sel[:, k], pos, ALU.mult))
                done(v.tensor_reduce(slotf[:, :, k:k + 1], lg2[:, :, :], AX.X, ALU.add))
            done(v.tensor_reduce(over[:, :], ps[0:TP, 7, 0:E1], AX.X, ALU.max))
            mark(v.tensor_scalar(overi[:, :], over[:, :], float(CAP), None, ALU.is_gt))
            done(v.tensor_scalar(fits[:, :, :], slotf[:, :, :], float(CAP), None, ALU.is_lt))
            done(v.tensor_scalar(slotf[:, :, :], slotf[:, :, :], float(CAP - 1), None, ALU.min))
            done(v.scalar_tensor_tensor(out=rowf[:, :, :], in0=i8f[:, :, 0:2], scalar=float(CAP),
                                        in1=slotf[:, :, :], op0=ALU.mult, op1=ALU.add))
            for k in range(2):
                mark(v.tensor_copy(get[:, k, :], rowf[:, :, k]))
                done(v.tensor_scalar(slotf[:, :, k], nodeid[:, :], float(SPARE + k * N), None, ALU.add))
                done(tt(rowf[:, :, k], rowf[:, :, k], slotf[:, :, k], ALU.subtract))
                done(tt(rowf[:, :, k], rowf[:, :, k], fits[:, :, k], ALU.mult))
                done(tt(rowf[:, :, k], rowf[:, :, k], slotf[:, :, k], ALU.add))
                m = v.tensor_copy(put[:, k, :], rowf[:, :, k])
                if k:
                    m.then_inc(put_ready, 1)
                else:
                    mark(m)
            done(tt(gate[:, :, 2:4], gate[:, :, 2:4], fits[:, :, :], ALU.mult))
            for k in range(2):
                done(tt(lg2[:, :, :], sel[:, k], gate[:, :, 2 + k:3 + k].to_broadcast([TP, NT, E1]), ALU.mult))
                done(tt(comb[:, :, :], comb[:, :, :], lg2[:, :, :], ALU.subtract))

            def keep_rows(s, c):
                dve.wait_ge(s_xT, at(s, c, 1))
                if c >= 2:
                    dve.wait_ge(s_h, at(s, c, -1))
                v.tensor_copy(xeT[:, c % 2].rearrange("p c n -> p (c n)"), ps[:, c % 2, 0:KD * CAP]
                              ).then_inc(s_xT_out, 1)

            def rectify(s, c):
                dve.wait_ge(s_hT, at(s, c, 1))
                if c >= 2:
                    dve.wait_ge(s_y, at(s, c, -1))
                b = s * 4 if isinstance(s, int) else s[0] * 16 + 4 * c
                done(tt(hact[:, c % 2], ps[:, 4 + c % 2, 0:4 * CAP].rearrange("p (c n) -> p c n", c=4),
                        b1cols[:, bass.ds(b, 4)].unsqueeze(2).to_broadcast([128, 4, CAP]), ALU.add))
                v.tensor_scalar(hact[:, c % 2], hact[:, c % 2], 0.0, None, ALU.max).then_inc(s_hT_out, 1)

            def dve_step(s, c):
                if c >= 1:
                    rectify(back(s), c - 1)
                keep_rows(ahead(s), c + 1)

            keep_rows(0, 0)
            for s in range(3):
                dve_step(s, s)
            with dve.Fori(0, (E1 - 4) // 4) as i:
                step.enter(i, 4)
                for c in range(3, 7):
                    dve_step((i,), c)
                step.leave((E1 - 4) // 4)
            rectify(E1 - 2, E1 - 2)
            rectify(E1 - 1, E1 - 1)
            dve.wait_ge(y_got, 160)
            for t in range(NT):
                done(v.scalar_tensor_tensor(out=x[:, t, :], in0=ya[:, t, :], scalar=gate[:, t, 2:3],
                                            in1=x[:, t, :], op0=ALU.mult, op1=ALU.add))
                m = v.scalar_tensor_tensor(out=x[:, t, :], in0=yb[:, t, :], scalar=gate[:, t, 3:4],
                                           in1=x[:, t, :], op0=ALU.mult, op1=ALU.add)
                if t < NT - 1:
                    mark(m)
            m.then_inc(sparse_done, 1)
            dve.wait_ge(sparse_done, 1)
            crowded = dve.value_load(overi[0:1, 0:1], min_val=0, max_val=1)
            with dve.If(crowded > 0):
                dense(E1, False)
            with dve.Else():
                dve.nop()
            v.memset(scr[:, 0:1], 0.0).then_inc(o_ready, NT)


_INS = ["x", "src", "dst", "edge_type_8", "L0_gnn_basis", "L0_gnn_comp", "L0_gnn_loop_weight",
        "L0_gnn_bias_param", "L0_mix_Wq", "L0_mix_bq", "L0_mix_Wk", "L0_mix_bk", "L0_mix_Wv", "L0_mix_bv",
        "L0_mix_Wo", "L0_mix_bo", "L0_mix_W1", "L0_mix_b1", "L0_mix_W2", "L0_mix_b2", "L0_mix_ln1_g",
        "L0_mix_ln1_b", "L0_mix_ln2_g", "L0_mix_ln2_b", "L0_ffn_Wr", "L0_ffn_br", "L0_ffn_ln_g", "L0_ffn_ln_b",
        "L0_ffn_W1", "L0_ffn_b1", "L0_ffn_W2", "L0_ffn_b2", "L1_gnn_W_bases", "L1_gnn_W_comb",
        "L1_gnn_b_comb", "L1_gnn_conv_bias", "L1_gnn_gn_weight", "L1_gnn_gn_bias", "L1_gnn_gn_mean_scale",
        "L1_mix_W_qk", "L1_mix_b_qk", "L1_mix_W_v", "L1_mix_b_v", "L1_mix_gamma", "L1_mix_beta", "L1_ffn_Wr",
        "L1_ffn_br", "L1_ffn_W1", "L1_ffn_b1", "L1_ffn_W2", "L1_ffn_b2"]


def kernel(**inputs):
    import numpy as _np
    import concourse.bacc as _bacc
    from concourse import mybir as _mybir
    from concourse.bass_utils import run_bass_kernel_spmd as _run

    nc = _bacc.Bacc("TRN2", target_bir_lowering=False, num_devices=1)
    arrays, args = {}, {}
    for name in _INS:
        v = _np.ascontiguousarray(inputs[name])
        arrays[f"in_{name}_dram"] = v
        args[name] = nc.dram_tensor(f"in_{name}_dram", v.shape, _mybir.dt.from_np(v.dtype),
                                    kind="ExternalInput").ap()
    args["out"] = nc.dram_tensor("out_0_dram", (N, D), _mybir.dt.float32, kind="ExternalOutput").ap()
    gps_kernel(nc, args)
    r = _run(nc, [arrays], core_ids=[0])
    return r.results[0]["out_0_dram"]
```

```python
from contextlib import ExitStack

import concourse.bass as bass
from concourse import mybir

F32 = mybir.dt.float32
BF16 = mybir.dt.bfloat16
I32 = mybir.dt.int32
U32 = mybir.dt.uint32
ALU = mybir.AluOpType
ACT = mybir.ActivationFunctionType
AX = mybir.AxisListType

N = 625
TP = 125
NT = N // TP
D = 256
KD = D // 128
NP = N + 1
HN = NP // 2
E = 20625
EP = 125
EC = E // EP
R0 = 8
NB0 = 4
DFF = 1024
E0, H0 = 8, 1024
E1, H1 = 64, 512
DB = 128
NH, NK, FH = 8, 12, 32
CAP = 64
NBLK = E0 + (2 * N - E0) // 128
NFULL = 14
SPARE = E1 * CAP
GRING = 15
EG = EC // GRING
WIN = 128
ROWCH = (128, EC - 128)
BIG = 2.0 ** 120
EPS = 1e-5

VECS = [("bq", 2), ("b1", 8), ("bqk", 4), ("gamma", 2), ("beta", 2), ("eg", 16), ("eb", 16), ("eb1", 64)]
VCOL, _n = {}, 0
for _name, _k in VECS:
    VCOL[_name] = _n
    _n += _k
NVEC = _n
ROWS = ["bk", "bv", "bo", "b2", "ln1_g", "ln1_b", "ln2_g", "ln2_b", "gbias", "cbias", "gnw", "gnb", "gnms", "lbv"]


class Chain:

    def __init__(self, eng, sem):
        self.eng, self.sem, self.n, self.off = eng, sem, 0, None

    def mark(self, ins):
        self.n += 1
        ins.then_inc(self.sem, 1)

    def wait(self):
        self.eng.wait_ge(self.sem, self.n if self.off is None else self.off + self.n)

    def done(self, ins):
        self.mark(ins)
        self.wait()

    def enter(self, i, k):
        self.off, self.k, self.n0 = i * k, k, self.n

    def leave(self, count):
        assert self.n - self.n0 == self.k, (self.n - self.n0, self.k)
        self.n, self.off = self.n0 + self.k * count, None


def gps_kernel(nc, a):
    with ExitStack() as ctx:
        def sb(name, shape, dt=F32):
            return ctx.enter_context(nc.sbuf_tensor(name, shape, dt))

        def sem(name):
            return ctx.enter_context(nc.semaphore(name))

        ps = ctx.enter_context(nc.psum_tensor("ps", [128, 8, 512], F32))
        iota_f = sb("iota_f", [128, N])
        ident = sb("ident", [128, 128])
        identb = sb("identb", [128, 128], BF16)
        headmask = sb("headmask", [128, 128])
        ones = sb("ones", [128, 128])
        zerob = sb("zerob", [128, 512], BF16)
        srcf = sb("srcf", [EP, EC])
        dstf = sb("dstf", [EP, EC])
        dstw = sb("dstw", [EP, EC])
        rowid = sb("rowid", [EP, EC], I32)
        winlow = sb("winlow", [1, EG], I32)
        wide = sb("wide", [1, 1], I32)
        srcs = sb("srcs", [EP, EC], I32)
        apart = sb("apart", [EP, EC])
        unsorted = sb("unsorted", [EP, 1])
        loose = sb("loose", [1, 1], I32)
        cnt = sb("cnt", [TP, NT])
        first = sb("first", [TP, NT])
        ends = sb("ends", [TP, 2, NT], U32)
        miss = sb("miss", [TP, 2, NT])
        nt2 = sb("nt2", [TP, NT])
        vecrows = sb("vecrows", [128, 128])
        vecs = sb("vecs", [128, NVEC])
        rows = sb("rows", [128, len(ROWS), D])
        comp = sb("comp", [128, R0 * NB0])
        rb0 = sb("rb0", [128, E0])
        rb1 = sb("rb1", [128, E1])
        bcomb = sb("bcomb", [128, NH * NK])
        b1rows = sb("b1rows", [128, 2, 128])
        b1cols = sb("b1cols", [128, E1 * 4])
        b2e0 = sb("b2e0", [E0, D])
        b2e1 = sb("b2e1", [E1, D])
        shared = sb("shared", [128, 8192])
        basis = shared[:, 0:NB0 * KD * D].rearrange("p (b c d) -> p b c d", b=NB0, c=KD)
        wrel = shared[:, NB0 * KD * D:(NB0 + R0) * KD * D].rearrange("p (c r d) -> p c r d", c=KD, r=R0)
        wa = shared[:, 0:4096].rearrange("p (s n) -> p s n", s=2)
        wb = shared[:, 4096:8192].rearrange("p (s n) -> p s n", s=2)
        loopw = sb("loopw", [128, KD, D])
        wq = sb("wq", [128, KD, D])
        wkv = sb("wkv", [128, KD, 2 * D])
        wo = sb("wo", [128, KD, D])
        w1 = sb("w1", [128, KD, DFF])
        w2 = sb("w2", [128, DFF // 128, D])
        wr0 = sb("wr0", [128, KD, E0])
        wr1 = sb("wr1", [128, KD, E1])
        wbc = sb("wbc", [128, KD, DB + NH * NK])
        lwq, lwk, lwv = wq, wkv[:, :, 0:D], wkv[:, :, D:2 * D]
        x = sb("x", [TP, NT, D])
        xn = sb("xn", [TP, NT, D])
        xnT = sb("xnT", [128, KD, NP])
        xT2 = sb("xT2", [128, KD, NP])
        ya = sb("ya", [TP, NT, D])
        yb = sb("yb", [TP, NT, D])
        stats = sb("stats", [TP, NT, 6])
        mv = sb("mv", [TP, NT, 2])
        rstd = sb("rstd", [TP, NT])
        adjT = sb("adjT", [TP, NT, N])
        ohf = sb("ohf", [EP, 3, N])
        stage = sb("stage", [TP, 2 * R0 * D])
        hrow = stage[:, :].rearrange("p (s n) -> p s n", s=8)
        maskb = stage[:, :].bitcast(BF16)[:, 0:NT * N].rearrange("p (t n) -> p t n", t=NT)
        gath = stage[:, 0:GRING * D].rearrange("p (s d) -> p s d", s=GRING)
        big = sb("big", [128, 8, NP])
        qphi = sb("qphi", [128, KD, NP])
        kphi = sb("kphi", [TP, NT, D])
        vext = big[0:TP, :, :].rearrange("p a b -> p (a b)")[:, 0:NT * KD * 129].rearrange(
            "p (t c n) -> p t c n", t=NT, c=KD)
        kvbd = sb("kvbd", [128, KD, 128])
        ksbd = sb("ksbd", [128, KD, 128])
        tmpf = sb("tmpf", [128, NP])
        scr = sb("scr", [128, NP])
        tmpg = scr
        tmpr = scr[0:TP, 0:2 * D]
        lg = sb("lg", [TP, NT, E1])
        lg2 = sb("lg2", [TP, NT, E1])
        m8 = sb("m8", [TP, NT, 8])
        i8 = sb("i8", [TP, NT, 8], U32)
        i8f = sb("i8f", [TP, NT, 8])
        gate = sb("gate", [TP, NT, 4])
        comb = sb("comb", [TP, NT, E1])
        combT = sb("combT", [128, N])
        bas = yb
        basT = combT
        wgt = sb("wgt", [TP, NT, NH * NK])
        agg = big[0:TP, :, :].rearrange("p a b -> p (a b)")[:, 0:NT * 3 * DB].rearrange("p (t n) -> p t n", t=NT)
        aggmT = xT2[:, 0, 0:N]
        deg = sb("deg", [TP, NT])
        dinv = sb("dinv", [TP, NT])
        max5 = sb("max5", [128, 5])
        held = sb("held", [128, 1])
        gmean = tmpf[:, 0:D]
        kmax = sb("kmax", [128, KD])
        ksum = sb("ksum", [128, KD])
        lam = tmpf[:, 0:KD * D].rearrange("p (c d) -> p c d", c=KD)
        sel = adjT[:, :, :].rearrange("p t n -> p (t n)")[:, 0:2 * NT * E1].rearrange(
            "p (k t e) -> p k t e", k=2, t=NT)
        tri = sb("tri", [TP, TP])
        nodeid = sb("nodeid", [TP, NT])
        slotf = sb("slotf", [TP, NT, 2])
        fits = sb("fits", [TP, NT, 2])
        put = sb("put", [TP, 2, NT], U32)
        get = sb("get", [TP, 2, NT], U32)
        rowf = sb("rowf", [TP, NT, 2])
        over = sb("over", [TP, 1])
        overi = sb("overi", [TP, 1], I32)
        flat = big[:, :, :].rearrange("p a b -> p (a b)")
        raw = flat[:, 2048:2048 + 6 * EP].bitcast(I32).rearrange("p (w h e) -> p w h e", w=3, h=2)
        crow = flat[:, 2048 + 6 * EP:2048 + 12 * EP].rearrange("p (w h e) -> p w h e", w=3, h=2)
        dpm = flat[0:EP, 3800:3800 + EC].bitcast(I32)
        dnx = flat[0:EP, 3800 + EC:3800 + 2 * EC].bitcast(I32)
        dcmp = flat[0:EP, 3800 + 2 * EC:3800 + 3 * EC]
        span = flat[:, 4400:4404].rearrange("p (h k) -> p h k", h=2)
        glow, ghigh, gover = (flat[0:1, 4410 + k * EG:4410 + (k + 1) * EG] for k in range(3))
        bound = stage[:, 0:TP]
        below = stage[:, TP:TP + NT * TP].rearrange("p (t q) -> p t q", t=NT)
        ohs = kphi[:, :, :].rearrange("p t d -> p (t d)").bitcast(BF16)[:, 0:3 * N].rearrange(
            "p (s n) -> p s n", s=3)
        ohd = qphi[0:EP, :, :].rearrange("p c n -> p (c n)").bitcast(BF16)[:, 0:3 * N].rearrange(
            "p (s n) -> p s n", s=3)
        run = stage[:, 0:2 * GRING * DB].rearrange("p (s d) -> p s d", d=DB)
        fx = flat[:, 0:2 * D].rearrange("p (s d) -> p s d", s=2)
        fy = flat[:, 512:512 + 2 * D].rearrange("p (s d) -> p s d", s=2)
        fxT = flat[:, 1024:1024 + 4 * 128].rearrange("p (s c n) -> p s c n", s=2, c=KD)
        fh = flat[:, 1536:1536 + 16 * 128].rearrange("p (s c n) -> p s c n", s=2, c=8)
        sel0 = flat[0:TP, 3584:3584 + 2 * NT * E0].rearrange("p (k t e) -> p k t e", k=2, t=NT)
        steps5 = flat[0:TP, 3700:3700 + 5 * E0].rearrange("p (e k) -> p e k", k=5)
        blocks = flat[0:TP, 3750:3750 + E0]
        blkend = flat[0:TP, 3760:3760 + E0]
        total = flat[0:TP, 3770:3770 + E0]
        ended = flat[0:1, 3780:3780 + NBLK * E0].rearrange("p (b e) -> p b e", e=E0)
        blkf = flat[0:1, 3920:3920 + NBLK]
        blkexp = sb("blkexp", [1, NBLK], I32)
        nblocks = sb("nblocks", [1, 1], I32)
        fw1 = shared[:, 0:4096].rearrange("p (s c h) -> p s c h", s=2, c=KD)
        fw2 = shared[:, 4096:8192].rearrange("p (s c d) -> p s c d", s=2, c=8)
        zerof = flat[:, 0:SPARE // 512 * D]
        xe = flat[0:CAP, 0:1024].rearrange("p (s d) -> p s d", s=4)
        ye = flat[0:CAP, 1024:2048].rearrange("p (s d) -> p s d", s=4)
        hact = flat[:, 3072:3072 + 8 * CAP].rearrange("p (s c n) -> p s c n", s=2, c=4)
        xeT = flat[:, 3584:3584 + 4 * CAP].rearrange("p (s c n) -> p s c n", s=2, c=2)
        ew1 = shared[:, 0:4096].rearrange("p (s c h) -> p s c h", s=4, c=KD)
        ew2 = shared[:, 4096:8192].rearrange("p (s c d) -> p s c d", s=4, c=4)
        carry = ohf[:, :, :].rearrange("p s n -> p (s n)")[:, NT * D:NT * D + DB]
        lst = sb("lst", [128, KD, 6])
        lmv = sb("lmv", [128, KD, 2])
        lrs = sb("lrs", [128, KD])
        lval = flat[0:TP, 1920:1920 + NT * D].rearrange("p (t d) -> p t d", t=NT)
        smx = flat[0:TP, 1920 + NT * D:1920 + 2 * NT * D].rearrange("p (t d) -> p t d", t=NT)
        prod = ohf[:, :, :].rearrange("p s n -> p (s n)")[:, 0:NT * D].rearrange("p (t h f) -> p t h f", t=NT, h=NH)

        rtab = nc.dram_tensor("rtab", [E, DB], F32, kind="Internal")
        btab = nc.dram_tensor("btab", [N, DB], F32, kind="Internal")
        xs = nc.dram_tensor("xs", [SPARE + 2 * N, D], F32, kind="Internal")
        fys = nc.dram_tensor("fys", [NBLK * 128, D], F32, kind="Internal")
        ys = nc.dram_tensor("ys", [SPARE, D], F32, kind="Internal")
        msgs = nc.dram_tensor("msgs", [N * R0, D], F32, kind="Internal")

        ld_edges = sem("ld_edges")
        ld_x = sem("ld_x")
        ld_vec = sem("ld_vec")
        ld_basis = sem("ld_basis")
        ld_w, ld_lw = sem("ld_w"), sem("ld_lw")
        consts_ready = sem("consts_ready")
        dchain, achain, pchain = sem("dve_step"), sem("act_step"), sem("pool_step")
        edges_ready, ed_mm, ed_low, ed_out = sem("edges_ready"), sem("ed_mm"), sem("ed_low"), sem("ed_out")
        wide_out = sem("wide_out")
        acc_zero, flushed, slow_step = sem("acc_zero"), sem("flushed"), sem("slow_step")
        e_oh, e_used, sums_out = sem("e_oh"), sem("e_used"), sem("sums_out")
        p_mm, p_out = sem("p_mm"), sem("p_out")
        run_loaded = [sem("run_loaded0"), sem("run_loaded1")]
        run_stored = [sem("run_stored0"), sem("run_stored1")]
        run_done, ends_got = sem("run_done"), sem("ends_got")
        btab_stored, mask_mm, mask_out, mx_turned = (sem("btab_stored"), sem("mask_mm"), sem("mask_out"),
                                                     sem("mx_turned"))
        adj_mm, adj_ready = sem("adj_mm"), sem("adj_ready")
        var_ready, rstd_ready = sem("var_ready"), sem("rstd_ready")
        norm_ready = sem("norm_ready")
        tr_mm, tr_copied = sem("tr_mm"), sem("tr_copied")
        wrel_ready = sem("wrel_ready")
        h_mm, h_copied = sem("h_mm"), sem("h_copied")
        h_stored = [sem(f"h_stored{i}") for i in range(8)]
        gathered = [sem(f"gathered{i}") for i in range(GRING)]
        m_mm, m_out, m_pre, m_exp = sem("m_mm"), sem("m_out"), sem("m_pre"), sem("m_exp")
        m_relu = sem("m_relu")
        moe_w = [sem("moe_w0"), sem("moe_w1")]
        moe_used = sem("moe_used")
        moe_h, moe_act, moe_y, moe_acc = sem("moe_h"), sem("moe_act"), sem("moe_y"), sem("moe_acc")
        run_step, mx_agg = sem("run_step"), sem("mx_agg")
        r_mm, r_out, r_pre, r_exp = sem("r_mm"), sem("r_out"), sem("r_pre"), sem("r_exp")
        c_mm, c_out = sem("c_mm"), sem("c_out")
        mx_mm, mx_out, mx_kept = sem("mx_mm"), sem("mx_out"), sem("mx_kept")
        l_mm, l_out, l_pre, l_exp = sem("l_mm"), sem("l_out"), sem("l_pre"), sem("l_exp")
        blk_ready = sem("blk_ready")
        b_xT, b_xT_out, b_h, b_h_out = sem("b_xT"), sem("b_xT_out"), sem("b_h"), sem("b_h_out")
        b_y, b_y_out = sem("b_y"), sem("b_y_out")
        fx_loaded = [sem("fx_loaded0"), sem("fx_loaded1")]
        fw1_loaded = [sem("fw1_loaded0"), sem("fw1_loaded1")]
        fw2_loaded = [sem("fw2_loaded0"), sem("fw2_loaded1")]
        fy_stored = [sem("fy_stored0"), sem("fy_stored1")]
        xs_zero, put_ready, xs_put = sem("xs_zero"), sem("put_ready"), sem("xs_put")
        xe_loaded = [sem(f"xe_loaded{i}") for i in range(4)]
        ew1_loaded = [sem(f"ew1_loaded{i}") for i in range(4)]
        ew2_loaded = [sem(f"ew2_loaded{i}") for i in range(4)]
        y_stored = [sem(f"y_stored{i}") for i in range(4)]
        s_xT, s_xT_out, s_h, s_h_out = sem("s_xT"), sem("s_xT_out"), sem("s_h"), sem("s_h_out")
        s_y, s_y_out = sem("s_y"), sem("s_y_out")
        y_got, sparse_done = [sem("y_got0"), sem("y_got1")], sem("sparse_done")
        o_ready, o_stored = sem("o_ready"), sem("o_stored")

        def node_major(ap):
            return ap.rearrange("(t p) d -> p t d", p=TP)

        def chunked(ap):
            return ap.rearrange("(c p) d -> p c d", p=128)

        def row(name, parts=TP):
            return rows[0:parts, ROWS.index(name), :]

        def row_ap(ap, parts=128):
            return ap.partition_broadcast(parts)

        n_vec = len(VECS) + 1 + len(ROWS) + 4
        n_w = 12

        def dense_weights(sp, first, w1d, w2d, ne):
            c1, f = KD, w1d.shape[2]
            c2 = f // 128
            w1v = w1d.rearrange("e (c p) h -> e p c h", p=128)
            w2v = w2d.rearrange("e (c p) d -> e p c d", p=128)
            for i, n in ((0, 1), (1, ne // 2 - 1)):
                if i == 0:
                    passes(sp, None, first, w1v, w2v, c1, c2, f)
                else:
                    with sp.Fori(1, ne // 2) as r:
                        passes(sp, r, first, w1v, w2v, c1, c2, f)

        def passes(sp, i, first, w1v, w2v, c1, c2, f):
            for u in range(2):
                e = u if i is None else i * 2 + u
                if i is not None or first:
                    sp.wait_ge(moe_used, first + u - 1 if i is None else i * 2 + (first + u - 1))
                sp.dma_start(wa[:, u, 0:c1 * f].rearrange("p (c h) -> p c h", c=c1),
                             w1v[bass.ds(e, 1)].rearrange("o p c h -> p (o c) h")).then_inc(moe_w[u], 16)
                sp.dma_start(wb[:, u, 0:c2 * D].rearrange("p (c h) -> p c h", c=c2),
                             w2v[bass.ds(e, 1)].rearrange("o p c h -> p (o c) h")).then_inc(moe_w[u], 16)

        def at(s, c, plus):
            return s + plus if isinstance(s, int) else s[0] * 4 + (c + plus)

        def back(s):
            return s - 1 if isinstance(s, int) else s

        def ahead(s):
            return s + 1 if isinstance(s, int) else s

        def no(s, c, plus, per=1):
            return s * per + plus if isinstance(s, int) else s[0] * (2 * per) + (per * c + plus)

        def loads(s, c, plus=1):
            return 16 * (s // 2 + plus) if isinstance(s, int) else (s[0] + (c // 2 + plus)) * 16

        def block_steps(eng, step, b0, b1):
            pairs = max((b1 - b0 - 5) // 2, 0)
            for s in range(b0, b0 + 3):
                step(s, s)
            if pairs:
                with eng.Fori(0, pairs) as i:
                    for c in (3, 4):
                        step((i,), c)
            for s in range(b0 + 3 + 2 * pairs, b1):
                step(s, s)

        def rest_of_blocks(eng, run):
            more = eng.value_load(nblocks[0:1, 0:1], min_val=0, max_val=NBLK)
            with eng.If(more > NFULL):
                run()
            with eng.Else():
                eng.nop()

        def is_last(s):
            return isinstance(s, int) and s in (NFULL - 1, NBLK - 1)

        block = ctx.enter_context(nc.Block())

        @block.sync
        def _(sp):
            sp.dma_start(x[:, :, :], node_major(a["x"])).then_inc(ld_x, 16)
            sp.dma_start(comp[:, :], row_ap(a["L0_gnn_comp"].rearrange("r b -> (r b)"))).then_inc(ld_basis, 16)
            for w, name in enumerate(("src", "dst", "edge_type_8")):
                by_chunk = a[name].rearrange("(c e) -> c e", e=EP)
                sp.dma_start(raw[:, w, 0, :], by_chunk[0:128]).then_inc(ld_edges, 16)
                sp.dma_start(raw[0:ROWCH[1], w, 1, :], by_chunk[128:EC]).then_inc(ld_edges, 16)
            sp.dma_start(srcs[:, :], a["src"].rearrange("(p c) -> p c", p=EP)).then_inc(ld_edges, 16)
            sp.dma_start(dpm, a["dst"].rearrange("(p c) -> p c", p=EP)).then_inc(ld_edges, 16)
            sp.dma_start(dnx[0:EP - 1, :], a["dst"][1:1 + (EP - 1) * EC].rearrange("(p c) -> p c", c=EC)
                         ).then_inc(ld_edges, 16)
            sp.dma_start(dnx[EP - 1:EP, 0:EC - 1], a["dst"][E - EC + 1:E].rearrange("(p c) -> p c", p=1)
                         ).then_inc(ld_edges, 16)
            sp.dma_start(basis[:, :, :, :], a["L0_gnn_basis"].rearrange("b (c p) d -> p b c d", p=128)
                         ).then_inc(ld_basis, 16)
            sp.wait_ge(ld_basis, 32)
            for name, src in (("bq", a["L0_mix_bq"]), ("b1", a["L0_mix_b1"]),
                              ("bqk", a["L1_mix_b_qk"].rearrange("k d -> (k d)")),
                              ("gamma", a["L1_mix_gamma"]), ("beta", a["L1_mix_beta"]),
                              ("eg", a["L0_ffn_ln_g"].rearrange("e d -> (e d)")),
                              ("eb", a["L0_ffn_ln_b"].rearrange("e d -> (e d)")),
                              ("eb1", a["L0_ffn_b1"].rearrange("e d -> (e d)"))):
                v = src.rearrange("(r c) -> r c", c=128)
                sp.dma_start(vecrows[VCOL[name]:VCOL[name] + v.shape[0], :], v).then_inc(ld_vec, 16)
            sp.dma_start(b1rows[:, :, :], a["L1_ffn_b1"].rearrange("e (j c) -> (e j) c", c=128)
                         .rearrange("(h r) c -> r h c", r=128)).then_inc(ld_vec, 16)
            for name, src in zip(ROWS, (a["L0_mix_bk"], a["L0_mix_bv"], a["L0_mix_bo"], a["L0_mix_b2"],
                                        a["L0_mix_ln1_g"], a["L0_mix_ln1_b"], a["L0_mix_ln2_g"],
                                        a["L0_mix_ln2_b"], a["L0_gnn_bias_param"], a["L1_gnn_conv_bias"],
                                        a["L1_gnn_gn_weight"], a["L1_gnn_gn_bias"],
                                        a["L1_gnn_gn_mean_scale"], a["L1_mix_b_v"])):
                sp.dma_start(rows[:, ROWS.index(name), :], row_ap(src)).then_inc(ld_vec, 16)
            sp.dma_start(rb0[:, :], row_ap(a["L0_ffn_br"])).then_inc(ld_vec, 16)
            sp.dma_start(rb1[:, :], row_ap(a["L1_ffn_br"])).then_inc(ld_vec, 16)
            sp.dma_start(bcomb[:, :], row_ap(a["L1_gnn_b_comb"])).then_inc(ld_vec, 16)
            sp.dma_start(b2e0[:, :], a["L0_ffn_b2"]).then_inc(ld_vec, 16)
            n = 0
            for dst, src in ((loopw[:, :, :], chunked(a["L0_gnn_loop_weight"])),
                             (wq[:, :, :], chunked(a["L0_mix_Wq"])),
                             (wkv[:, :, 0:D], chunked(a["L0_mix_Wk"])),
                             (wkv[:, :, D:2 * D], chunked(a["L0_mix_Wv"])),
                             (wo[:, :, :], chunked(a["L0_mix_Wo"])),
                             (w1[:, :, :], chunked(a["L0_mix_W1"])),
                             (w2[:, :, :], chunked(a["L0_mix_W2"])),
                             (wr0[:, :, :], chunked(a["L0_ffn_Wr"])),
                             (wr1[:, :, :], chunked(a["L1_ffn_Wr"])),
                             (wbc[:, :, 0:DB], chunked(a["L1_gnn_W_bases"])),
                             (wbc[:, :, DB:], chunked(a["L1_gnn_W_comb"])),
                             (b2e1[:, :], a["L1_ffn_b2"])):
                sp.dma_start(dst, src).then_inc(ld_w, 16)
                n += 1
            hd = msgs.ap().rearrange("(t p r) d -> t p (r d)", p=TP, r=R0)
            for n in range(4 * NT):
                g, t = n // NT, n % NT
                sp.wait_ge(h_copied, n + 1)
                sp.dma_start(hd[t][:, g * 2 * D:(g + 1) * 2 * D], hrow[:, n % 8, :]).then_inc(h_stored[n % 8], 16)
            sp.wait_ge(m_mm, 7)
            for dst, src in ((lwq, a["L1_mix_W_qk"][0]), (lwk, a["L1_mix_W_qk"][1]), (lwv, a["L1_mix_W_v"])):
                sp.dma_start(dst[:, :, :], chunked(src)).then_inc(ld_lw, 16)
            f1v = a["L0_ffn_W1"].rearrange("e (c p) h -> e p c h", p=128)
            f2v = a["L0_ffn_W2"].rearrange("e (c p) d -> e p c d", p=128)
            sp.wait_ge(m_out, 8)
            sp.wait_ge(blk_ready, 1)

            def block_weights(s, c):
                e = sp.value_load(blkexp[0:1, bass.ds(no(s, c, 0), 1)], min_val=0, max_val=E0 - 1)
                if c >= 2:
                    sp.wait_ge(b_h, no(s, c, -2, 2))
                sp.dma_start(fw1[:, c % 2], f1v[bass.ds(e, 1)].rearrange("o p c h -> p (o c) h")
                             ).then_inc(fw1_loaded[c % 2], 16)
                if c >= 2:
                    sp.wait_ge(b_y, no(s, c, -1))
                sp.dma_start(fw2[:, c % 2], f2v[bass.ds(e, 1)].rearrange("o p c h -> p (o c) h")
                             ).then_inc(fw2_loaded[c % 2], 16)

            block_steps(sp, block_weights, 0, NFULL)
            sp.wait_ge(b_y, NFULL)

            def rest():
                block_steps(sp, block_weights, NFULL, NBLK)
                sp.wait_ge(b_y, NBLK)

            rest_of_blocks(sp, rest)
            w1v = a["L1_ffn_W1"].rearrange("e (c p) h -> e p c h", p=128)
            w2v = a["L1_ffn_W2"].rearrange("e (c p) d -> e p c d", p=128)

            def expert_w1(e, slot):
                sp.dma_start(ew1[:, slot], w1v[bass.ds(e, 1)].rearrange("o p c h -> p (o c) h")
                             ).then_inc(ew1_loaded[slot], 16)

            for q in range(4):
                expert_w1(q, q)
                sp.dma_start(ew2[:, q], w2v[q:q + 1].rearrange("o p c h -> p (o c) h")
                             ).then_inc(ew2_loaded[q], 16)
            sp.wait_ge(p_out, 2)
            slow = sp.value_load(loose[0:1, 0:1], min_val=0, max_val=E)
            with sp.If(slow > 0):
                sp.nop()
            with sp.Else():
                for g in range(EG):
                    sp.wait_ge(run_done, g + 1)
                    sp.dma_start(rtab.ap().rearrange("(p c) d -> p c d", c=EC)[:, g * GRING:(g + 1) * GRING, :],
                                 run[:, (g % 2) * GRING:(g % 2 + 1) * GRING, :]).then_inc(run_stored[g % 2], 16)
                sp.nop()
            with sp.Fori(1, E1 // 4) as i:
                for q in range(4):
                    sp.wait_ge(s_h, i * 4 + (q - 3))
                    expert_w1(i * 4 + q, q)
                    sp.wait_ge(s_y, i * 4 + (q - 3))
                    sp.dma_start(ew2[:, q], w2v[bass.ds(i * 4 + q, 1)].rearrange("o p c h -> p (o c) h")
                                 ).then_inc(ew2_loaded[q], 16)
            sp.wait_ge(sparse_done, 1)
            crowded = sp.value_load(overi[0:1, 0:1], min_val=0, max_val=1)
            with sp.If(crowded > 0):
                dense_weights(sp, 0, a["L1_ffn_W1"], a["L1_ffn_W2"], E1)
            with sp.Else():
                sp.nop()
            sp.wait_ge(o_ready, NT)
            sp.dma_start(node_major(a["out"]), x[:, :, :]).then_inc(o_stored, 16)
            sp.wait_ge(o_stored, 16)

        @block.gpsimd
        def _(pool):
            step = Chain(pool, pchain)
            pool.iota(iota_f[:, :], pattern=[[1, N]], base=0, channel_multiplier=0,
                      allow_small_or_imprecise_dtypes=True).then_inc(consts_ready, 1)
            step.done(pool.memset(ident[:, :], 0.0))
            step.done(pool.affine_select(out=ident[:, :], in_=ident[:, :], compare_op=ALU.not_equal, fill=1.0,
                                         base=0, pattern=[[-1, 128]], channel_multiplier=1))
            pool.tensor_copy(identb[:, :], ident[:, :]).then_inc(consts_ready, 1)
            step.done(pool.memset(headmask[:, :], 0.0))
            for h in range(4):
                step.done(pool.memset(headmask[32 * h:32 * h + 32, 32 * h:32 * h + 32], 1.0))
            step.done(pool.memset(tri[:, :], 1.0))
            step.done(pool.affine_select(out=tri[:, :], in_=tri[:, :], compare_op=ALU.is_gt, fill=0.0, base=0,
                                         pattern=[[1, TP]], channel_multiplier=-1))
            step.done(pool.iota(nodeid[:, :], pattern=[[TP, NT]], base=0, channel_multiplier=1,
                                allow_small_or_imprecise_dtypes=True))
            pool.memset(ones[:, :], 1.0).then_inc(consts_ready, 1)
            pool.memset(adjT[:, :, :], 0.0).then_inc(acc_zero, 1)
            pool.memset(xT2[:, :, 0:N], 0.0).then_inc(acc_zero, 1)
            pool.wait_ge(ed_out, 1)
            for q in range(8):
                pool.wait_ge(h_stored[q], 16 * ((4 * NT - q + 7) // 8))
            for c in range(EC):
                if c >= GRING:
                    pool.wait_ge(e_used, c - GRING + 4)
                pool.indirect_dma_start(gath[:, c % GRING, :], None, msgs.ap(),
                                        bass.IndirectOffsetOnAxis(ap=rowid[:, c:c + 1].bitcast(U32), axis=0)
                                        ).then_inc(gathered[c % GRING], 16)

            def dispatch(n):
                pool.wait_ge(put_ready, n + 1)
                for k in range(2):
                    for t in range(NT):
                        pool.indirect_dma_start(xs.ap(), bass.IndirectOffsetOnAxis(ap=put[:, k, t:t + 1], axis=0),
                                                xn[:, t, :], None).then_inc(xs_put, 16)

            def fetch(results):
                for k in range(2):
                    for t in range(NT):
                        pool.indirect_dma_start((ya, yb)[k][:, t, :], None, results.ap(),
                                                bass.IndirectOffsetOnAxis(ap=get[:, k, t:t + 1], axis=0)
                                                ).then_inc(y_got[k], 16)

            pool.wait_ge(xs_zero, 16 * 5)
            dispatch(0)
            for q in range(2):
                pool.wait_ge(fy_stored[q], 16 * ((NFULL + 1 - q) // 2))

            def rest():
                for q in range(2):
                    pool.wait_ge(fy_stored[q], 16 * ((NBLK + 1 - q) // 2))
                pool.nop()

            rest_of_blocks(pool, rest)
            fetch(fys)

            pool.wait_ge(p_out, 2)
            pool.wait_ge(btab_stored, 16)
            slow = pool.value_load(loose[0:1, 0:1], min_val=0, max_val=E)
            with pool.If(slow > 0):
                pool.nop()
            with pool.Else():
                for g in range(EC // GRING):
                    if g >= 2:
                        pool.wait_ge(run_stored[g % 2], 16 * (g // 2))
                    for u in range(GRING):
                        c = g * GRING + u
                        pool.indirect_dma_start(run[:, (g % 2) * GRING + u, :], None, btab.ap(),
                                                bass.IndirectOffsetOnAxis(ap=srcs[:, c:c + 1].bitcast(U32),
                                                                          axis=0)).then_inc(run_loaded[g % 2], 16)
                pool.wait_ge(run_stored[0], 16 * 6)
                pool.wait_ge(run_stored[1], 16 * 5)
                for k in range(2):
                    for t in range(NT):
                        pool.indirect_dma_start(kphi[:, t, k * DB:(k + 1) * DB], None, rtab.ap(),
                                                bass.IndirectOffsetOnAxis(ap=ends[:, k, t:t + 1], axis=0)
                                                ).then_inc(ends_got, 16)
                pool.nop()
            dispatch(1)
            for q in range(4):
                pool.wait_ge(y_stored[q], 16 * (E1 // 4))
            fetch(ys)

        @block.tensor
        def _(pe):
            pe.wait_ge(consts_ready, 4)

            pe.wait_ge(edges_ready, 1)
            for w in range(3):
                for h, n in enumerate(ROWCH):
                    pe.transpose(ps[0:EP, w // 2, (w % 2) * EC + h * 128:(w % 2) * EC + h * 128 + n],
                                 crow[0:n, w, h, :], ident[0:n, 0:n])
            for h, n in enumerate(ROWCH):
                pe.transpose(ps[0:1, 2, h * 128:h * 128 + n], span[0:n, h, 0:1], ident[0:n, 0:n])
                m = pe.transpose(ps[0:1, 2, 256 + h * 128:256 + h * 128 + n], span[0:n, h, 1:2], ident[0:n, 0:n])
            m.then_inc(ed_mm, 1)
            pe.wait_ge(ed_low, 1)
            pe.matmul(ps[0:EP, 3, 0:EG], ones[0:1, 0:EP], glow, start=True, stop=True).then_inc(ed_mm, 1)
            pe.wait_ge(ed_out, 1)

            ntr = [0]

            def turn(src, ready, count, b0=0):
                pe.wait_ge(ready, count)
                for j in range(KD):
                    for t in range(NT):
                        bk, off = (b0 + j, t * TP) if t < 4 else (b0 + 2, j * TP)
                        m = pe.transpose(ps[:, bk, off:off + TP], src[:, t, j * 128:(j + 1) * 128],
                                         ident[0:TP, 0:TP])
                m.then_inc(tr_mm, 1)
                ntr[0] += 1

            def turned():
                pe.wait_ge(tr_copied, ntr[0])

            turn(xn, norm_ready, 1)
            turned()
            for g in range(4):
                pe.wait_ge(wrel_ready, g + 1)
                for t in range(NT):
                    n = NT * g + t
                    if n >= 4:
                        pe.wait_ge(h_copied, n - 3)
                    for k in range(KD):
                        m = pe.matmul(ps[0:TP, n % 4, :], xnT[:, k, t * TP:(t + 1) * TP],
                                      wrel[:, k, 2 * g:2 * g + 2, :].rearrange("p r d -> p (r d)"),
                                      start=(k == 0), stop=(k == KD - 1))
                    m.then_inc(h_mm, 1)

            pe.wait_ge(h_copied, 4 * NT)
            pe.wait_ge(ld_w, 16 * n_w)
            for t in range(NT):
                for k in range(KD):
                    m = pe.matmul(ps[0:TP, t // 2, (t % 2) * D:(t % 2 + 1) * D], xnT[:, k, t * TP:(t + 1) * TP],
                                  loopw[:, k, :], start=(k == 0), stop=(k == KD - 1))
            m.then_inc(adj_mm, 1)

            def clear(banks, parts):
                for b in banks:
                    pe.matmul(ps[0:parts, b, :], zerob[:, 0:parts], zerob[:, :], start=True, stop=True)

            def narrow_groups():
                with pe.Fori(0, EG) as i:
                    pe.wait_ge(flushed, i * 3 + 3)
                    clear((0, 1), 128)
                    for u in range(GRING):
                        pe.wait_ge(e_oh, i * GRING + (u + 1))
                        pe.wait_ge(gathered[u], i * 16 + 16)
                        for j in range(KD):
                            pe.matmul(ps[:, 0, j * WIN:(j + 1) * WIN], gath[:, u, j * 128:(j + 1) * 128],
                                      ohf[:, u % 3, 0:WIN], start=False, stop=False, skip_group_check=True)
                        for s in range(NT):
                            bk, off = (1, s * WIN) if s < 4 else (0, KD * WIN)
                            m = pe.matmul(ps[0:TP, bk, off:off + WIN], ohs[:, u % 3, s * TP:(s + 1) * TP],
                                          ohd[:, u % 3, 0:WIN], start=False, stop=False, skip_group_check=True)
                        m.then_inc(e_used, 1)

            def wide_pass(base, tiles, bank0, with_sums):
                halves = ((0, 0, 512), (1, 512, N))
                with pe.Fori(0, EG) as i:
                    for u in range(GRING):
                        pe.wait_ge(e_oh, i * GRING + (base + u + 1))
                        if with_sums:
                            pe.wait_ge(gathered[u], i * 16 + 16)
                            for j in range(KD):
                                for b, lo, hi in halves:
                                    pe.matmul(ps[:, 2 * j + b, 0:hi - lo], gath[:, u, j * 128:(j + 1) * 128],
                                              ohf[:, u % 3, lo:hi], start=False, stop=False, skip_group_check=True)
                        for k, s in enumerate(tiles):
                            for b, lo, hi in halves:
                                m = pe.matmul(ps[0:TP, bank0 + 2 * k + b, 0:hi - lo],
                                              ohs[:, u % 3, s * TP:(s + 1) * TP], ohd[:, u % 3, lo:hi],
                                              start=False, stop=False, skip_group_check=True)
                        m.then_inc(e_used, 1)

            pe.sem_inc(e_used, 3)
            pe.sem_inc(flushed, 3)
            pe.wait_ge(sums_out, 1)
            spread = pe.value_load(wide[0:1, 0:1], min_val=0, max_val=E)
            with pe.If(spread > 0):
                clear(range(4), 128)
                clear(range(4, 8), TP)
                wide_pass(0, (0, 1), 4, True)
                pe.wait_ge(wide_out, 1)
                clear(range(6), TP)
                wide_pass(EC, (2, 3, 4), 0, False)
                pe.nop()
            with pe.Else():
                narrow_groups()
                pe.nop()
            pe.wait_ge(sums_out, 2)
            for t in range(NT):
                for j in range(KD):
                    m = pe.transpose(ps[0:TP, t // 2, (t % 2) * D + j * 128:(t % 2) * D + (j + 1) * 128],
                                     xT2[:, j, t * TP:(t + 1) * TP], ident[:, :])
            m.then_inc(adj_mm, 1)
            pe.wait_ge(ld_vec, 16 * n_vec)
            pe.wait_ge(sums_out, 3)
            pe.transpose(ps[:, 0, 0:NVEC], vecrows[0:NVEC, :], ident[0:NVEC, 0:NVEC])
            pe.transpose(ps[:, 1, 0:128], b1rows[:, 0, :], ident[:, :])
            pe.transpose(ps[:, 1, 128:256], b1rows[:, 1, :], ident[:, :]).then_inc(tr_mm, 1)
            ntr[0] += 1
            turned()

            nm = [0]

            def product(m):
                nm[0] += 1
                m.then_inc(m_mm, 1)

            def feature_major(w, src, j, b0, w_off=0):
                for hf in range(2):
                    for k in range(KD):
                        m = pe.matmul(ps[:, b0 + hf, 0:HN], w[:, k, w_off + j * 128:w_off + (j + 1) * 128],
                                      src[:, k, hf * HN:(hf + 1) * HN], start=(k == 0), stop=(k == KD - 1))
                return m

            pe.wait_ge(h_copied, 4 * NT)
            for j in range(KD):
                product(feature_major(wq, xnT, j, 2 * j))
            for t in range(NT):
                if t == 1:
                    pe.wait_ge(m_out, 1)
                if t >= 2:
                    pe.wait_ge(m_out, t + 1)
                for k in range(KD):
                    m = pe.matmul(ps[0:TP, 4 * (1 - t % 2), :], xnT[:, k, t * TP:(t + 1) * TP], wkv[:, k, :],
                                  start=(k == 0), stop=(k == KD - 1))
                product(m)
            pe.wait_ge(m_out, 7)
            for j in range(KD):
                for t in range(NT):
                    m = pe.matmul(ps[:, j, 0:129], kphi[:, t, j * 128:(j + 1) * 128], vext[:, t, j, :],
                                  start=(t == 0), stop=(t == NT - 1))
            product(m)
            pe.wait_ge(m_out, 8)
            for j in range(KD):
                if j:
                    pe.wait_ge(m_out, 9)
                for hf in range(2):
                    pe.matmul(ps[:, 2 + hf, 0:HN], ksbd[:, j, :], qphi[:, j, hf * HN:(hf + 1) * HN],
                              start=True, stop=True)
                    m = pe.matmul(ps[:, hf, 0:HN], kvbd[:, j, :], qphi[:, j, hf * HN:(hf + 1) * HN],
                                  start=True, stop=True)
                product(m)
            pe.wait_ge(m_out, 10)
            for t in range(NT):
                if t >= 2:
                    pe.wait_ge(m_out, 10 + t - 1)
                for k in range(KD):
                    m = pe.matmul(ps[0:TP, t % 2, 0:D], xT2[:, k, t * TP:(t + 1) * TP], wo[:, k, :],
                                  start=(k == 0), stop=(k == KD - 1))
                product(m)
            pe.wait_ge(m_out, 15)
            turn(ya, norm_ready, 2)
            turned()
            for m8_ in range(8):
                if m8_ >= 2:
                    pe.wait_ge(m_relu, m8_ - 1)
                product(feature_major(w1, xT2, m8_, 2 * (m8_ % 2)))
            pe.wait_ge(m_relu, 8)
            for t in range(NT):
                if t >= 2:
                    pe.wait_ge(m_out, 15 + t - 1)
                for k in range(8):
                    m = pe.matmul(ps[0:TP, t % 2, 0:D], big[:, k, t * TP:(t + 1) * TP], w2[:, k, :],
                                  start=(k == 0), stop=(k == 7))
                product(m)

            moe = dict(h=0, y=0, r=0)

            def router(ne, w_r, b2, logits_src):
                for t in range(NT):
                    for k in range(KD):
                        m = pe.matmul(ps[0:TP, 6, t * ne:(t + 1) * ne], logits_src[:, k, t * TP:(t + 1) * TP],
                                      w_r[:, k, :], start=(k == 0), stop=(k == KD - 1))
                m.then_inc(r_mm, 1)
                moe["r"] += 1
                pe.wait_ge(r_out, moe["r"])
                for t in range(NT):
                    bk, off = (6, t * TP) if t < 4 else (7, 0)
                    m = pe.transpose(ps[0:ne, bk, off:off + TP], comb[:, t, 0:ne], ident[0:TP, 0:TP])
                m.then_inc(r_mm, 1)
                moe["r"] += 1
                pe.wait_ge(r_out, moe["r"])
                y0 = moe["y"]
                for t in range(NT):
                    if t >= 2:
                        pe.wait_ge(moe_acc, y0 + t - 1)
                    pe.matmul(ps[0:TP, 4 + t % 2, 0:D], combT[0:ne, t * TP:(t + 1) * TP], b2[:, :], start=True,
                              stop=True).then_inc(moe_y, 1)
                moe["y"] = y0 + NT
                pe.wait_ge(moe_acc, moe["y"])

            def slots(ne):
                pe.wait_ge(r_out, moe["r"] + 1)
                for t in range(NT):
                    for s in range(t + 1):
                        pe.matmul(ps[0:TP, 6, t * ne:(t + 1) * ne], (tri if s == t else ones)[0:TP, 0:TP],
                                  lg[:, s, 0:ne], start=(s == 0), stop=(s == t))
                for s in range(NT):
                    m = pe.matmul(ps[0:TP, 7, 0:ne], ones[0:TP, 0:TP], lg[:, s, 0:ne], start=(s == 0),
                                  stop=(s == NT - 1))
                m.then_inc(r_mm, 1)
                moe["r"] += 1

            def carry_waits(bank):
                pe.matmul(ps[:, bank, 511:512], zerob[:, 0:128], zerob[:, 0:1], start=True, stop=True)

            def dense(ne, nh, exp_src):
                h0, y0 = moe["h"], moe["y"]
                with pe.Fori(0, ne // 2) as i:
                    for u in range(2):
                        pe.wait_ge(moe_w[u], i * 32 + 32)
                        wav = wa[:, u, 0:KD * nh * 128].rearrange("p (c h) -> p c h", c=KD)
                        wbv = wb[:, u, 0:nh * D].rearrange("p (c h) -> p c h", c=nh)
                        for m_ in range(nh):
                            pe.wait_ge(moe_act, i * (2 * nh) + (h0 + u * nh + m_ + 1))
                            feature_major(wav, exp_src, m_, 2 * (m_ % 2)).then_inc(moe_h, 1)
                        pe.wait_ge(moe_act, i * (2 * nh) + (h0 + 2 + (u + 1) * nh))
                        for t in range(NT):
                            pe.wait_ge(moe_acc, i * (2 * NT) + (y0 + u * NT + t - 1))
                            for k in range(nh):
                                m = pe.matmul(ps[0:TP, 4 + (u * NT + t) % 2, 0:D], big[:, k, t * TP:(t + 1) * TP],
                                              wbv[:, k, :], start=(k == 0), stop=(k == nh - 1))
                            m.then_inc(moe_y, 1)
                        m = pe.matmul(ps[0:1, 7, 0:1], zerob[:, 0:1], zerob[:, 0:1], start=True, stop=True)
                        m.then_inc(moe_used, 1)

            turn(ya, norm_ready, 3)
            turned()
            router(E0, wr0, b2e0, xT2)
            slots(E0)
            pe.wait_ge(put_ready, 1)

            def turn_block(s, c):
                pe.wait_ge(fx_loaded[c % 2], loads(s, c))
                if c >= 2:
                    pe.wait_ge(b_xT_out, no(s, c, -1))
                carry_waits(c % 2)
                for j in range(KD):
                    m = pe.transpose(ps[:, c % 2, j * 128:(j + 1) * 128], fx[:, c % 2, j * 128:(j + 1) * 128],
                                     ident[:, :])
                m.then_inc(b_xT, 1)

            def block_hidden(s, c):
                pe.wait_ge(fw1_loaded[c % 2], loads(s, c))
                pe.wait_ge(b_xT_out, no(s, c, 1))
                if c >= 2:
                    pe.wait_ge(b_h_out, no(s, c, -1))
                for h in range(2):
                    for m_ in range(4):
                        for k in range(KD):
                            m = pe.matmul(ps[:, 2 + 2 * (c % 2) + h, m_ * 128:(m_ + 1) * 128],
                                          fw1[:, c % 2, k, (4 * h + m_) * 128:(4 * h + m_ + 1) * 128],
                                          fxT[:, c % 2, k, :], start=(k == 0), stop=(k == KD - 1))
                    m.then_inc(b_h, 1)

            def block_result(s, c):
                pe.wait_ge(fw2_loaded[c % 2], loads(s, c))
                pe.wait_ge(b_h_out, no(s, c, 1))
                if c >= 2:
                    pe.wait_ge(b_y_out, no(s, c, -1))
                for k in range(8):
                    m = pe.matmul(ps[:, 6 + c % 2, 0:D], fh[:, c % 2, k, :], fw2[:, c % 2, k, :],
                                  start=(k == 0), stop=(k == 7))
                m.then_inc(b_y, 1)

            def block_step(s, c):
                block_hidden(s, c)
                if c not in (0, NFULL):
                    block_result(back(s), c - 1)
                if not is_last(s):
                    turn_block(ahead(s), c + 1)

            pe.wait_ge(adj_ready, 5)
            for t in range(NT):
                for s in range(NT):
                    m = pe.matmul(ps[0:TP, 6, t:t + 1], adjT[:, s, t * TP:(t + 1) * TP], ones[0:TP, 0:1],
                                  start=(s == 0), stop=(s == NT - 1))
            m.then_inc(p_mm, 1)
            pe.wait_ge(p_out, 1)
            for t in range(NT):
                for s in range(t + 1):
                    pe.matmul(ps[0:TP, 6, t:t + 1], (tri if s == t else ones)[0:TP, 0:TP], cnt[:, s:s + 1],
                              start=(s == 0), stop=(s == t))
            pe.matmul(ps[0:1, 7, 0:1], unsorted[:, :], ones[0:EP, 0:1], start=True, stop=True).then_inc(p_mm, 1)

            def run_blocks(b0, b1):
                turn_block(b0, b0)
                block_steps(pe, block_step, b0, b1)
                block_result(b1 - 1, b1 - 1)

            run_blocks(0, NFULL)
            rest_of_blocks(pe, lambda: run_blocks(NFULL, NBLK))

            turn(xn, norm_ready, 5)
            turned()
            nc_ = [0]

            def cproduct(m):
                nc_[0] += 1
                m.then_inc(c_mm, 1)

            for t in range(NT):
                if t >= 2:
                    pe.wait_ge(c_out, t - 1)
                for k in range(KD):
                    m = pe.matmul(ps[0:TP, t % 2, 0:DB + NH * NK], xnT[:, k, t * TP:(t + 1) * TP], wbc[:, k, :],
                                  start=(k == 0), stop=(k == KD - 1))
                cproduct(m)
            for hf in range(2):
                for k in range(KD):
                    m = pe.matmul(ps[:, 2 + hf, 0:HN], wbc[:, k, 0:DB], xnT[:, k, hf * HN:(hf + 1) * HN],
                                  start=(k == 0), stop=(k == KD - 1))
            cproduct(m)
            pe.wait_ge(c_out, 7)
            for t in range(NT):
                if t >= 2:
                    pe.wait_ge(c_out, 7 + t - 1)
                for s in range(NT):
                    m = pe.matmul(ps[0:TP, t % 2, 0:2 * DB], adjT[:, s, t * TP:(t + 1) * TP], bas[:, s, :],
                                  start=(s == 0), stop=(s == NT - 1))
                cproduct(m)
            pe.wait_ge(c_out, 12)

            def lproduct(m):
                m.then_inc(l_mm, 1)

            pe.wait_ge(ld_lw, 48)
            for j in range(KD):
                lproduct(feature_major(lwq, xnT, j, 2 * j))
            for j in range(KD):
                pe.wait_ge(l_out, j + 1)
                lproduct(feature_major(lwk, xnT, j, 2 * j))
            for t in range(NT):
                if t >= 2:
                    pe.wait_ge(l_out, 4 + t - 1)
                for k in range(KD):
                    m = pe.matmul(ps[0:TP, 4 + t % 2, 0:D], xnT[:, k, t * TP:(t + 1) * TP], lwv[:, k, :],
                                  start=(k == 0), stop=(k == KD - 1))
                lproduct(m)
            pe.wait_ge(l_out, 9)
            for t in range(NT):
                for j in range(KD):
                    q = 2 * t + j
                    m = pe.transpose(ps[0:TP, q // 4, (q % 4) * 128:(q % 4 + 1) * 128],
                                     xT2[:, j, t * TP:(t + 1) * TP], ident[:, :])
            lproduct(m)
            pe.wait_ge(l_out, 10)
            for j in range(KD):
                for t in range(NT):
                    m = pe.matmul(ps[:, j, 0:D], smx[:, t, j * 128:(j + 1) * 128], lval[:, t, :],
                                  start=(t == 0), stop=(t == NT - 1))
            lproduct(m)
            pe.wait_ge(l_out, 11)
            for t in range(NT):
                if t >= 2:
                    pe.wait_ge(l_out, 11 + t - 1)
                for k in range(KD):
                    m = pe.matmul(ps[0:TP, 4 + t % 2, 0:D], qphi[:, k, t * TP:(t + 1) * TP], lam[:, k, :],
                                  start=(k == 0), stop=(k == KD - 1))
                lproduct(m)
            pe.wait_ge(l_out, 16)
            pe.wait_ge(p_out, 2)
            slow = pe.value_load(loose[0:1, 0:1], min_val=0, max_val=E)
            with pe.If(slow > 0):
                for d in range(NT):
                    if d:
                        pe.wait_ge(mask_out, 2 * d)
                    for s in range(NT):
                        bk, off = (0, s * TP) if s < 4 else (1, 0)
                        m = pe.transpose(ps[0:TP, bk, off:off + TP], adjT[:, s, d * TP:(d + 1) * TP],
                                         ident[0:TP, 0:TP])
                    m.then_inc(mask_mm, 1)
                pe.wait_ge(mask_out, 2 * NT)
                for t in range(NT):
                    with pe.Fori(0, TP // 5) as i:
                        for u in range(5):
                            pe.wait_ge(mx_out, i * 5 + max(t * TP + u, 1))
                            row_ = identb[0:TP, bass.ds(i * 5 + u, 1)].to_broadcast([TP, 128])
                            b0 = 0 if u in (0, 2) else 2 if u in (1, 3) else 4
                            pe.matmul(ps[:, b0, 0:512], row_, maskb[:, t, 0:512], start=True, stop=True)
                            pe.matmul(ps[:, b0 + 1, 0:N - 512], row_, maskb[:, t, 512:N], start=True,
                                      stop=True).then_inc(mx_mm, 1)
                pe.wait_ge(mx_kept, N // 5)
                for t in range(NT):
                    bk, off = (0, t * 128) if t < 4 else (1, 0)
                    m = pe.transpose(ps[0:TP, bk, off:off + 128], aggmT[:, t * TP:(t + 1) * TP], ident[:, :])
                m.then_inc(mx_turned, 1)
                pe.nop()
            with pe.Else():
                pe.nop()
            pe.wait_ge(c_out, 14)
            for t in range(NT):
                m = pe.matmul(ps[:, 2, 0:D], ones[0:TP, :], ya[:, t, :], start=(t == 0), stop=(t == NT - 1))
            cproduct(m)
            pe.wait_ge(c_out, 16)
            for t in range(NT):
                m = pe.matmul(ps[:, 3, 0:D], ones[0:TP, :], yb[:, t, :], start=(t == 0), stop=(t == NT - 1))
            cproduct(m)
            pe.wait_ge(c_out, 17)

            turn(xn, norm_ready, 6)
            turned()
            router(E1, wr1, b2e1, xnT)
            slots(E1)
            pe.wait_ge(put_ready, 2)

            def turn_rows(s, c):
                pe.wait_ge(xe_loaded[c % 4], 16 * (s // 4 + 1) if isinstance(s, int) else (s[0] + (c // 4 + 1)) * 16)
                carry_waits(c % 2)
                for j in range(KD):
                    m = pe.transpose(ps[:, c % 2, j * CAP:(j + 1) * CAP], xe[:, c % 4, j * 128:(j + 1) * 128],
                                     ident[0:CAP, 0:CAP])
                m.then_inc(s_xT, 1)

            def hidden(s, c):
                pe.wait_ge(ew1_loaded[c % 4], 16 * (s // 4 + 1) if isinstance(s, int) else (s[0] + (c // 4 + 1)) * 16)
                pe.wait_ge(s_xT_out, at(s, c, 1))
                for j in range(4):
                    for k in range(KD):
                        m = pe.matmul(ps[:, 4 + c % 2, j * CAP:(j + 1) * CAP],
                                      ew1[:, c % 4, k, j * 128:(j + 1) * 128], xeT[:, c % 2, k, :],
                                      start=(k == 0), stop=(k == KD - 1))
                m.then_inc(s_h, 1)

            def result(s, c):
                pe.wait_ge(ew2_loaded[c % 4], 16 * (s // 4 + 1) if isinstance(s, int) else (s[0] + (c // 4 + 1)) * 16)
                pe.wait_ge(s_h_out, at(s, c, 1))
                if c >= 2:
                    pe.wait_ge(s_y_out, at(s, c, -1))
                for k in range(4):
                    m = pe.matmul(ps[0:CAP, 6 + c % 2, 0:D], hact[:, c % 2, k, :], ew2[:, c % 4, k, :],
                                  start=(k == 0), stop=(k == 3))
                m.then_inc(s_y, 1)

            def pe_step(s, c, first=False, last=False):
                hidden(s, c)
                if not last:
                    turn_rows(ahead(ahead(s)), c + 2)
                if not first:
                    result(back(s), c - 1)

            turn_rows(0, 0)
            turn_rows(1, 1)
            for s in range(3):
                pe_step(s, s, first=(s == 0))
            with pe.Fori(0, (E1 - 8) // 4) as i:
                for c in range(3, 7):
                    pe_step((i,), c)
            for s in range(E1 - 5, E1 - 1):
                pe_step(s, s, last=(s == E1 - 2))
            pe_step(E1 - 1, E1 - 1, last=True)
            result(E1 - 1, E1 - 1)
            pe.wait_ge(sparse_done, 1)
            crowded = pe.value_load(overi[0:1, 0:1], min_val=0, max_val=1)
            with pe.If(crowded > 0):
                dense(E1, H1 // 128, xnT)
            with pe.Else():
                pe.nop()

        @block.scalar
        def _(act):
            def sqrt_of(dst, src, count):
                act.wait_ge(var_ready, count)
                nc.scalar.activation(dst, src, ACT.Sqrt).then_inc(rstd_ready, 1)

            act.sem_inc(moe_act, 2)
            act.wait_ge(consts_ready, 4)
            for q in range(4):
                act.dma_start(xs.ap()[0:SPARE, :].rearrange("(q p r) d -> q p (r d)", q=4, p=128)[q],
                              zerof[:, :]).then_inc(xs_zero, 16)
            act.dma_start(fys.ap()[NFULL * 128:NBLK * 128, :].rearrange("(p r) d -> p (r d)", p=128),
                          zerof[:, 0:(NBLK - NFULL) * D]).then_inc(xs_zero, 16)
            sqrt_of(rstd[:, :], rstd[:, :], 1)
            for n in range(4 * NT):
                act.wait_ge(h_mm, n + 1)
                if n >= 8:
                    act.wait_ge(h_stored[n % 8], 16 * (n // 8))
                nc.scalar.activation(hrow[:, n % 8, :], ps[0:TP, n % 4, :], ACT.Copy).then_inc(h_copied, 1)
            for j in range(KD):
                act.wait_ge(m_pre, j + 1)
                nc.scalar.activation((tmpf, tmpg)[j][:, :], (tmpf, tmpg)[j][:, :], ACT.Exp).then_inc(m_exp, 1)
            for t in range(NT):
                act.wait_ge(m_pre, 3 + t)
                nc.scalar.activation(tmpr[:, (t % 2) * D:(t % 2 + 1) * D], tmpr[:, (t % 2) * D:(t % 2 + 1) * D],
                                     ACT.Exp).then_inc(m_exp, 1)
            sqrt_of(rstd[:, :], rstd[:, :], 2)
            for m_ in range(8):
                act.wait_ge(m_mm, 16 + m_)
                c = VCOL["b1"] + m_
                nc.scalar.activation(big[:, m_, :].rearrange("p (b n) -> p b n", b=2),
                                     ps[:, 2 * (m_ % 2):2 * (m_ % 2) + 2, 0:HN], ACT.Relu,
                                     bias=vecs[:, c:c + 1]).then_inc(m_relu, 1)
            for n in (3, 4, 5):
                sqrt_of(rstd[:, :], rstd[:, :], n)
            moe = dict(r=0)

            def gates():
                moe["r"] += 1
                act.wait_ge(r_pre, moe["r"])
                nc.scalar.activation(gate[:, :, 1:2], gate[:, :, 0:1], ACT.Exp).then_inc(r_exp, 1)

            def dense(ne, nh, func, bias_of):
                h0, y0 = 0, 2 * NT
                with act.Fori(0, ne // 2) as i:
                    for u in range(2):
                        for m_ in range(nh):
                            act.wait_ge(moe_h, i * (2 * nh) + (h0 + u * nh + m_ + 1))
                            if m_ == 0:
                                act.wait_ge(moe_acc, i * (2 * NT) + (y0 + u * NT))
                            nc.scalar.activation(big[:, m_, :].rearrange("p (b n) -> p b n", b=2),
                                                 ps[:, 2 * (m_ % 2):2 * (m_ % 2) + 2, 0:HN], func,
                                                 bias=bias_of(i, u, m_)).then_inc(moe_act, 1)

            gates()
            act.wait_ge(xs_put, 160)
            act.wait_ge(blk_ready, 1)

            def load_block(s, c):
                n_ = no(s, c, 0)
                act.dma_start(fx[:, c % 2, :], xs.ap()[bass.ds(n_ * 128, 128), :]).then_inc(fx_loaded[c % 2], 16)

            def store_block(s, c):
                act.wait_ge(b_y_out, no(s, c, 1))
                n_ = no(s, c, 0)
                act.dma_start(fys.ap()[bass.ds(n_ * 128, 128), :], fy[:, c % 2, :]).then_inc(fy_stored[c % 2], 16)

            def block_act(s, c):
                e = act.value_load(blkexp[0:1, bass.ds(no(s, c, 0), 1)], min_val=0, max_val=E0 - 1)
                for m_ in range(8):
                    if m_ % 4 == 0:
                        act.wait_ge(b_h, no(s, c, 1 + m_ // 4, 2))
                    if m_ == 0 and c >= 2:
                        act.wait_ge(b_y, no(s, c, -1))
                    m = nc.scalar.activation(fh[:, c % 2, m_, :],
                                             ps[:, 2 + 2 * (c % 2) + m_ // 4, (m_ % 4) * 128:(m_ % 4 + 1) * 128],
                                             ACT.Gelu, bias=vecs[:, bass.ds(e * 8 + (VCOL["eb1"] + m_), 1)])
                m.then_inc(b_h_out, 1)
                if c not in (0, NFULL):
                    store_block(back(s), c - 1)
                if not (isinstance(s, int) and (is_last(s) or is_last(s + 1))):
                    act.wait_ge(b_xT, no(s, c, 1))
                    load_block(s + 2 if isinstance(s, int) else s, c + 2)

            def run_blocks(b0, b1):
                load_block(b0, b0)
                load_block(b0 + 1, b0 + 1)
                block_steps(act, block_act, b0, b1)
                store_block(b1 - 1, b1 - 1)

            run_blocks(0, NFULL)
            rest_of_blocks(act, lambda: run_blocks(NFULL, NBLK))
            sqrt_of(rstd[:, :], rstd[:, :], 6)
            act.wait_ge(var_ready, 7)
            nc.scalar.activation(dinv[:, :], dinv[:, :], ACT.Sqrt).then_inc(rstd_ready, 1)
            act.wait_ge(c_out, 5)
            act.dma_start(node_major(btab.ap()), bas[:, :, 0:DB]).then_inc(btab_stored, 16)
            for j in range(KD):
                act.wait_ge(l_pre, j + 1)
                nc.scalar.activation(xT2[:, j, 0:N], xT2[:, j, 0:N], ACT.Exp, bias=kmax[:, j:j + 1],
                                     accum_out=ksum[:, j:j + 1]).then_inc(l_exp, 1)
            sqrt_of(lrs[:, :], lrs[:, :], 8)
            sqrt_of(gmean[:, :], gmean[:, :], 9)
            sqrt_of(rstd[:, :], rstd[:, :], 10)
            gates()
            act.wait_ge(xs_put, 320)

            def load_rows(s, c):
                e = s if isinstance(s, int) else s[0] * 4 + c
                act.dma_start(xe[:, c % 4, :], xs.ap()[bass.ds(e * CAP, CAP), :]).then_inc(xe_loaded[c % 4], 16)

            def keep_result(s, c):
                act.wait_ge(s_y, at(s, c, 1))
                if c >= 4:
                    act.wait_ge(y_stored[c % 4], 16 * (s // 4) if isinstance(s, int) else (s[0] + c // 4) * 16)
                nc.scalar.copy(ye[:, c % 4, :], ps[0:CAP, 6 + c % 2, 0:D]).then_inc(s_y_out, 1)
                act.wait_ge(s_y_out, at(s, c, 1))
                e = s if isinstance(s, int) else s[0] * 4 + c
                act.dma_start(ys.ap()[bass.ds(e * CAP, CAP), :], ye[:, c % 4, :]).then_inc(y_stored[c % 4], 16)

            for q in range(4):
                load_rows(q, q)

            def act_step(s, c, load=True):
                if load:
                    act.wait_ge(s_xT, at(s, c, 1))
                    load_rows(s + 4 if isinstance(s, int) else s, c + 4)
                if c >= 1:
                    keep_result(back(s), c - 1)

            for s in range(3):
                act_step(s, s)
            with act.Fori(0, (E1 - 8) // 4) as i:
                for c in range(3, 7):
                    act_step((i,), c)
            for s in range(E1 - 5, E1):
                act_step(s, s, load=(s + 4 < E1))
            keep_result(E1 - 1, E1 - 1)
            act.wait_ge(sparse_done, 1)
            crowded = act.value_load(overi[0:1, 0:1], min_val=0, max_val=1)
            with act.If(crowded > 0):
                dense(E1, 4, ACT.Relu, lambda i, u, m_: b1cols[:, bass.ds(i * 8 + (u * 4 + m_), 1)])
            with act.Else():
                act.nop()

        @block.vector
        def _(dve):
            v = nc.vector
            step = Chain(dve, dchain)
            done, mark = step.done, step.mark

            def mark_free(ins):
                ins.then_inc(mx_agg, 1)

            def tt(out, p, q, op):
                return v.tensor_tensor(out, p, q, op)

            mark(v.memset(zerof[:, :], 0.0))
            step.wait()
            v.memset(zerob[:, :], 0.0).then_inc(consts_ready, 1)
            for dst in (xnT, xT2, qphi):
                mark(v.memset(dst[:, :, N:NP], 0.0))
            step.wait()
            dve.wait_ge(ld_edges, 160)
            dve.wait_ge(consts_ready, 4)
            for h, n in enumerate(ROWCH):
                srow, drow, rrow = (crow[0:n, w, h, :] for w in range(3))
                mark(v.tensor_copy(srow, raw[0:n, 0, h, :]))
                mark(v.tensor_copy(drow, raw[0:n, 1, h, :]))
                mark(v.scalar_tensor_tensor(out=rrow, in0=raw[0:n, 0, h, :], scalar=float(R0),
                                            in1=raw[0:n, 2, h, :], op0=ALU.mult, op1=ALU.add))
                step.wait()
                mark(v.tensor_reduce(span[0:n, h, 0:1], drow, AX.X, ALU.min))
                m = v.tensor_reduce(span[0:n, h, 1:2], drow, AX.X, ALU.max)
                if h:
                    m.then_inc(edges_ready, 1)
                else:
                    mark(m)
            mark(v.memset(apart[:, 0:1], 0.0))
            done(tt(apart[:, 1:EC], dpm[:, 1:EC], dpm[:, 0:EC - 1], ALU.not_equal))
            mark(v.tensor_scalar(apart[:, 1:EC], apart[:, 1:EC], -BIG, None, ALU.mult))
            done(v.memset(dcmp[:, :], 0.0))
            mark(tt(dcmp[0:EP, 0:EC - 1], dpm[:, 0:EC - 1], dnx[:, 0:EC - 1], ALU.is_gt))
            done(tt(dcmp[0:EP - 1, EC - 1:EC], dpm[0:EP - 1, EC - 1:EC], dnx[0:EP - 1, EC - 1:EC], ALU.is_gt))
            mark(v.tensor_reduce(unsorted[:, :], dcmp[:, :], AX.X, ALU.add))
            dve.wait_ge(ed_mm, 1)
            mark(v.tensor_copy(srcf[:, :], ps[0:EP, 0, 0:EC]))
            mark(v.tensor_copy(dstf[:, :], ps[0:EP, 0, EC:2 * EC]))
            mark(v.tensor_copy(rowid[:, :], ps[0:EP, 1, 0:EC]))
            done(v.tensor_reduce(glow, ps[0:1, 2, 0:EC].rearrange("p (g u) -> p g u", u=GRING), AX.X, ALU.min))
            v.tensor_scalar(glow, glow, float(N - WIN), None, ALU.min).then_inc(ed_low, 1)
            done(v.tensor_reduce(ghigh, ps[0:1, 2, 256:256 + EC].rearrange("p (g u) -> p g u", u=GRING), AX.X,
                                 ALU.max))
            dve.wait_ge(ed_low, 1)
            done(tt(ghigh, ghigh, glow, ALU.subtract))
            mark(v.tensor_copy(winlow[:, :], glow))
            done(v.tensor_scalar(gover, ghigh, float(WIN), None, ALU.is_ge))
            done(v.tensor_reduce(wide[:, :], gover, AX.X, ALU.max))
            dve.wait_ge(ed_mm, 2)
            tt(dstw[:, :].rearrange("p (g u) -> p g u", u=GRING),
               dstf[:, :].rearrange("p (g u) -> p g u", u=GRING),
               ps[0:EP, 3, 0:EG].unsqueeze(2).to_broadcast([EP, EG, GRING]), ALU.subtract).then_inc(ed_out, 1)
            dve.wait_ge(ed_out, 1)
            ntr = [0]

            def turn(dst, b0=0):
                ntr[0] += 1
                dve.wait_ge(tr_mm, ntr[0])
                for j in range(KD):
                    mark(v.tensor_copy(dst[:, j, 0:4 * TP], ps[:, b0 + j, 0:4 * TP]))
                v.tensor_copy(dst[:, :, 4 * TP:N], ps[:, b0 + 2, 0:KD * TP].rearrange("p (c n) -> p c n", c=KD)
                              ).then_inc(tr_copied, 1)

            nsq = [0]

            def root(out, var, eps):
                done(v.tensor_scalar(out, var, eps, None, ALU.add))
                v.reciprocal(out, out).then_inc(var_ready, 1)
                nsq[0] += 1
                dve.wait_ge(rstd_ready, nsq[0])

            nnorm = [0]

            def layernorm(dst, src, last=True):
                for t in range(NT):
                    mark(v.bn_stats(stats[:, t, :], src[:, t, :]))
                step.wait()
                for t in range(NT):
                    mark(v.bn_aggr(mv[:, t, :], stats[:, t, :]))
                step.wait()
                root(rstd[:, :], mv[:, :, 1:2].rearrange("p t o -> p (t o)"), EPS)
                for t in range(NT):
                    m = v.tensor_scalar(dst[:, t, :], src[:, t, :], mv[:, t, 0:1], rstd[:, t:t + 1],
                                        ALU.subtract, ALU.mult)
                    if t < NT - 1 or not last:
                        mark(m)
                if last:
                    m.then_inc(norm_ready, 1)
                    nnorm[0] += 1
                    dve.wait_ge(norm_ready, nnorm[0])
                else:
                    step.wait()

            def all_tiles(name):
                return row(name).unsqueeze(1).to_broadcast([TP, NT, D])

            def affine(dst, g, b):
                done(tt(dst[:, :, :], dst[:, :, :], all_tiles(g), ALU.mult))
                return tt(dst[:, :, :], dst[:, :, :], all_tiles(b), ALU.add)

            dve.wait_ge(ld_x, 16)
            layernorm(xn, x)
            turn(xnT)
            dve.wait_ge(ld_basis, 32)
            for r in range(R0):
                for b in range(NB0):
                    c = comp[:, r * NB0 + b:r * NB0 + b + 1]
                    if b == 0:
                        m = v.tensor_scalar(wrel[:, :, r, :], basis[:, b, :, :], c, None, ALU.mult)
                    else:
                        m = v.scalar_tensor_tensor(out=wrel[:, :, r, :], in0=basis[:, b, :, :], scalar=c,
                                                   in1=wrel[:, :, r, :], op0=ALU.mult, op1=ALU.add)
                    if r % 2 == 1 and b == NB0 - 1:
                        m.then_inc(wrel_ready, 1)
                    else:
                        done(m)

            def add_to_x():
                done(tt(x[:, 0:4, :], x[:, 0:4, :], ps[0:TP, 0:2, :].rearrange("p b (t d) -> p (b t) d", t=2),
                        ALU.add))
                return tt(x[:, 4, :], x[:, 4, :], ps[0:TP, 2, 0:D], ALU.add)

            dve.wait_ge(ld_vec, 16 * n_vec)
            done(tt(x[:, :, :], x[:, :, :], row("gbias").unsqueeze(1).to_broadcast([TP, NT, D]), ALU.add))
            dve.wait_ge(adj_mm, 1)
            add_to_x().then_inc(sums_out, 1)
            dve.wait_ge(sums_out, 1)
            dve.wait_ge(acc_zero, 2)

            def one_hots(i, u, base, tiles, with_sums, dn, wn):
                s0, s1 = tiles[0] * TP, (tiles[-1] + 1) * TP
                dve.wait_ge(e_used, i * GRING + (base + u + 1))
                at_ = bass.ds(i * GRING + u, 1)
                v.tensor_scalar(ohs[:, u % 3, s0:s1], iota_f[0:EP, s0:s1], srcf[:, at_], None, ALU.is_equal)
                if with_sums:
                    v.tensor_scalar(ohf[:, u % 3, 0:wn], iota_f[0:EP, 0:wn], dn[:, at_], None, ALU.is_equal)
                v.tensor_scalar(ohd[:, u % 3, 0:wn], iota_f[0:EP, 0:wn], dn[:, at_], None,
                                ALU.is_equal).then_inc(e_oh, 1)

            def narrow_groups():
                with dve.Fori(0, EG) as i:
                    for u in range(GRING):
                        one_hots(i, u, 0, range(NT), True, dstw, WIN)
                    low = dve.value_load(winlow[0:1, bass.ds(i, 1)], min_val=0, max_val=N - WIN)
                    dve.wait_ge(e_used, i * GRING + (GRING + 3))
                    dve.wait_ge(flushed, i * 3 + 3)
                    held_()
                    win = bass.ds(low, WIN)
                    tt(xT2[:, :, win], xT2[:, :, win], ps[:, 0, 0:KD * WIN].rearrange("p (c n) -> p c n", c=KD),
                       ALU.add).then_inc(flushed, 1)
                    tt(adjT[:, 4, win], adjT[:, 4, win], ps[0:TP, 0, KD * WIN:(KD + 1) * WIN],
                       ALU.add).then_inc(flushed, 1)
                    tt(adjT[:, 0:4, win], adjT[:, 0:4, win], ps[0:TP, 1, :].rearrange("p (s n) -> p s n", s=4),
                       ALU.add).then_inc(flushed, 1)
                dve.wait_ge(flushed, EG * 3 + 3)

            def held_():
                v.memset(held[:, :], 0.0)

            wide_step = Chain(dve, slow_step)

            def wide_pass(base, tiles, with_sums):
                with dve.Fori(0, EG) as i:
                    for u in range(GRING):
                        one_hots(i, u, base, tiles, with_sums, dstf, N)
                dve.wait_ge(e_used, base + EC + 3)

            def keep(dst, bank, parts):
                wide_step.mark(v.tensor_copy(dst[:, 0:512], ps[0:parts, bank, :]))
                wide_step.mark(v.tensor_copy(dst[:, 512:N], ps[0:parts, bank + 1, 0:N - 512]))

            spread = dve.value_load(wide[0:1, 0:1], min_val=0, max_val=E)
            with dve.If(spread > 0):
                wide_pass(0, (0, 1), True)
                for j in range(KD):
                    keep(xT2[:, j, 0:N], 2 * j, 128)
                for s in (0, 1):
                    keep(adjT[:, s, :], 4 + 2 * s, TP)
                wide_step.wait()
                v.memset(held[:, :], 0.0).then_inc(wide_out, 1)
                wide_pass(EC, (2, 3, 4), False)
                for k, s in enumerate((2, 3, 4)):
                    keep(adjT[:, s, :], 2 * k, TP)
                wide_step.wait()
                dve.nop()
            with dve.Else():
                narrow_groups()
                dve.nop()
            v.memset(held[:, :], 0.0).then_inc(sums_out, 1)
            for s in range(NT):
                tt(adjT[:, s, s * TP:(s + 1) * TP], adjT[:, s, s * TP:(s + 1) * TP], ident[0:TP, 0:TP],
                   ALU.add).then_inc(adj_ready, 1)
            dve.wait_ge(adj_mm, 2)
            add_to_x().then_inc(sums_out, 1)
            dve.wait_ge(sums_out, 3)
            ntr[0] += 1
            dve.wait_ge(tr_mm, ntr[0])
            mark(v.tensor_copy(vecs[:, :], ps[:, 0, 0:NVEC]))
            v.tensor_copy(b1cols[:, :], ps[:, 1, 0:256]).then_inc(tr_copied, 1)

            dve.wait_ge(xs_zero, 16 * 5)
            mark(v.memset(vext[:, :, :, 128:129], 1.0))
            dve.wait_ge(h_copied, 4 * NT)
            for j in range(KD):
                dve.wait_ge(m_mm, j + 1)
                src = ps[:, 2 * j:2 * j + 2, 0:HN]
                bq = vecs[:, VCOL["bq"] + j:VCOL["bq"] + j + 1]
                tf = (tmpf, tmpg)[j][:, :].rearrange("p (b n) -> p b n", b=2)
                v.tensor_scalar(tf, src, bq, 0.0, ALU.add, ALU.min).then_inc(m_pre, 1)
                mark(v.tensor_scalar(qphi[:, j, :].rearrange("p (b n) -> p b n", b=2), src, bq, 0.0, ALU.add,
                                     ALU.max))
                step.wait()
                dve.wait_ge(m_exp, j + 1)
                tt(qphi[:, j, :], qphi[:, j, :], (tmpf, tmpg)[j][:, :], ALU.add).then_inc(m_out, 1)
            for t in range(NT):
                dve.wait_ge(m_mm, 3 + t)
                bank = 4 * (1 - t % 2)
                done(tt(kphi[:, t, :], ps[0:TP, bank, 0:D], row("bk"), ALU.add))
                e_ = tmpr[:, (t % 2) * D:(t % 2 + 1) * D]
                v.tensor_scalar(e_, kphi[:, t, :], 0.0, None, ALU.min).then_inc(m_pre, 1)
                mark(tt(vext[:, t, :, 0:128], ps[0:TP, bank, D:2 * D].rearrange("p (c n) -> p c n", c=KD),
                        row("bv").rearrange("p (c n) -> p c n", c=KD), ALU.add))
                dve.wait_ge(m_exp, 3 + t)
                v.scalar_tensor_tensor(out=kphi[:, t, :], in0=kphi[:, t, :], scalar=0.0, in1=e_, op0=ALU.max,
                                       op1=ALU.add).then_inc(m_out, 1)
            dve.wait_ge(m_mm, 8)
            for j in range(KD):
                mark(tt(kvbd[:, j, :], ps[:, j, 0:128], headmask[:, :], ALU.mult))
                mark(v.tensor_copy(scr[:, j:j + 1], ps[:, j, 128:129]))
                step.wait()
                m = v.tensor_scalar(ksbd[:, j, :], headmask[:, :], scr[:, j:j + 1], None, ALU.mult)
                if j == KD - 1:
                    m.then_inc(m_out, 1)
                else:
                    mark(m)
            for j in range(KD):
                dve.wait_ge(m_mm, 9 + j)
                t3 = tmpf[:, :].rearrange("p (b n) -> p b n", b=2)
                done(v.tensor_scalar(t3, ps[:, 2:4, 0:HN], 1e-6, None, ALU.add))
                done(v.reciprocal(tmpf[:, :], tmpf[:, :]))
                tt(xT2[:, j, :].rearrange("p (b n) -> p b n", b=2), ps[:, 0:2, 0:HN], t3,
                   ALU.mult).then_inc(m_out, 1)
                dve.wait_ge(m_out, 9 + j)
            for t in range(NT):
                dve.wait_ge(m_mm, 11 + t)
                done(tt(ya[:, t, :], ps[0:TP, t % 2, 0:D], row("bo"), ALU.add))
                tt(ya[:, t, :], ya[:, t, :], xn[:, t, :], ALU.add).then_inc(m_out, 1)
            dve.wait_ge(m_out, 15)
            layernorm(ya, ya, last=False)
            affine(ya, "ln1_g", "ln1_b").then_inc(norm_ready, 1)
            nnorm[0] += 1
            dve.wait_ge(norm_ready, nnorm[0])
            turn(xT2)
            for t in range(NT):
                dve.wait_ge(m_mm, 24 + t)
                done(tt(yb[:, t, :], ps[0:TP, t % 2, 0:D], row("b2"), ALU.add))
                tt(yb[:, t, :], yb[:, t, :], ya[:, t, :], ALU.add).then_inc(m_out, 1)
            dve.wait_ge(m_out, 20)
            layernorm(yb, yb, last=False)
            done(affine(yb, "ln2_g", "ln2_b"))
            done(tt(x[:, :, :], x[:, :, :], yb[:, :, :], ALU.add))

            moe = dict(y=0, r=0, x=0, g=0)

            def router(ne, rb, kept):
                r0 = moe["r"]
                dve.wait_ge(r_mm, r0 + 1)
                step.done(tt(lg[:, :, 0:ne], ps[0:TP, 6, 0:NT * ne].rearrange("p (t e) -> p t e", t=NT),
                             rb[0:TP, :].unsqueeze(1).to_broadcast([TP, NT, ne]), ALU.add))
                for k in range(2):
                    cur = (lg, lg2)[k]
                    for t in range(NT):
                        mark(v.max(m8[:, t, :], cur[:, t, 0:ne]))
                    step.wait()
                    for t in range(NT):
                        mark(v.max_index(i8[:, t, :], m8[:, t, :], cur[:, t, 0:ne]))
                    step.wait()
                    done(v.tensor_copy(i8f[:, :, k:k + 1], i8[:, :, 0:1]))
                    mark(v.tensor_copy(gate[:, :, 2 * k:2 * k + 1], m8[:, :, 0:1]))
                    done(tt((comb, lg2)[k][:, :, 0:ne], iota_f[0:TP, 0:ne].unsqueeze(1).to_broadcast([TP, NT, ne]),
                            i8f[:, :, k:k + 1].to_broadcast([TP, NT, ne]), ALU.is_equal))
                    if k == 0:
                        done(v.scalar_tensor_tensor(out=lg2[:, :, 0:ne], in0=comb[:, :, 0:ne], scalar=-3e38,
                                                    in1=lg[:, :, 0:ne], op0=ALU.mult, op1=ALU.add))
                mark(v.tensor_copy(kept[:, 0], comb[:, :, 0:ne]))
                mark(v.tensor_copy(kept[:, 1], lg2[:, :, 0:ne]))
                tt(gate[:, :, 0:1], gate[:, :, 2:3], gate[:, :, 0:1], ALU.subtract).then_inc(r_pre, 1)
                moe["g"] += 1
                dve.wait_ge(r_exp, moe["g"])
                done(v.tensor_scalar(gate[:, :, 2:3], gate[:, :, 1:2], 1.0, None, ALU.add))
                done(v.reciprocal(gate[:, :, 2:3], gate[:, :, 2:3]))
                done(tt(gate[:, :, 3:4], gate[:, :, 1:2], gate[:, :, 2:3], ALU.mult))
                done(tt(comb[:, :, 0:ne], comb[:, :, 0:ne], gate[:, :, 2:3].to_broadcast([TP, NT, ne]), ALU.mult))
                done(tt(lg2[:, :, 0:ne], lg2[:, :, 0:ne], gate[:, :, 3:4].to_broadcast([TP, NT, ne]), ALU.mult))
                tt(comb[:, :, 0:ne], comb[:, :, 0:ne], lg2[:, :, 0:ne], ALU.add).then_inc(r_out, 1)
                dve.wait_ge(r_out, r0 + 1)
                dve.wait_ge(r_mm, r0 + 2)
                mark(v.tensor_copy(combT[0:ne, 0:4 * TP], ps[0:ne, 6, 0:4 * TP]))
                v.tensor_copy(combT[0:ne, 4 * TP:N], ps[0:ne, 7, 0:TP]).then_inc(r_out, 1)
                moe["r"] = r0 + 2
                y0 = moe["y"]
                for t in range(NT):
                    dve.wait_ge(moe_y, y0 + t + 1)
                    tt(x[:, t, :], x[:, t, :], ps[0:TP, 4 + t % 2, 0:D], ALU.add).then_inc(moe_acc, 1)
                moe["y"] = y0 + NT
                dve.wait_ge(moe_acc, y0 + NT)

            def dense(ne):
                y0 = moe["y"]
                with dve.Fori(0, ne // 2) as i:
                    step.enter(i, 0)
                    for u in range(2):
                        for t in range(NT):
                            dve.wait_ge(moe_y, i * (2 * NT) + (y0 + u * NT + t + 1))
                            dve.wait_ge(moe_acc, i * (2 * NT) + (y0 + u * NT + t - (NT - 1)))
                            v.scalar_tensor_tensor(out=x[:, t, :], in0=ps[0:TP, 4 + (u * NT + t) % 2, 0:D],
                                                   scalar=comb[:, t, bass.ds(i * 2 + u, 1)], in1=x[:, t, :],
                                                   op0=ALU.mult, op1=ALU.add).then_inc(moe_acc, 1)
                    step.leave(ne // 2)
                moe["y"] = y0 + ne * NT
                dve.wait_ge(moe_acc, moe["y"])

            def ask_slots(ne, kept):
                tt(lg[:, :, 0:ne], kept[:, 0], kept[:, 1], ALU.add).then_inc(r_out, 1)
                moe["r"] += 1
                dve.wait_ge(r_out, moe["r"])
                dve.wait_ge(r_mm, moe["r"])

            layernorm(ya, x)
            turn(xT2)
            layernorm(xn, ya)
            router(E0, rb0, sel0)
            ask_slots(E0, sel0)
            mark(v.tensor_copy(total[:, :], ps[0:TP, 7, 0:E0]))
            done(v.tensor_scalar(nt2[:, :], iota_f[0:TP, 0:NT], 128.0, None, ALU.mult))
            done(tt(steps5[:, :, :], total[:, :].unsqueeze(2).to_broadcast([TP, E0, 5]),
                    nt2[:, :].unsqueeze(1).to_broadcast([TP, E0, 5]), ALU.is_gt))
            done(v.tensor_reduce(blocks[:, :], steps5[:, :, :], AX.X, ALU.add))
            done(v.tensor_copy(blkend[:, :], blocks[:, :]))
            for e in range(1, E0):
                done(tt(blkend[:, e:e + 1], blkend[:, e:e + 1], blkend[:, e - 1:e], ALU.add))
            mark(tt(ended[:, :, :], iota_f[0:1, 0:NBLK].unsqueeze(2).to_broadcast([1, NBLK, E0]),
                    blkend[0:1, :].unsqueeze(1).to_broadcast([1, NBLK, E0]), ALU.is_ge))
            done(tt(blocks[:, :], blkend[:, :], blocks[:, :], ALU.subtract))
            mark(v.tensor_copy(nblocks[:, :], blkend[0:1, E0 - 1:E0]))
            mark(v.tensor_reduce(blkf[:, :], ended[:, :, :], AX.X, ALU.add))
            done(v.tensor_scalar(blocks[:, :], blocks[:, :], 128.0, None, ALU.mult))
            v.tensor_scalar(blkexp[:, :], blkf[:, :], float(E0 - 1), None, ALU.min).then_inc(blk_ready, 1)
            done(tt(lg[:, :, 0:E0], ps[0:TP, 6, 0:NT * E0].rearrange("p (t e) -> p t e", t=NT),
                    blocks[:, :].unsqueeze(1).to_broadcast([TP, NT, E0]), ALU.add))
            for k in range(2):
                done(tt(lg2[:, :, 0:E0], sel0[:, k], lg[:, :, 0:E0], ALU.mult))
                done(v.tensor_reduce(rowf[:, :, k:k + 1], lg2[:, :, 0:E0], AX.X, ALU.add))
                mark(v.tensor_copy(get[:, k, :], rowf[:, :, k]))
                m = v.tensor_copy(put[:, k, :], rowf[:, :, k])
                if k:
                    m.then_inc(put_ready, 1)
                else:
                    mark(m)

            def expert_of(s, c):
                return dve.value_load(blkexp[0:1, bass.ds(no(s, c, 0), 1)], min_val=0, max_val=E0 - 1)

            def keep_block(s, c, e):
                dve.wait_ge(b_xT, no(s, c, 1))
                if c >= 2:
                    dve.wait_ge(b_h, no(s, c, -2, 2))
                for j in range(KD):
                    m = v.tensor_scalar(fxT[:, c % 2, j, :], ps[:, c % 2, j * 128:(j + 1) * 128],
                                        vecs[:, bass.ds(e * 2 + (VCOL["eg"] + j), 1)],
                                        vecs[:, bass.ds(e * 2 + (VCOL["eb"] + j), 1)], ALU.mult, ALU.add)
                m.then_inc(b_xT_out, 1)

            def keep_y(s, c):
                dve.wait_ge(b_y, no(s, c, 1))
                if c >= 2:
                    dve.wait_ge(fy_stored[c % 2], loads(s, c, 0))
                v.tensor_copy(fy[:, c % 2, :], ps[:, 6 + c % 2, 0:D]).then_inc(b_y_out, 1)

            def block_dve(s, c):
                more = not is_last(s)
                if more:
                    e = expert_of(ahead(s), c + 1)
                if c not in (0, NFULL):
                    keep_y(back(s), c - 1)
                if more:
                    keep_block(ahead(s), c + 1, e)

            dve.wait_ge(p_mm, 1)
            done(v.tensor_copy(deg[:, :], ps[0:TP, 6, 0:NT]))
            done(v.tensor_scalar(cnt[:, :], deg[:, :], 1.0, None, ALU.subtract))
            done(v.tensor_scalar(nt2[:, :], cnt[:, :], float(EC), None, ALU.is_gt))
            done(v.tensor_reduce(over[:, :], nt2[:, :], AX.X, ALU.add))
            tt(unsorted[:, :], unsorted[:, :], over[:, :], ALU.add).then_inc(p_out, 1)
            dve.wait_ge(p_mm, 2)
            mark(v.tensor_copy(first[:, :], ps[0:TP, 6, 0:NT]))
            mark(v.tensor_copy(loose[:, :], ps[0:1, 7, 0:1]))
            mark(v.tensor_scalar(bound[:, :], iota_f[0:TP, 0:TP], float(EC), None, ALU.mult))
            mark(v.tensor_scalar(miss[:, 0, :], cnt[:, :], 0.0, -BIG, ALU.is_equal, ALU.mult))
            step.wait()
            done(tt(nt2[:, :], first[:, :], cnt[:, :], ALU.add))
            done(v.tensor_scalar(nt2[:, :], nt2[:, :], -1.0, 0.0, ALU.add, ALU.max))
            mark(v.tensor_copy(ends[:, 0, :], nt2[:, :]))
            done(tt(below[:, :, :], bound[:, :].unsqueeze(1).to_broadcast([TP, NT, TP]),
                    nt2[:, :].unsqueeze(2).to_broadcast([TP, NT, TP]), ALU.is_le))
            done(v.tensor_reduce(nt2[:, :], below[:, :, :], AX.X, ALU.add))
            done(v.tensor_scalar(nt2[:, :], nt2[:, :], float(EC), float(EC + 1), ALU.mult, ALU.subtract))
            done(tt(miss[:, 1, :], first[:, :], nt2[:, :], ALU.is_gt))
            mark(v.tensor_scalar(miss[:, 1, :], miss[:, 1, :], -BIG, None, ALU.mult))
            done(v.tensor_scalar(nt2[:, :], nt2[:, :], 0.0, None, ALU.max))
            v.tensor_copy(ends[:, 1, :], nt2[:, :]).then_inc(p_out, 1)
            dve.wait_ge(p_out, 2)

            dve.wait_ge(blk_ready, 1)

            def run_blocks(b0, b1):
                keep_block(b0, b0, expert_of(b0, b0))
                block_steps(dve, block_dve, b0, b1)
                keep_y(b1 - 1, b1 - 1)

            run_blocks(0, NFULL)
            rest_of_blocks(dve, lambda: run_blocks(NFULL, NBLK))

            def add_results(n):
                for k in range(2):
                    dve.wait_ge(y_got[k], 80 * (n + 1))
                    for t in range(NT):
                        m = v.scalar_tensor_tensor(out=x[:, t, :], in0=(ya, yb)[k][:, t, :],
                                                   scalar=gate[:, t, 2 + k:3 + k], in1=x[:, t, :], op0=ALU.mult,
                                                   op1=ALU.add)
                        if k == 0 or t < NT - 1:
                            mark(m)
                    if k == 0:
                        step.wait()
                return m

            done(add_results(0))

            layernorm(xn, x)
            turn(xnT)
            for t in range(NT):
                dve.wait_ge(c_mm, t + 1)
                mark(v.tensor_copy(bas[:, t, 0:DB], ps[0:TP, t % 2, 0:DB]))
                tt(wgt[:, t, :], ps[0:TP, t % 2, DB:DB + NH * NK], bcomb[0:TP, :], ALU.add).then_inc(c_out, 1)
            dve.wait_ge(c_mm, 6)
            mark(v.tensor_copy(basT[:, 0:HN], ps[:, 2, 0:HN]))
            v.tensor_copy(basT[:, HN:N], ps[:, 3, 0:N - HN]).then_inc(c_out, 1)
            v.reciprocal(dinv[:, :], deg[:, :]).then_inc(var_ready, 1)
            nsq[0] += 1
            dve.wait_ge(rstd_ready, nsq[0])
            for t in range(NT):
                m = v.tensor_scalar(bas[:, t, DB:2 * DB], bas[:, t, 0:DB], dinv[:, t:t + 1], None, ALU.mult)
                if t < NT - 1:
                    mark(m)
            m.then_inc(c_out, 1)
            for t in range(NT):
                dve.wait_ge(c_mm, 7 + t)
                mark(v.tensor_scalar(agg[:, t, 0:DB], ps[0:TP, t % 2, DB:2 * DB], dinv[:, t:t + 1], None,
                                     ALU.mult))
                v.tensor_copy(agg[:, t, DB:2 * DB], ps[0:TP, t % 2, 0:DB]).then_inc(c_out, 1)
            ya4 = ya[:, :, :].rearrange("p t (h f) -> p t h f", h=NH)

            def weigh(k0, k1):
                for k in range(k0, k1):
                    w = wgt[:, :, :].rearrange("p t (h k) -> p t h k", h=NH)[:, :, :, k:k + 1].to_broadcast(
                        [TP, NT, NH, FH])
                    g = agg[:, :, k * FH:(k + 1) * FH].unsqueeze(2).to_broadcast([TP, NT, NH, FH])
                    if k == 0:
                        done(tt(ya4, w, g, ALU.mult))
                        done(tt(ya[:, :, :], ya[:, :, :], row("cbias").unsqueeze(1).to_broadcast([TP, NT, D]),
                                ALU.add))
                    else:
                        done(tt(prod, w, g, ALU.mult))
                        m = tt(ya4, ya4, prod, ALU.add)
                        if k < NK - 1:
                            done(m)
                        else:
                            m.then_inc(c_out, 2)
                            dve.wait_ge(c_out, 14)

            def queries_and_keys():
                for j in range(KD):
                    dve.wait_ge(l_mm, j + 1)
                    c = VCOL["bqk"] + j
                    v.tensor_scalar(qphi[:, j, :].rearrange("p (b n) -> p b n", b=2), ps[:, 2 * j:2 * j + 2, 0:HN],
                                    vecs[:, c:c + 1], None, ALU.add).then_inc(l_out, 1)
                for j in range(KD):
                    dve.wait_ge(l_mm, 3 + j)
                    c = VCOL["bqk"] + 2 + j
                    done(v.tensor_scalar(xT2[:, j, :].rearrange("p (b n) -> p b n", b=2),
                                         ps[:, 2 * j:2 * j + 2, 0:HN], vecs[:, c:c + 1], None, ALU.add))
                    v.tensor_reduce(kmax[:, j:j + 1], xT2[:, j, 0:N], AX.X, ALU.max, negate=True
                                    ).then_inc(l_pre, 1)
                    dve.wait_ge(l_exp, j + 1)
                    v.reciprocal(ksum[:, j:j + 1], ksum[:, j:j + 1]).then_inc(l_out, 1)

            def values():
                for t in range(NT):
                    dve.wait_ge(l_mm, 5 + t)
                    tt(lval[:, t, :], ps[0:TP, 4 + t % 2, 0:D], row("lbv"), ALU.add).then_inc(l_out, 1)
                dve.wait_ge(l_mm, 10)
                mark(v.tensor_copy(smx[:, 0:4, :], ps[0:TP, 0:2, :].rearrange("p b (t d) -> p (b t) d", t=2)))
                v.tensor_copy(smx[:, 4, :], ps[0:TP, 2, 0:D]).then_inc(l_out, 1)

            def make_lambda():
                dve.wait_ge(l_mm, 11)
                for j in range(KD):
                    mark(v.tensor_scalar(lam[:, j, :], ps[:, j, 0:D], ksum[:, j:j + 1], None, ALU.mult))
                step.wait()
                for j in range(KD):
                    mark(v.bn_stats(lst[:, j, :], lam[:, j, :]))
                step.wait()
                for j in range(KD):
                    mark(v.bn_aggr(lmv[:, j, :], lst[:, j, :]))
                step.wait()
                root(lrs[:, :], lmv[:, :, 1:2].rearrange("p t o -> p (t o)"), EPS)
                done(tt(lrs[:, :], lrs[:, :], vecs[:, VCOL["gamma"]:VCOL["gamma"] + KD], ALU.mult))
                for j in range(KD):
                    done(v.tensor_scalar(lam[:, j, :], lam[:, j, :], lmv[:, j, 0:1], lrs[:, j:j + 1], ALU.subtract,
                                         ALU.mult))
                    m = v.tensor_scalar(lam[:, j, :], lam[:, j, :], vecs[:, VCOL["beta"] + j:VCOL["beta"] + j + 1],
                                        None, ALU.add)
                    if j < KD - 1:
                        mark(m)
                m.then_inc(l_out, 1)

            def add_lambda():
                for t in range(NT):
                    dve.wait_ge(l_mm, 12 + t)
                    tt(x[:, t, :], x[:, t, :], ps[0:TP, 4 + t % 2, 0:D], ALU.add).then_inc(l_out, 1)
                dve.wait_ge(l_out, 16)

            dve.wait_ge(c_out, 12)
            counts = step.n, nsq[0]
            slow = dve.value_load(loose[0:1, 0:1], min_val=0, max_val=E)
            with dve.If(slow > 0):
                weigh(0, 8)
                queries_and_keys()
                values()
                make_lambda()
                add_lambda()
                for d in range(NT):
                    dve.wait_ge(mask_mm, 1 + d)
                    v.tensor_scalar(maskb[:, d, 0:4 * TP], ps[0:TP, 0, 0:4 * TP], 0.0, -BIG, ALU.is_equal,
                                    ALU.mult).then_inc(mask_out, 1)
                    v.tensor_scalar(maskb[:, d, 4 * TP:N], ps[0:TP, 1, 0:TP], 0.0, -BIG, ALU.is_equal,
                                    ALU.mult).then_inc(mask_out, 1)
                dve.sem_inc(mx_out, 1)
                for t in range(NT):
                    with dve.Fori(0, TP // 5) as i:
                        for u in range(5):
                            n = t * TP + u
                            dve.wait_ge(mx_mm, i * 5 + (n + 1))
                            dve.wait_ge(mx_out, i * 5 + (n + 1))
                            v.memset(held[:, :], 0.0)
                            b0 = 0 if u in (0, 2) else 2 if u in (1, 3) else 4
                            src = ps[:, b0:b0 + 2, :].rearrange("p b n -> p (b n)")[:, 0:N]
                            v.tensor_tensor_reduce(out=scr[:, 0:N], in0=src, in1=basT[:, :], scale=1.0,
                                                   scalar=-3e38, op0=ALU.add, op1=ALU.max,
                                                   accum_out=max5[:, u:u + 1]).then_inc(mx_out, 1)
                        dve.wait_ge(mx_out, i * 5 + (t * TP + 6))
                        v.tensor_copy(aggmT[:, bass.ds(i * 5 + t * TP, 5)], max5[:, :]).then_inc(mx_kept, 1)
                        dve.wait_ge(mx_kept, i + (t * TP // 5 + 1))
                dve.wait_ge(mx_turned, 1)
                mark_free(v.tensor_copy(agg[:, 0:4, 2 * DB:3 * DB],
                                        ps[0:TP, 0, :].rearrange("p (t d) -> p t d", t=4)))
                mark_free(v.tensor_copy(agg[:, 4, 2 * DB:3 * DB], ps[0:TP, 1, 0:DB]))
                dve.wait_ge(mx_agg, 2)
                dve.nop()
            with dve.Else():
                step.n, nsq[0] = counts
                def group(g):
                    half = g % 2
                    dve.wait_ge(run_loaded[half], 16 * GRING * (g // 2 + 1))
                    for u in range(GRING):
                        c, slot = g * GRING + u, half * GRING + u
                        if c:
                            v.scalar_tensor_tensor(out=run[:, slot, :], in0=run[:, slot - 1, :] if u else carry,
                                                   scalar=apart[:, c:c + 1], in1=run[:, slot, :], op0=ALU.add,
                                                   op1=ALU.max).then_inc(run_step, 1)
                            dve.wait_ge(run_step, c)
                    v.tensor_copy(carry, run[:, slot, :]).then_inc(run_done, 1)
                    dve.wait_ge(run_done, g + 1)

                for g in range(4):
                    group(g)
                    weigh(2 * g, 2 * g + 2)
                group(4)
                queries_and_keys()
                group(5)
                values()
                group(6)
                make_lambda()
                group(7)
                add_lambda()
                for g in range(8, EG):
                    group(g)
                dve.wait_ge(ends_got, 160)
                got = [kphi[:, :, k * DB:(k + 1) * DB] for k in range(2)]
                for k in range(2):
                    mark_free(tt(got[k], got[k], miss[:, k, :].unsqueeze(2).to_broadcast([TP, NT, DB]), ALU.add))
                dve.wait_ge(mx_agg, 2)
                mark_free(tt(got[0], got[0], got[1], ALU.max))
                dve.wait_ge(mx_agg, 3)
                mark_free(tt(agg[:, :, 2 * DB:3 * DB], got[0], bas[:, :, 0:DB], ALU.max))
                dve.wait_ge(mx_agg, 4)
                dve.nop()
            weigh(8, NK)
            dve.wait_ge(c_mm, 12)
            done(v.scalar_tensor_tensor(out=gmean[:, :], in0=ps[:, 2, 0:D], scalar=1.0 / N,
                                        in1=row("gnms", 128), op0=ALU.mult, op1=ALU.mult))
            everywhere = gmean[0:TP, :].unsqueeze(1).to_broadcast([TP, NT, D])
            done(tt(ya[:, :, :], ya[:, :, :], everywhere, ALU.subtract))
            dve.wait_ge(btab_stored, 16)
            tt(yb[:, :, :], ya[:, :, :], ya[:, :, :], ALU.mult).then_inc(c_out, 2)
            dve.wait_ge(c_mm, 13)
            done(v.tensor_scalar(gmean[:, :], ps[:, 3, 0:D], 1.0 / N, EPS, ALU.mult, ALU.add))
            v.reciprocal(gmean[:, :], gmean[:, :]).then_inc(var_ready, 1)
            nsq[0] += 1
            dve.wait_ge(rstd_ready, nsq[0])
            done(tt(gmean[:, :], gmean[:, :], row("gnw", 128), ALU.mult))
            done(tt(ya[:, :, :], ya[:, :, :], everywhere, ALU.mult))
            done(tt(ya[:, :, :], ya[:, :, :], row("gnb").unsqueeze(1).to_broadcast([TP, NT, D]), ALU.add))
            v.scalar_tensor_tensor(out=x[:, :, :], in0=ya[:, :, :], scalar=0.0, in1=x[:, :, :], op0=ALU.max,
                                   op1=ALU.add).then_inc(c_out, 1)
            dve.wait_ge(c_out, 17)

            layernorm(xn, x)
            turn(xnT)
            router(E1, rb1, sel)
            ask_slots(E1, sel)
            pos = ps[0:TP, 6, 0:NT * E1].rearrange("p (t e) -> p t e", t=NT)
            for k in range(2):
                done(tt(lg2[:, :, :], sel[:, k], pos, ALU.mult))
                done(v.tensor_reduce(slotf[:, :, k:k + 1], lg2[:, :, :], AX.X, ALU.add))
            done(v.tensor_reduce(over[:, :], ps[0:TP, 7, 0:E1], AX.X, ALU.max))
            mark(v.tensor_scalar(overi[:, :], over[:, :], float(CAP), None, ALU.is_gt))
            done(v.tensor_scalar(fits[:, :, :], slotf[:, :, :], float(CAP), None, ALU.is_lt))
            done(v.tensor_scalar(slotf[:, :, :], slotf[:, :, :], float(CAP - 1), None, ALU.min))
            done(v.scalar_tensor_tensor(out=rowf[:, :, :], in0=i8f[:, :, 0:2], scalar=float(CAP),
                                        in1=slotf[:, :, :], op0=ALU.mult, op1=ALU.add))
            for k in range(2):
                mark(v.tensor_copy(get[:, k, :], rowf[:, :, k]))
                done(v.tensor_scalar(slotf[:, :, k], nodeid[:, :], float(SPARE + k * N), None, ALU.add))
                done(tt(rowf[:, :, k], rowf[:, :, k], slotf[:, :, k], ALU.subtract))
                done(tt(rowf[:, :, k], rowf[:, :, k], fits[:, :, k], ALU.mult))
                done(tt(rowf[:, :, k], rowf[:, :, k], slotf[:, :, k], ALU.add))
                m = v.tensor_copy(put[:, k, :], rowf[:, :, k])
                if k:
                    m.then_inc(put_ready, 1)
                else:
                    mark(m)
            done(tt(gate[:, :, 2:4], gate[:, :, 2:4], fits[:, :, :], ALU.mult))
            for k in range(2):
                done(tt(lg2[:, :, :], sel[:, k], gate[:, :, 2 + k:3 + k].to_broadcast([TP, NT, E1]), ALU.mult))
                done(tt(comb[:, :, :], comb[:, :, :], lg2[:, :, :], ALU.subtract))

            def keep_rows(s, c):
                dve.wait_ge(s_xT, at(s, c, 1))
                if c >= 2:
                    dve.wait_ge(s_h, at(s, c, -1))
                v.tensor_copy(xeT[:, c % 2].rearrange("p c n -> p (c n)"), ps[:, c % 2, 0:KD * CAP]
                              ).then_inc(s_xT_out, 1)

            def rectify(s, c):
                dve.wait_ge(s_h, at(s, c, 1))
                if c >= 2:
                    dve.wait_ge(s_y, at(s, c, -1))
                b = s * 4 if isinstance(s, int) else s[0] * 16 + 4 * c
                done(tt(hact[:, c % 2], ps[:, 4 + c % 2, 0:4 * CAP].rearrange("p (c n) -> p c n", c=4),
                        b1cols[:, bass.ds(b, 4)].unsqueeze(2).to_broadcast([128, 4, CAP]), ALU.add))
                v.tensor_scalar(hact[:, c % 2], hact[:, c % 2], 0.0, None, ALU.max).then_inc(s_h_out, 1)

            def dve_step(s, c, last=False):
                rectify(s, c)
                if not last:
                    keep_rows(ahead(ahead(s)), c + 2)

            keep_rows(0, 0)
            keep_rows(1, 1)
            for s in range(3):
                dve_step(s, s)
            with dve.Fori(0, (E1 - 8) // 4) as i:
                step.enter(i, 4)
                for c in range(3, 7):
                    dve_step((i,), c)
                step.leave((E1 - 8) // 4)
            for s in range(E1 - 5, E1 - 1):
                dve_step(s, s, last=(s == E1 - 2))
            rectify(E1 - 1, E1 - 1)
            add_results(1).then_inc(sparse_done, 1)
            dve.wait_ge(sparse_done, 1)
            crowded = dve.value_load(overi[0:1, 0:1], min_val=0, max_val=1)
            with dve.If(crowded > 0):
                dense(E1)
            with dve.Else():
                dve.nop()
            v.memset(scr[:, 0:1], 0.0).then_inc(o_ready, NT)


_INS = ["x", "src", "dst", "edge_type_8", "L0_gnn_basis", "L0_gnn_comp", "L0_gnn_loop_weight",
        "L0_gnn_bias_param", "L0_mix_Wq", "L0_mix_bq", "L0_mix_Wk", "L0_mix_bk", "L0_mix_Wv", "L0_mix_bv",
        "L0_mix_Wo", "L0_mix_bo", "L0_mix_W1", "L0_mix_b1", "L0_mix_W2", "L0_mix_b2", "L0_mix_ln1_g",
        "L0_mix_ln1_b", "L0_mix_ln2_g", "L0_mix_ln2_b", "L0_ffn_Wr", "L0_ffn_br", "L0_ffn_ln_g", "L0_ffn_ln_b",
        "L0_ffn_W1", "L0_ffn_b1", "L0_ffn_W2", "L0_ffn_b2", "L1_gnn_W_bases", "L1_gnn_W_comb",
        "L1_gnn_b_comb", "L1_gnn_conv_bias", "L1_gnn_gn_weight", "L1_gnn_gn_bias", "L1_gnn_gn_mean_scale",
        "L1_mix_W_qk", "L1_mix_b_qk", "L1_mix_W_v", "L1_mix_b_v", "L1_mix_gamma", "L1_mix_beta", "L1_ffn_Wr",
        "L1_ffn_br", "L1_ffn_W1", "L1_ffn_b1", "L1_ffn_W2", "L1_ffn_b2"]


def kernel(**inputs):
    import numpy as _np
    import concourse.bacc as _bacc
    from concourse import mybir as _mybir
    from concourse.bass_utils import run_bass_kernel_spmd as _run

    nc = _bacc.Bacc("TRN2", target_bir_lowering=False, num_devices=1)
    arrays, args = {}, {}
    for name in _INS:
        v = _np.ascontiguousarray(inputs[name])
        arrays[f"in_{name}_dram"] = v
        args[name] = nc.dram_tensor(f"in_{name}_dram", v.shape, _mybir.dt.from_np(v.dtype),
                                    kind="ExternalInput").ap()
    args["out"] = nc.dram_tensor("out_0_dram", (N, D), _mybir.dt.float32, kind="ExternalOutput").ap()
    gps_kernel(nc, args)
    r = _run(nc, [arrays], core_ids=[0])
    return r.results[0]["out_0_dram"]
```
